# Optimizing a Trainium2 kernel written in Bass

```python
import numpy as np
import jax
import jax.numpy as jnp

def _softmax(x, axis=-1):
    return jax.nn.softmax(x, axis=axis)

def _gelu(x):
    return jax.nn.gelu(x, approximate=True)

def _silu(x):
    return jax.nn.silu(x)

def _sigmoid(x):
    return jax.nn.sigmoid(x)

def _layernorm(x, axis=-1, eps=1e-05):
    m = jnp.mean(x, axis=axis, keepdims=True)
    v = jnp.var(x, axis=axis, keepdims=True)
    return (x - m) / jnp.sqrt(v + eps)

def _scatter_add(tgt, idx, src, axis=0):
    return tgt.at[idx].add(src)

def _segment_sum(src, seg, n):
    return jax.ops.segment_sum(src, seg, n)
kernel_name = 'mk_seq_postln_d4_jaxref_r8_f7c715'

def setup_inputs(seed: int=0):
    np.random.seed(seed)
    _w = jnp.asarray

    def _L0_attn_setup():
        import jax, jax.numpy as jnp
        import numpy as np
        D_MODEL = 128
        D_STATE = 16
        D_CONV = 4
        EXPAND = 2
        E = EXPAND * D_MODEL
        B, L = (4, 512)
        key = jax.random.key(seed)
        ks = jax.random.split(key, 8)
        x = jax.random.normal(ks[0], (B, L, D_MODEL), dtype=jnp.float32)
        W_in = jax.random.normal(ks[1], (D_MODEL, 2 * E), dtype=jnp.float32) * 0.02
        b_in = jnp.zeros((2 * E,), dtype=jnp.float32)
        conv_w = jax.random.normal(ks[2], (E, 1, D_CONV), dtype=jnp.float32) * 0.1
        conv_b = jnp.zeros((E,), dtype=jnp.float32)
        A = jax.random.normal(ks[3], (E, D_STATE), dtype=jnp.float32) * 0.01
        C = jax.random.normal(ks[4], (E, D_STATE), dtype=jnp.float32) * 0.01
        Dp = jnp.ones((E,), dtype=jnp.float32) * 0.01
        W_out = jax.random.normal(ks[5], (E, D_MODEL), dtype=jnp.float32) * 0.02
        b_out = jnp.zeros((D_MODEL,), dtype=jnp.float32)
        return {'x': x, 'W_in': W_in, 'b_in': b_in, 'conv_w': conv_w, 'conv_b': conv_b, 'A': A, 'C': C, 'Dp': Dp, 'W_out': W_out, 'b_out': b_out}
    _L0_attn_in = _L0_attn_setup()

    def _L0_ffn_setup():
        import jax, jax.numpy as jnp
        import numpy as np
        K = 4
        ROUTED_SCALING = 1.0
        NORM_TOPK = True

        def _gate(hidden_states, router_w, router_bias):
            logits = jnp.einsum('bsh,he->bse', hidden_states, router_w).astype(jnp.float32)
            scores = jax.nn.softmax(logits, axis=-1)
            corrected = scores + router_bias
            _, top_k_indices = jax.lax.top_k(corrected, K)
            top_k_weights = jnp.take_along_axis(scores, top_k_indices, axis=-1)
            if NORM_TOPK:
                top_k_weights = top_k_weights / (top_k_weights.sum(-1, keepdims=True) + 1e-20)
            top_k_weights = top_k_weights * ROUTED_SCALING
            return (top_k_weights.astype(hidden_states.dtype), top_k_indices)
        key = jax.random.key(seed)
        ks = jax.random.split(key, 9)
        B, S, H, E, I, IS = (2, 128, 128, 8, 64, 256)
        sc = 0.02
        return {'hidden_states': jax.random.normal(ks[0], (B, S, H), jnp.float32), 'router_w': jax.random.normal(ks[1], (H, E), jnp.float32) * sc, 'router_bias': jnp.zeros((), jnp.float32), 'gate_w': jax.random.normal(ks[2], (E, H, I), jnp.float32) * sc, 'up_w': jax.random.normal(ks[3], (E, H, I), jnp.float32) * sc, 'down_w': jax.random.normal(ks[4], (E, I, H), jnp.float32) * sc, 's_gate_w': jax.random.normal(ks[5], (H, IS), jnp.float32) * sc, 's_up_w': jax.random.normal(ks[6], (H, IS), jnp.float32) * sc, 's_down_w': jax.random.normal(ks[7], (IS, H), jnp.float32) * sc}
    _L0_ffn_in = _L0_ffn_setup()

    def _L1_attn_setup():
        import jax, jax.numpy as jnp
        import numpy as np
        import math
        B, T, D = (4, 512, 128)
        K, H, KH, C = (64, 4, 16, 64)
        MLP = 512
        EPS = 1e-05

        def _layernorm(x, g, b):
            m = jnp.mean(x, axis=-1, keepdims=True)
            v = jnp.mean((x - m) ** 2, axis=-1, keepdims=True)
            return (x - m) / jnp.sqrt(v + EPS) * g + b

        def _chunked_eigenstate(log_decay, frequency, beta_r, beta_i):
            Bt, Tt, Kt = beta_r.shape
            T_pad = (Tt + C - 1) // C * C
            if T_pad > Tt:
                beta_r = jnp.pad(beta_r, ((0, 0), (0, T_pad - Tt), (0, 0)))
                beta_i = jnp.pad(beta_i, ((0, 0), (0, T_pad - Tt), (0, 0)))
            n_chunks = T_pad // C
            mag = jax.nn.sigmoid(log_decay)
            powers = jnp.arange(C, dtype=log_decay.dtype)
            mag_pow = mag[:, None] ** powers[None, :]
            phases = frequency[:, None] * powers[None, :]
            kr = mag_pow * jnp.cos(phases)
            ki = mag_pow * jnp.sin(phases)
            ii = jnp.arange(C)
            idx = ii[None, :] - ii[:, None]
            mask = (idx >= 0).astype(kr.dtype)
            idxc = jnp.clip(idx, 0, C - 1)
            L_r = kr[:, idxc] * mask[None]
            L_i = ki[:, idxc] * mask[None]
            br = beta_r.reshape(Bt, n_chunks, C, Kt)
            bi = beta_i.reshape(Bt, n_chunks, C, Kt)
            intra_r = jnp.einsum('kjs,bnsk->bnjk', L_r, br) - jnp.einsum('kjs,bnsk->bnjk', L_i, bi)
            intra_i = jnp.einsum('kjs,bnsk->bnjk', L_r, bi) + jnp.einsum('kjs,bnsk->bnjk', L_i, br)
            first_col_r = L_r[:, :, 0]
            first_col_i = L_i[:, :, 0]

            def step(carry, intra):
                sr, si = carry
                ir, im = intra
                cr = first_col_r[None] * sr[:, :, None] - first_col_i[None] * si[:, :, None]
                ci = first_col_r[None] * si[:, :, None] + first_col_i[None] * sr[:, :, None]
                o_r = ir + jnp.transpose(cr, (0, 2, 1))
                o_i = im + jnp.transpose(ci, (0, 2, 1))
                return ((o_r[:, -1, :], o_i[:, -1, :]), (o_r, o_i))
            xs = (jnp.transpose(intra_r, (1, 0, 2, 3)), jnp.transpose(intra_i, (1, 0, 2, 3)))
            init = (jnp.zeros((Bt, Kt), beta_r.dtype), jnp.zeros((Bt, Kt), beta_r.dtype))
            _, (out_r, out_i) = jax.lax.scan(step, init, xs)
            c_r = jnp.transpose(out_r, (1, 0, 2, 3)).reshape(Bt, T_pad, Kt)[:, :Tt]
            c_i = jnp.transpose(out_i, (1, 0, 2, 3)).reshape(Bt, T_pad, Kt)[:, :Tt]
            return (c_r, c_i)
        key = jax.random.key(seed)
        ks = jax.random.split(key, 8)

        def n(k, shape, scale):
            return jax.random.normal(k, shape, dtype=jnp.float32) * scale
        return {'x': jax.random.normal(ks[0], (B, T, D), dtype=jnp.float32), 'w_in': n(ks[1], (2 * K, D), D ** (-0.5)), 'w_out': n(ks[2], (D, 2 * K), (2 * K) ** (-0.5)), 'w_gate': n(ks[3], (D, D), D ** (-0.5)), 'b_gate': jnp.full((D,), -2.0, dtype=jnp.float32), 'log_decay': jax.random.uniform(ks[4], (K,), minval=-3.0, maxval=-0.1, dtype=jnp.float32), 'frequency': jnp.linspace(0.0, 2.0 * math.pi * (1.0 - 1.0 / K), K, dtype=jnp.float32), 'coupling': jnp.eye(KH, dtype=jnp.float32)[None] + 0.01 * jax.random.normal(ks[5], (H, KH, KH), dtype=jnp.float32) / math.sqrt(KH), 'w_mlp1': n(ks[6], (MLP, D), D ** (-0.5)), 'b_mlp1': jnp.zeros((MLP,), jnp.float32), 'w_mlp2': n(ks[7], (D, MLP), MLP ** (-0.5)), 'b_mlp2': jnp.zeros((D,), jnp.float32), 'ln1_g': jnp.ones((D,), jnp.float32), 'ln1_b': jnp.zeros((D,), jnp.float32), 'ln2_g': jnp.ones((D,), jnp.float32), 'ln2_b': jnp.zeros((D,), jnp.float32)}
    _L1_attn_in = _L1_attn_setup()

    def _L1_ffn_setup():
        import jax, jax.numpy as jnp
        import numpy as np
        EPS = 1e-06
        LN_EPS = 1e-05

        def _absmean_core(W):
            gamma = jnp.mean(jnp.abs(W)) + EPS
            Ws = W / gamma
            Wq = jnp.sign(Ws) * jnp.minimum(jnp.round(jnp.abs(Ws)), 1.0)
            return (Wq, gamma)

        @jax.custom_vjp
        def absmean(W):
            return _absmean_core(W)[0]

        def _absmean_fwd(W):
            Wq, gamma = _absmean_core(W)
            return (Wq, gamma)

        def _absmean_bwd(gamma, g):
            return (g / gamma,)
        absmean.defvjp(_absmean_fwd, _absmean_bwd)

        def layernorm(x, w, b, eps=LN_EPS):
            mu = jnp.mean(x, axis=-1, keepdims=True)
            var = jnp.mean((x - mu) ** 2, axis=-1, keepdims=True)
            return (x - mu) * jax.lax.rsqrt(var + eps) * w + b
        key = jax.random.key(seed)
        k1, k2, k3 = jax.random.split(key, 3)
        d, h = (128, 512)
        B, T = (8, 256)
        return {'x': jax.random.normal(k1, (B, T, d), jnp.float32), 'W_fc': jax.random.normal(k2, (h, d), jnp.float32), 'ln_w': jnp.ones((h,), jnp.float32), 'ln_b': jnp.zeros((h,), jnp.float32), 'W_proj': jax.random.normal(k3, (d, h), jnp.float32)}
    _L1_ffn_in = _L1_ffn_setup()

    def _L2_attn_setup():
        import jax, jax.numpy as jnp
        import numpy as np
        import math
        B, S, E = (2, 256, 128)
        H, DK, DV = (16, 64, 64)

        def _rope(q, k):
            D = q.shape[-1]
            theta = 10000.0 ** (jnp.arange(0, D, 2, dtype=jnp.float32) / D)
            pos = jnp.arange(q.shape[-2], dtype=jnp.float32)
            freqs = pos[:, None] * (1.0 / theta)[None, :]
            emb = jnp.concatenate([freqs, freqs], axis=-1)
            cos = jnp.cos(emb)[None, None]
            sin = jnp.sin(emb)[None, None]

            def rotate(x):
                x1 = x[..., ::2]
                x2 = x[..., 1::2]
                return jnp.stack([-x2, x1], axis=-1).reshape(x.shape)
            return (q * cos + rotate(q) * sin, k * cos + rotate(k) * sin)
        key = jax.random.key(seed)
        ks = jax.random.split(key, 9)
        sE = 1.0 / math.sqrt(E)
        sV = 1.0 / math.sqrt(H * DV)
        return {'x': jax.random.normal(ks[0], (B, S, E), dtype=jnp.float32), 'wq': jax.random.uniform(ks[1], (H * DK, E), jnp.float32, -sE, sE), 'bq': jax.random.uniform(ks[2], (H * DK,), jnp.float32, -sE, sE), 'wk': jax.random.uniform(ks[3], (H * DK, E), jnp.float32, -sE, sE), 'bk': jax.random.uniform(ks[4], (H * DK,), jnp.float32, -sE, sE), 'wv': jax.random.uniform(ks[5], (H * DV, E), jnp.float32, -sE, sE), 'bv': jax.random.uniform(ks[6], (H * DV,), jnp.float32, -sE, sE), 'wo': jax.random.uniform(ks[7], (E, H * DV), jnp.float32, -sV, sV), 'bo': jax.random.uniform(ks[8], (E,), jnp.float32, -sV, sV)}
    _L2_attn_in = _L2_attn_setup()

    def _L2_ffn_setup():
        import jax, jax.numpy as jnp
        import numpy as np
        HIDDEN = 128
        INTER = 512
        key = jax.random.key(seed)
        k1, k2, k3, k4, k5 = jax.random.split(key, 5)
        hidden_states = jax.random.normal(k1, (4, 256, HIDDEN), dtype=jnp.float32)
        W1 = jax.random.normal(k2, (HIDDEN, INTER), dtype=jnp.float32) * (1.0 / np.sqrt(HIDDEN))
        b1 = jax.random.normal(k3, (INTER,), dtype=jnp.float32) * 0.02
        W2 = jax.random.normal(k4, (INTER, HIDDEN), dtype=jnp.float32) * (1.0 / np.sqrt(INTER))
        b2 = jax.random.normal(k5, (HIDDEN,), dtype=jnp.float32) * 0.02
        return {'hidden_states': hidden_states, 'W1': W1, 'b1': b1, 'W2': W2, 'b2': b2}
    _L2_ffn_in = _L2_ffn_setup()

    def _L3_attn_setup():
        import jax, jax.numpy as jnp
        import numpy as np
        B, N, D, H = (4, 512, 128, 16)
        DH = D // H
        M = int(DH * np.log(DH))
        EPS = 0.0001

        def softmax_kernel(t, proj, is_query):
            dn = t.shape[-1] ** (-0.25)
            ratio = proj.shape[0] ** (-0.5)
            td = jnp.einsum('bhnd,md->bhnm', t * dn, proj)
            diag = 0.5 * dn ** 2 * jnp.sum(t * t, axis=-1, keepdims=True)
            if is_query:
                mx = jnp.max(td, axis=-1, keepdims=True)
            else:
                mx = jnp.max(td, axis=(-1, -2), keepdims=True)
            return ratio * (jnp.exp(td - diag - mx) + EPS)
        key = jax.random.key(seed)
        ks = jax.random.split(key, 12)
        s = 0.02
        inp = {'x': jax.random.normal(ks[0], (B, N, D), jnp.float32), 'Wq': jax.random.normal(ks[1], (D, D), jnp.float32) * s, 'bq': jnp.zeros((D,), jnp.float32), 'Wk': jax.random.normal(ks[2], (D, D), jnp.float32) * s, 'bk': jnp.zeros((D,), jnp.float32), 'Wv': jax.random.normal(ks[3], (D, D), jnp.float32) * s, 'bv': jnp.zeros((D,), jnp.float32), 'Wo': jax.random.normal(ks[4], (D, D), jnp.float32) * s, 'bo': jnp.zeros((D,), jnp.float32), 'Wfc': jax.random.normal(ks[5], (D, D), jnp.float32) * s, 'bfc': jnp.zeros((D,), jnp.float32), 'proj': jax.random.normal(ks[6], (M, DH), jnp.float32)}
        return inp
    _L3_attn_in = _L3_attn_setup()

    def _L3_ffn_setup():
        import jax, jax.numpy as jnp
        import numpy as np
        DIM = 128
        DEPTH = 6
        HEADS = 16
        DIM_HEAD = 64
        WINDOW = 32
        INNER = HEADS * DIM_HEAD
        DIM_INNER = int(DIM * 4 * 2 / 3)
        QK_SCALE = 8.0

        def shift_tokens(t):
            a, s = jnp.split(t, 2, -1)
            s = jnp.pad(s, ((0, 0), (1, 0), (0, 0)))[:, :-1]
            return jnp.concatenate([a, s], -1)

        def l2norm(t):
            return t / jnp.maximum(jnp.linalg.norm(t, axis=-1, keepdims=True), 1e-12)

        def rotate_half(x):
            x1, x2 = jnp.split(x, 2, -1)
            return jnp.concatenate([-x2, x1], -1)

        def rotary_tables(n):
            half = jnp.arange(0, DIM_HEAD, 2, dtype=jnp.float32)
            inv_freq = 1.0 / 10000.0 ** (half / DIM_HEAD)
            t = jnp.arange(n, dtype=jnp.float32)
            freqs = t[:, None] * inv_freq[None, :]
            freqs = jnp.concatenate([freqs, freqs], -1)
            base_scale = (half + 0.4 * DIM_HEAD) / (1.4 * DIM_HEAD)
            power = (t - n // 2) / (WINDOW // 2)
            scale = base_scale[None, :] ** power[:, None]
            scale = jnp.concatenate([scale, scale], -1)
            return (freqs, scale)

        def local_attention(q, k, v):
            b, h, n, d = q.shape
            w = WINDOW
            nw = n // w
            bq = q.reshape(b, h, nw, w, d)
            bk = k.reshape(b, h, nw, w, d)
            bv = v.reshape(b, h, nw, w, d)

            def look(t):
                p = jnp.pad(t, ((0, 0), (0, 0), (1, 0), (0, 0), (0, 0)))
                return jnp.concatenate([p[:, :, :nw], p[:, :, 1:]], axis=3)
            bk2, bv2 = (look(bk), look(bv))
            seq = jnp.arange(n).reshape(nw, w)
            seq_p = jnp.pad(seq, ((1, 0), (0, 0)), constant_values=-1)
            jt = jnp.concatenate([seq_p[:nw], seq_p[1:]], axis=1)
            it = seq[:, :, None]
            jb = jt[:, None, :]
            mask = (it < jb) | (it > jb + w) | (jb == -1)
            sim = jnp.einsum('bhwie,bhwje->bhwij', bq, bk2) * QK_SCALE
            sim = jnp.where(mask, -jnp.finfo(sim.dtype).max, sim)
            attn = jax.nn.softmax(sim, -1)
            out = jnp.einsum('bhwij,bhwje->bhwie', attn, bv2)
            return out.reshape(b, h, n, d)

        def attn_layer(x, Wqkv, qs, ksc, Wo):
            b, n, _ = x.shape
            qkv = x @ Wqkv
            q, k, v = jnp.split(qkv, 3, -1)
            sh = lambda t: t.reshape(b, n, HEADS, DIM_HEAD).transpose(0, 2, 1, 3)
            q, k, v = (sh(q), sh(k), sh(v))
            q = l2norm(q) * qs
            k = l2norm(k) * ksc
            freqs, scale = rotary_tables(n)
            cos, sin = (jnp.cos(freqs), jnp.sin(freqs))
            q = q * cos * scale + rotate_half(q) * sin * scale
            inv = 1.0 / scale
            k = k * cos * inv + rotate_half(k) * sin * inv
            out = local_attention(q, k, v)
            out = out.transpose(0, 2, 1, 3).reshape(b, n, INNER)
            return out @ Wo

        def ffn_layer(x, g, bln, W1, b1, W2, b2):
            mu = x.mean(-1, keepdims=True)
            var = ((x - mu) ** 2).mean(-1, keepdims=True)
            xn = (x - mu) / jnp.sqrt(var + 1e-05) * g + bln
            hg = xn @ W1 + b1
            a, gate = jnp.split(hg, 2, -1)
            return a * jax.nn.gelu(gate, approximate=False) @ W2 + b2
        key = jax.random.key(seed)
        ks = jax.random.split(key, 8)
        B, N = (2, 256)
        init = lambda k, shape: jax.random.normal(k, shape, jnp.float32) * 0.02
        return {'x': jax.random.normal(ks[0], (B, N, DIM), jnp.float32), 'Wqkv': init(ks[1], (DEPTH, DIM, 3 * INNER)), 'q_scale': jnp.ones((DEPTH, DIM_HEAD), jnp.float32), 'k_scale': jnp.ones((DEPTH, DIM_HEAD), jnp.float32), 'Wo': init(ks[2], (DEPTH, INNER, DIM)), 'ln_g': jnp.ones((DEPTH, DIM), jnp.float32), 'ln_b': jnp.zeros((DEPTH, DIM), jnp.float32), 'W1': init(ks[3], (DEPTH, DIM, 2 * DIM_INNER)), 'b1': jnp.zeros((DEPTH, 2 * DIM_INNER), jnp.float32), 'W2': init(ks[4], (DEPTH, DIM_INNER, DIM)), 'b2': jnp.zeros((DEPTH, DIM), jnp.float32)}
    _L3_ffn_in = _L3_ffn_setup()
    _d = {'L0_attn_x': _L0_attn_in['x'], 'L0_attn_W_in': _L0_attn_in['W_in'], 'L0_attn_b_in': _L0_attn_in['b_in'], 'L0_attn_conv_w': _L0_attn_in['conv_w'], 'L0_attn_conv_b': _L0_attn_in['conv_b'], 'L0_attn_A': _L0_attn_in['A'], 'L0_attn_C': _L0_attn_in['C'], 'L0_attn_Dp': _L0_attn_in['Dp'], 'L0_attn_W_out': _L0_attn_in['W_out'], 'L0_attn_b_out': _L0_attn_in['b_out'], 'L0_ffn_router_w': _L0_ffn_in['router_w'], 'L0_ffn_router_bias': _L0_ffn_in['router_bias'], 'L0_ffn_gate_w': _L0_ffn_in['gate_w'], 'L0_ffn_up_w': _L0_ffn_in['up_w'], 'L0_ffn_down_w': _L0_ffn_in['down_w'], 'L0_ffn_s_gate_w': _L0_ffn_in['s_gate_w'], 'L0_ffn_s_up_w': _L0_ffn_in['s_up_w'], 'L0_ffn_s_down_w': _L0_ffn_in['s_down_w'], 'L1_attn_w_in': _L1_attn_in['w_in'], 'L1_attn_w_out': _L1_attn_in['w_out'], 'L1_attn_w_gate': _L1_attn_in['w_gate'], 'L1_attn_b_gate': _L1_attn_in['b_gate'], 'L1_attn_log_decay': _L1_attn_in['log_decay'], 'L1_attn_frequency': _L1_attn_in['frequency'], 'L1_attn_coupling': _L1_attn_in['coupling'], 'L1_attn_w_mlp1': _L1_attn_in['w_mlp1'], 'L1_attn_b_mlp1': _L1_attn_in['b_mlp1'], 'L1_attn_w_mlp2': _L1_attn_in['w_mlp2'], 'L1_attn_b_mlp2': _L1_attn_in['b_mlp2'], 'L1_attn_ln1_g': _L1_attn_in['ln1_g'], 'L1_attn_ln1_b': _L1_attn_in['ln1_b'], 'L1_attn_ln2_g': _L1_attn_in['ln2_g'], 'L1_attn_ln2_b': _L1_attn_in['ln2_b'], 'L1_ffn_W_fc': _L1_ffn_in['W_fc'], 'L1_ffn_ln_w': _L1_ffn_in['ln_w'], 'L1_ffn_ln_b': _L1_ffn_in['ln_b'], 'L1_ffn_W_proj': _L1_ffn_in['W_proj'], 'L2_attn_wq': _L2_attn_in['wq'], 'L2_attn_bq': _L2_attn_in['bq'], 'L2_attn_wk': _L2_attn_in['wk'], 'L2_attn_bk': _L2_attn_in['bk'], 'L2_attn_wv': _L2_attn_in['wv'], 'L2_attn_bv': _L2_attn_in['bv'], 'L2_attn_wo': _L2_attn_in['wo'], 'L2_attn_bo': _L2_attn_in['bo'], 'L2_ffn_W1': _L2_ffn_in['W1'], 'L2_ffn_b1': _L2_ffn_in['b1'], 'L2_ffn_W2': _L2_ffn_in['W2'], 'L2_ffn_b2': _L2_ffn_in['b2'], 'L3_attn_Wq': _L3_attn_in['Wq'], 'L3_attn_bq': _L3_attn_in['bq'], 'L3_attn_Wk': _L3_attn_in['Wk'], 'L3_attn_bk': _L3_attn_in['bk'], 'L3_attn_Wv': _L3_attn_in['Wv'], 'L3_attn_bv': _L3_attn_in['bv'], 'L3_attn_Wo': _L3_attn_in['Wo'], 'L3_attn_bo': _L3_attn_in['bo'], 'L3_attn_Wfc': _L3_attn_in['Wfc'], 'L3_attn_bfc': _L3_attn_in['bfc'], 'L3_attn_proj': _L3_attn_in['proj'], 'L3_ffn_Wqkv': _L3_ffn_in['Wqkv'], 'L3_ffn_q_scale': _L3_ffn_in['q_scale'], 'L3_ffn_k_scale': _L3_ffn_in['k_scale'], 'L3_ffn_Wo': _L3_ffn_in['Wo'], 'L3_ffn_ln_g': _L3_ffn_in['ln_g'], 'L3_ffn_ln_b': _L3_ffn_in['ln_b'], 'L3_ffn_W1': _L3_ffn_in['W1'], 'L3_ffn_b1': _L3_ffn_in['b1'], 'L3_ffn_W2': _L3_ffn_in['W2'], 'L3_ffn_b2': _L3_ffn_in['b2']}
    _x0 = _d['L0_attn_x']
    _d['L0_attn_x'] = jax.random.normal(jax.random.fold_in(jax.random.key(seed), 1), (4, 512, 128), dtype=_x0.dtype)
    del _x0
    return _d

def reference(L0_attn_x, L0_attn_W_in, L0_attn_b_in, L0_attn_conv_w, L0_attn_conv_b, L0_attn_A, L0_attn_C, L0_attn_Dp, L0_attn_W_out, L0_attn_b_out, L0_ffn_router_w, L0_ffn_router_bias, L0_ffn_gate_w, L0_ffn_up_w, L0_ffn_down_w, L0_ffn_s_gate_w, L0_ffn_s_up_w, L0_ffn_s_down_w, L1_attn_w_in, L1_attn_w_out, L1_attn_w_gate, L1_attn_b_gate, L1_attn_log_decay, L1_attn_frequency, L1_attn_coupling, L1_attn_w_mlp1, L1_attn_b_mlp1, L1_attn_w_mlp2, L1_attn_b_mlp2, L1_attn_ln1_g, L1_attn_ln1_b, L1_attn_ln2_g, L1_attn_ln2_b, L1_ffn_W_fc, L1_ffn_ln_w, L1_ffn_ln_b, L1_ffn_W_proj, L2_attn_wq, L2_attn_bq, L2_attn_wk, L2_attn_bk, L2_attn_wv, L2_attn_bv, L2_attn_wo, L2_attn_bo, L2_ffn_W1, L2_ffn_b1, L2_ffn_W2, L2_ffn_b2, L3_attn_Wq, L3_attn_bq, L3_attn_Wk, L3_attn_bk, L3_attn_Wv, L3_attn_bv, L3_attn_Wo, L3_attn_bo, L3_attn_Wfc, L3_attn_bfc, L3_attn_proj, L3_ffn_Wqkv, L3_ffn_q_scale, L3_ffn_k_scale, L3_ffn_Wo, L3_ffn_ln_g, L3_ffn_ln_b, L3_ffn_W1, L3_ffn_b1, L3_ffn_W2, L3_ffn_b2):

    def _L0_attn_ref(x, W_in, b_in, conv_w, conv_b, A, C, Dp, W_out, b_out):
        import jax, jax.numpy as jnp
        import numpy as np
        D_MODEL = 128
        D_STATE = 16
        D_CONV = 4
        EXPAND = 2
        E = EXPAND * D_MODEL
        B, L = (4, 512)
        Bb, Ll, _ = x.shape
        x_and_z = x @ W_in + b_in
        x_proj, z = jnp.split(x_and_z, 2, axis=-1)
        xc = jnp.transpose(x_proj, (0, 2, 1))
        xc = jax.lax.conv_general_dilated(xc, conv_w, window_strides=(1,), padding=[(D_CONV - 1, 0)], dimension_numbers=('NCH', 'OIH', 'NCH'), feature_group_count=E)
        x_conv = jnp.transpose(xc + conv_b[None, :, None], (0, 2, 1))

        def step(h, xt):
            h = jnp.tanh(xt @ A + h)
            yt = h @ C.T + Dp * xt
            return (h, yt)
        h0 = jnp.zeros((Bb, D_STATE), dtype=x.dtype)
        _, ys = jax.lax.scan(step, h0, jnp.transpose(x_conv, (1, 0, 2)))
        x_s4 = jnp.transpose(ys, (1, 0, 2))
        y = jax.nn.sigmoid(z) * x_s4
        return y @ W_out + b_out

    def _L0_ffn_ref(hidden_states, router_w, router_bias, gate_w, up_w, down_w, s_gate_w, s_up_w, s_down_w):
        import jax, jax.numpy as jnp
        import numpy as np
        K = 4
        ROUTED_SCALING = 1.0
        NORM_TOPK = True

        def _gate(hidden_states, router_w, router_bias):
            logits = jnp.einsum('bsh,he->bse', hidden_states, router_w).astype(jnp.float32)
            scores = jax.nn.softmax(logits, axis=-1)
            corrected = scores + router_bias
            _, top_k_indices = jax.lax.top_k(corrected, K)
            top_k_weights = jnp.take_along_axis(scores, top_k_indices, axis=-1)
            if NORM_TOPK:
                top_k_weights = top_k_weights / (top_k_weights.sum(-1, keepdims=True) + 1e-20)
            top_k_weights = top_k_weights * ROUTED_SCALING
            return (top_k_weights.astype(hidden_states.dtype), top_k_indices)
        B, S, H = hidden_states.shape
        tk_w, tk_i = _gate(hidden_states, router_w, router_bias)
        hf = hidden_states.reshape(-1, H)
        tk_w = tk_w.reshape(-1, K)
        tk_i = tk_i.reshape(-1, K)
        gate_all = jnp.einsum('nh,ehi->nei', hf, gate_w)
        up_all = jnp.einsum('nh,ehi->nei', hf, up_w)
        act = jax.nn.silu(gate_all) * up_all
        down_all = jnp.einsum('nei,eih->neh', act, down_w)
        sel = jnp.take_along_axis(down_all, tk_i[:, :, None], axis=1)
        routed = (sel * tk_w[:, :, None]).sum(axis=1).reshape(B, S, H)
        g = jnp.einsum('bsh,hm->bsm', hidden_states, s_gate_w)
        u = jnp.einsum('bsh,hm->bsm', hidden_states, s_up_w)
        shared = jnp.einsum('bsm,mh->bsh', jax.nn.silu(g) * u, s_down_w)
        return routed + shared

    def _L1_attn_ref(x, w_in, w_out, w_gate, b_gate, log_decay, frequency, coupling, w_mlp1, b_mlp1, w_mlp2, b_mlp2, ln1_g, ln1_b, ln2_g, ln2_b):
        import jax, jax.numpy as jnp
        import numpy as np
        import math
        B, T, D = (4, 512, 128)
        K, H, KH, C = (64, 4, 16, 64)
        MLP = 512
        EPS = 1e-05

        def _layernorm(x, g, b):
            m = jnp.mean(x, axis=-1, keepdims=True)
            v = jnp.mean((x - m) ** 2, axis=-1, keepdims=True)
            return (x - m) / jnp.sqrt(v + EPS) * g + b

        def _chunked_eigenstate(log_decay, frequency, beta_r, beta_i):
            Bt, Tt, Kt = beta_r.shape
            T_pad = (Tt + C - 1) // C * C
            if T_pad > Tt:
                beta_r = jnp.pad(beta_r, ((0, 0), (0, T_pad - Tt), (0, 0)))
                beta_i = jnp.pad(beta_i, ((0, 0), (0, T_pad - Tt), (0, 0)))
            n_chunks = T_pad // C
            mag = jax.nn.sigmoid(log_decay)
            powers = jnp.arange(C, dtype=log_decay.dtype)
            mag_pow = mag[:, None] ** powers[None, :]
            phases = frequency[:, None] * powers[None, :]
            kr = mag_pow * jnp.cos(phases)
            ki = mag_pow * jnp.sin(phases)
            ii = jnp.arange(C)
            idx = ii[None, :] - ii[:, None]
            mask = (idx >= 0).astype(kr.dtype)
            idxc = jnp.clip(idx, 0, C - 1)
            L_r = kr[:, idxc] * mask[None]
            L_i = ki[:, idxc] * mask[None]
            br = beta_r.reshape(Bt, n_chunks, C, Kt)
            bi = beta_i.reshape(Bt, n_chunks, C, Kt)
            intra_r = jnp.einsum('kjs,bnsk->bnjk', L_r, br) - jnp.einsum('kjs,bnsk->bnjk', L_i, bi)
            intra_i = jnp.einsum('kjs,bnsk->bnjk', L_r, bi) + jnp.einsum('kjs,bnsk->bnjk', L_i, br)
            first_col_r = L_r[:, :, 0]
            first_col_i = L_i[:, :, 0]

            def step(carry, intra):
                sr, si = carry
                ir, im = intra
                cr = first_col_r[None] * sr[:, :, None] - first_col_i[None] * si[:, :, None]
                ci = first_col_r[None] * si[:, :, None] + first_col_i[None] * sr[:, :, None]
                o_r = ir + jnp.transpose(cr, (0, 2, 1))
                o_i = im + jnp.transpose(ci, (0, 2, 1))
                return ((o_r[:, -1, :], o_i[:, -1, :]), (o_r, o_i))
            xs = (jnp.transpose(intra_r, (1, 0, 2, 3)), jnp.transpose(intra_i, (1, 0, 2, 3)))
            init = (jnp.zeros((Bt, Kt), beta_r.dtype), jnp.zeros((Bt, Kt), beta_r.dtype))
            _, (out_r, out_i) = jax.lax.scan(step, init, xs)
            c_r = jnp.transpose(out_r, (1, 0, 2, 3)).reshape(Bt, T_pad, Kt)[:, :Tt]
            c_i = jnp.transpose(out_i, (1, 0, 2, 3)).reshape(Bt, T_pad, Kt)[:, :Tt]
            return (c_r, c_i)
        residual = x
        x_norm = _layernorm(x, ln1_g, ln1_b)
        beta = x_norm @ w_in.T
        beta_r, beta_i = jnp.split(beta, 2, axis=-1)
        c_r, c_i = _chunked_eigenstate(log_decay, frequency, beta_r, beta_i)
        c_rh = c_r.reshape(x.shape[0], x.shape[1], H, KH)
        c_ih = c_i.reshape(x.shape[0], x.shape[1], H, KH)
        c_r = jnp.einsum('hjk,bthk->bthj', coupling, c_rh).reshape(x.shape[0], x.shape[1], K)
        c_i = jnp.einsum('hjk,bthk->bthj', coupling, c_ih).reshape(x.shape[0], x.shape[1], K)
        h = jnp.concatenate([c_r, c_i], axis=-1) @ w_out.T
        gate = jax.nn.sigmoid(x_norm @ w_gate.T + b_gate)
        x1 = residual + gate * h
        x2n = _layernorm(x1, ln2_g, ln2_b)
        mlp = jax.nn.silu(x2n @ w_mlp1.T + b_mlp1) @ w_mlp2.T + b_mlp2
        return x1 + mlp

    def _L1_ffn_ref(x, W_fc, ln_w, ln_b, W_proj):
        import jax, jax.numpy as jnp
        import numpy as np
        EPS = 1e-06
        LN_EPS = 1e-05

        def _absmean_core(W):
            gamma = jnp.mean(jnp.abs(W)) + EPS
            Ws = W / gamma
            Wq = jnp.sign(Ws) * jnp.minimum(jnp.round(jnp.abs(Ws)), 1.0)
            return (Wq, gamma)

        @jax.custom_vjp
        def absmean(W):
            return _absmean_core(W)[0]

        def _absmean_fwd(W):
            Wq, gamma = _absmean_core(W)
            return (Wq, gamma)

        def _absmean_bwd(gamma, g):
            return (g / gamma,)
        absmean.defvjp(_absmean_fwd, _absmean_bwd)

        def layernorm(x, w, b, eps=LN_EPS):
            mu = jnp.mean(x, axis=-1, keepdims=True)
            var = jnp.mean((x - mu) ** 2, axis=-1, keepdims=True)
            return (x - mu) * jax.lax.rsqrt(var + eps) * w + b
        h = jnp.einsum('btd,hd->bth', x, absmean(W_fc))
        h = jax.nn.gelu(h, approximate=False)
        h = layernorm(h, ln_w, ln_b)
        return jnp.einsum('bth,dh->btd', h, absmean(W_proj))

    def _L2_attn_ref(x, wq, bq, wk, bk, wv, bv, wo, bo):
        import jax, jax.numpy as jnp
        import numpy as np
        import math
        B, S, E = (2, 256, 128)
        H, DK, DV = (16, 64, 64)

        def _rope(q, k):
            D = q.shape[-1]
            theta = 10000.0 ** (jnp.arange(0, D, 2, dtype=jnp.float32) / D)
            pos = jnp.arange(q.shape[-2], dtype=jnp.float32)
            freqs = pos[:, None] * (1.0 / theta)[None, :]
            emb = jnp.concatenate([freqs, freqs], axis=-1)
            cos = jnp.cos(emb)[None, None]
            sin = jnp.sin(emb)[None, None]

            def rotate(x):
                x1 = x[..., ::2]
                x2 = x[..., 1::2]
                return jnp.stack([-x2, x1], axis=-1).reshape(x.shape)
            return (q * cos + rotate(q) * sin, k * cos + rotate(k) * sin)
        Bx, Sx, Ex = x.shape
        q = (x @ wq.T + bq).reshape(Bx, Sx, H, DK).transpose(0, 2, 1, 3)
        k = (x @ wk.T + bk).reshape(Bx, Sx, H, DK).transpose(0, 2, 1, 3)
        v = (x @ wv.T + bv).reshape(Bx, Sx, H, DV).transpose(0, 2, 1, 3)
        q, k = _rope(q, k)
        scores = jnp.einsum('bhqd,bhkd->bhqk', q, k)
        causal = jnp.triu(jnp.ones((Sx, Sx), dtype=bool), k=1)
        scores = jnp.where(causal[None, None], -jnp.inf, scores)
        attn = jax.nn.softmax(scores / math.sqrt(DK), axis=-1)
        out = jnp.einsum('bhqk,bhkd->bhqd', attn, v)
        out = out.transpose(0, 2, 1, 3).reshape(Bx, Sx, H * DV)
        return out @ wo.T + bo

    def _L2_ffn_ref(hidden_states, W1, b1, W2, b2):
        import jax, jax.numpy as jnp
        import numpy as np
        HIDDEN = 128
        INTER = 512
        h = jax.nn.relu(jnp.einsum('bsh,hi->bsi', hidden_states, W1) + b1)
        return jnp.einsum('bsi,ih->bsh', h, W2) + b2

    def _L3_attn_ref(x, Wq, bq, Wk, bk, Wv, bv, Wo, bo, Wfc, bfc, proj):
        import jax, jax.numpy as jnp
        import numpy as np
        B, N, D, H = (4, 512, 128, 16)
        DH = D // H
        M = int(DH * np.log(DH))
        EPS = 0.0001

        def softmax_kernel(t, proj, is_query):
            dn = t.shape[-1] ** (-0.25)
            ratio = proj.shape[0] ** (-0.5)
            td = jnp.einsum('bhnd,md->bhnm', t * dn, proj)
            diag = 0.5 * dn ** 2 * jnp.sum(t * t, axis=-1, keepdims=True)
            if is_query:
                mx = jnp.max(td, axis=-1, keepdims=True)
            else:
                mx = jnp.max(td, axis=(-1, -2), keepdims=True)
            return ratio * (jnp.exp(td - diag - mx) + EPS)
        b, n, d = x.shape

        def heads(t):
            return t.reshape(b, n, H, DH).transpose(0, 2, 1, 3)
        q = heads(x @ Wq.T + bq)
        k = heads(x @ Wk.T + bk)
        v = heads(x @ Wv.T + bv)
        qp = softmax_kernel(q, proj, is_query=True)
        kp = softmax_kernel(k, proj, is_query=False)
        k_sum = jnp.sum(kp, axis=-2)
        d_inv = 1.0 / jnp.einsum('bhnm,bhm->bhn', qp, k_sum)
        context = jnp.einsum('bhnm,bhnd->bhmd', kp, v)
        out = jnp.einsum('bhmd,bhnm,bhn->bhnd', context, qp, d_inv)
        out = out.transpose(0, 2, 1, 3).reshape(b, n, d)
        h = out @ Wo.T + bo
        return jax.nn.relu(h @ Wfc.T + bfc)

    def _L3_ffn_ref(x, Wqkv, q_scale, k_scale, Wo, ln_g, ln_b, W1, b1, W2, b2):
        import jax, jax.numpy as jnp
        import numpy as np
        DIM = 128
        DEPTH = 6
        HEADS = 16
        DIM_HEAD = 64
        WINDOW = 32
        INNER = HEADS * DIM_HEAD
        DIM_INNER = int(DIM * 4 * 2 / 3)
        QK_SCALE = 8.0

        def shift_tokens(t):
            a, s = jnp.split(t, 2, -1)
            s = jnp.pad(s, ((0, 0), (1, 0), (0, 0)))[:, :-1]
            return jnp.concatenate([a, s], -1)

        def l2norm(t):
            return t / jnp.maximum(jnp.linalg.norm(t, axis=-1, keepdims=True), 1e-12)

        def rotate_half(x):
            x1, x2 = jnp.split(x, 2, -1)
            return jnp.concatenate([-x2, x1], -1)

        def rotary_tables(n):
            half = jnp.arange(0, DIM_HEAD, 2, dtype=jnp.float32)
            inv_freq = 1.0 / 10000.0 ** (half / DIM_HEAD)
            t = jnp.arange(n, dtype=jnp.float32)
            freqs = t[:, None] * inv_freq[None, :]
            freqs = jnp.concatenate([freqs, freqs], -1)
            base_scale = (half + 0.4 * DIM_HEAD) / (1.4 * DIM_HEAD)
            power = (t - n // 2) / (WINDOW // 2)
            scale = base_scale[None, :] ** power[:, None]
            scale = jnp.concatenate([scale, scale], -1)
            return (freqs, scale)

        def local_attention(q, k, v):
            b, h, n, d = q.shape
            w = WINDOW
            nw = n // w
            bq = q.reshape(b, h, nw, w, d)
            bk = k.reshape(b, h, nw, w, d)
            bv = v.reshape(b, h, nw, w, d)

            def look(t):
                p = jnp.pad(t, ((0, 0), (0, 0), (1, 0), (0, 0), (0, 0)))
                return jnp.concatenate([p[:, :, :nw], p[:, :, 1:]], axis=3)
            bk2, bv2 = (look(bk), look(bv))
            seq = jnp.arange(n).reshape(nw, w)
            seq_p = jnp.pad(seq, ((1, 0), (0, 0)), constant_values=-1)
            jt = jnp.concatenate([seq_p[:nw], seq_p[1:]], axis=1)
            it = seq[:, :, None]
            jb = jt[:, None, :]
            mask = (it < jb) | (it > jb + w) | (jb == -1)
            sim = jnp.einsum('bhwie,bhwje->bhwij', bq, bk2) * QK_SCALE
            sim = jnp.where(mask, -jnp.finfo(sim.dtype).max, sim)
            attn = jax.nn.softmax(sim, -1)
            out = jnp.einsum('bhwij,bhwje->bhwie', attn, bv2)
            return out.reshape(b, h, n, d)

        def attn_layer(x, Wqkv, qs, ksc, Wo):
            b, n, _ = x.shape
            qkv = x @ Wqkv
            q, k, v = jnp.split(qkv, 3, -1)
            sh = lambda t: t.reshape(b, n, HEADS, DIM_HEAD).transpose(0, 2, 1, 3)
            q, k, v = (sh(q), sh(k), sh(v))
            q = l2norm(q) * qs
            k = l2norm(k) * ksc
            freqs, scale = rotary_tables(n)
            cos, sin = (jnp.cos(freqs), jnp.sin(freqs))
            q = q * cos * scale + rotate_half(q) * sin * scale
            inv = 1.0 / scale
            k = k * cos * inv + rotate_half(k) * sin * inv
            out = local_attention(q, k, v)
            out = out.transpose(0, 2, 1, 3).reshape(b, n, INNER)
            return out @ Wo

        def ffn_layer(x, g, bln, W1, b1, W2, b2):
            mu = x.mean(-1, keepdims=True)
            var = ((x - mu) ** 2).mean(-1, keepdims=True)
            xn = (x - mu) / jnp.sqrt(var + 1e-05) * g + bln
            hg = xn @ W1 + b1
            a, gate = jnp.split(hg, 2, -1)
            return a * jax.nn.gelu(gate, approximate=False) @ W2 + b2
        for i in range(DEPTH):
            x = attn_layer(shift_tokens(x), Wqkv[i], q_scale[i], k_scale[i], Wo[i]) + x
            x = ffn_layer(shift_tokens(x), ln_g[i], ln_b[i], W1[i], b1[i], W2[i], b2[i]) + x
        return x
    x = L0_attn_x
    x = _layernorm(x + _L0_attn_ref(x, L0_attn_W_in, L0_attn_b_in, L0_attn_conv_w, L0_attn_conv_b, L0_attn_A, L0_attn_C, L0_attn_Dp, L0_attn_W_out, L0_attn_b_out), axis=-1)
    x = _layernorm(x + _L0_ffn_ref(x, L0_ffn_router_w, L0_ffn_router_bias, L0_ffn_gate_w, L0_ffn_up_w, L0_ffn_down_w, L0_ffn_s_gate_w, L0_ffn_s_up_w, L0_ffn_s_down_w), axis=-1)
    x = _layernorm(x + _L1_attn_ref(x, L1_attn_w_in, L1_attn_w_out, L1_attn_w_gate, L1_attn_b_gate, L1_attn_log_decay, L1_attn_frequency, L1_attn_coupling, L1_attn_w_mlp1, L1_attn_b_mlp1, L1_attn_w_mlp2, L1_attn_b_mlp2, L1_attn_ln1_g, L1_attn_ln1_b, L1_attn_ln2_g, L1_attn_ln2_b), axis=-1)
    x = _layernorm(x + _L1_ffn_ref(x, L1_ffn_W_fc, L1_ffn_ln_w, L1_ffn_ln_b, L1_ffn_W_proj), axis=-1)
    x = _layernorm(x + _L2_attn_ref(x, L2_attn_wq, L2_attn_bq, L2_attn_wk, L2_attn_bk, L2_attn_wv, L2_attn_bv, L2_attn_wo, L2_attn_bo), axis=-1)
    x = _layernorm(x + _L2_ffn_ref(x, L2_ffn_W1, L2_ffn_b1, L2_ffn_W2, L2_ffn_b2), axis=-1)
    x = _layernorm(x + _L3_attn_ref(x, L3_attn_Wq, L3_attn_bq, L3_attn_Wk, L3_attn_bk, L3_attn_Wv, L3_attn_bv, L3_attn_Wo, L3_attn_bo, L3_attn_Wfc, L3_attn_bfc, L3_attn_proj), axis=-1)
    x = _layernorm(x + _L3_ffn_ref(x, L3_ffn_Wqkv, L3_ffn_q_scale, L3_ffn_k_scale, L3_ffn_Wo, L3_ffn_ln_g, L3_ffn_ln_b, L3_ffn_W1, L3_ffn_b1, L3_ffn_W2, L3_ffn_b2), axis=-1)
    return x

_drawn_inputs = setup_inputs


def setup_inputs(seed=0):
    import zlib

    import numpy as np

    out = dict(_drawn_inputs(seed))
    spreads = {'L0_attn_b_in': (0.0, 0.8),
     'L0_attn_conv_b': (0.0, 0.8),
     'L0_attn_Dp': (0.009999999776482582, 0.6),
     'L0_attn_b_out': (0.0, 0.1),
     'L1_attn_b_gate': (-2.0, 0.2),
     'L1_attn_b_mlp1': (0.0, 0.1),
     'L1_attn_b_mlp2': (0.0, 0.1),
     'L1_attn_ln1_g': (1.0, 0.2),
     'L1_attn_ln1_b': (0.0, 0.444),
     'L1_attn_ln2_g': (1.0, 0.2),
     'L1_attn_ln2_b': (0.0, 0.1),
     'L1_ffn_ln_w': (1.0, 0.2),
     'L1_ffn_ln_b': (0.0, 0.1),
     'L3_attn_bq': (0.0, 2.0),
     'L3_attn_bk': (0.0, 2.0),
     'L3_attn_bv': (0.0, 0.8),
     'L3_attn_bo': (0.0, 0.48),
     'L3_attn_bfc': (0.0, 0.1),
     'L3_ffn_q_scale': (1.0, 0.6),
     'L3_ffn_k_scale': (1.0, 0.6),
     'L3_ffn_ln_g': (1.0, 0.6),
     'L3_ffn_ln_b': (0.0, 0.8),
     'L3_ffn_b1': (0.0, 0.8),
     'L3_ffn_b2': (0.0, 0.1)}
    factors = {'L0_attn_W_in': 8.0,
     'L0_attn_conv_w': 8.0,
     'L0_attn_A': 8.0,
     'L0_attn_C': 8.0,
     'L0_attn_W_out': 8.0,
     'L0_ffn_router_w': 8.0,
     'L0_ffn_gate_w': 8.0,
     'L0_ffn_up_w': 8.0,
     'L0_ffn_down_w': 8.0,
     'L0_ffn_s_gate_w': 6.114,
     'L0_ffn_s_up_w': 6.044,
     'L0_ffn_s_down_w': 6.034,
     'L1_attn_log_decay': 70.552,
     'L2_attn_wq': 3.939,
     'L2_attn_bq': 8.0,
     'L2_attn_wk': 3.92,
     'L2_attn_bk': 8.0,
     'L2_attn_bo': 3.138,
     'L2_ffn_b1': 5.134,
     'L2_ffn_b2': 3.42,
     'L3_attn_Wq': 200.0,
     'L3_attn_Wk': 64.0,
     'L3_attn_Wv': 8.0,
     'L3_attn_Wo': 8.0,
     'L3_attn_Wfc': 3.047,
     'L3_attn_proj': 200.0,
     'L3_ffn_W1': 3.769,
     'L3_ffn_W2': 3.745,
     'L1_attn_frequency': 7.847}
    for name, (base, spread) in spreads.items():
        noise = np.random.default_rng([zlib.crc32(name.encode()), seed]).standard_normal(out[name].shape)
        drawn = base * np.exp(spread * noise) if base else spread * noise
        out[name] = jnp.asarray(drawn.astype(out[name].dtype))
    for name, factor in factors.items():
        out[name] = (out[name] * factor).astype(out[name].dtype)
    return out
```

```python
from contextlib import ExitStack, contextmanager

import numpy as np

import concourse.bass as bass
from concourse import mybir

F32 = mybir.dt.float32
BF16 = mybir.dt.bfloat16
ALU = mybir.AluOpType
ACT = mybir.ActivationFunctionType
AX_X = mybir.AxisListType.X
ds = bass.ds

P = 128
B, L, D = 4, 512, 128
NT = L // P
LN_EPS = 1e-5
FIRST_SEMAPHORE = 110
MASKED = -1e30


class Signals:

    def __init__(self, nc, ctx, stage, names):
        self.nums = []
        self.of = {}
        for i, n in enumerate(names.split()):
            s = ctx.enter_context(nc.semaphore(f"{stage}_{n}", num=FIRST_SEMAPHORE + i))
            self.nums.append(s.num)
            self.of[n] = s

    def __getitem__(self, name):
        return self.of[name]


@contextmanager
def stage(nc, name, signals):
    with ExitStack() as ctx:
        s = Signals(nc, ctx, name, signals)
        with nc.Block(no_gpsimd_drain=True) as block:
            yield block, s
        nc.all_engine_barrier(sems_to_clear=range(min(s.nums), max(s.nums) + 1))



NORM_SIGNALS = " sum_ready stats_ready moments_ready eps_added rstd_ready"


class NormBuffers:
    def __init__(self, sb):
        self.r = sb("norm_sum", [P, NT, D])
        self.stats = sb("norm_stats", [P, NT, 6])
        self.moments = sb("norm_moments", [P, NT, 2])
        self.veps = sb("norm_veps", [P, NT])
        self.rstd = sb("norm_rstd", [P, NT])


def vector_moments(e, s, nb, value, round_=0):
    for t in range(NT):
        e.wait_ge(s["sum_ready"], NT * round_ + t + 1)
        e.bn_stats(nb.stats[:, t], value(t)).then_inc(s["stats_ready"], 1)
    for t in range(NT):
        e.wait_ge(s["stats_ready"], NT * round_ + t + 1)
        e.bn_aggr(nb.moments[:, t], nb.stats[:, t]).then_inc(s["moments_ready"], 1)


def pool_rstd(e, s, nb, half, eps=LN_EPS, round_=0):
    e.wait_ge(s["moments_ready"], NT * (round_ + 1))
    e.tensor_scalar(nb.veps[:], nb.moments[:, :, 1], eps, None, ALU.add).then_inc(s["eps_added"], 1)
    e.wait_ge(s["eps_added"], round_ + 1)
    e.tensor_tensor(nb.rstd[:], nb.veps[:], half.to_broadcast([P, NT]), ALU.pow).then_inc(s["rstd_ready"], 1)


def vector_normalize(e, s, nb, value, out, round_=0, signal=None):
    e.wait_ge(s["rstd_ready"], round_ + 1)
    for t in range(NT):
        i = e.tensor_scalar(out(t), value(t), nb.moments[:, t, 0:1], nb.rstd[:, t:t + 1],
                            ALU.subtract, ALU.mult)
        if signal is not None:
            i.then_inc(s[signal], 1)



E0 = 256
NS = 16
TAPS = 4
SCAN_STEPS = 8


def recurrence_stage(nc, ps, x_dram, x_all, W, C, CE, half, nb):
    EC = E0 // P
    with ExitStack() as ctx:
        sbl = lambda n, shape: ctx.enter_context(nc.sbuf_tensor(n, shape, F32))
        xT = sbl("r_xT", [P, B, L])
        xp = sbl("r_xp", [P, EC, B, TAPS - 1 + L])
        xconv = sbl("r_xconv", [P, EC, B, L])
        sig = sbl("r_sig", [P, EC, B, L])
        h = sbl("r_h", [P, 1 + L])
        u = ps[5]
        names = ("x_loaded w_rest early_loaded w_loaded c_loaded xT_psum xT_ready xp_psum xp_ready z_psum sig_ready pad_zero tap_done "
                 "conv_ready u_ready h_zero h_step scan_done ch_psum skip_done y_ready out_psum out_read" + NORM_SIGNALS)
        with stage(nc, "rec", names) as (block, s):
            @block.sync
            def _(e):
                e.dma_start(C.all[:], C.dram).then_inc(s["c_loaded"], 16)
                e.dma_start(x_all[:], x_dram.rearrange("b (j p) d -> p (b j) d", p=P)).then_inc(s["x_loaded"], 16)
                e.dma_start(W.all[:, 0:W.first], W.dram[:, 0:W.first]).then_inc(s["w_loaded"], 16)
                e.dma_start(W.all[:, W.first:], W.dram[:, W.first:]).then_inc(s["w_rest"], 16)
                e.dma_start(CE.all[:], CE.dram).then_inc(s["early_loaded"], 16)
                e.wait_ge(s["w_rest"], 16)
                e.wait_ge(s["early_loaded"], 16)

            @block.tensor
            def _(e):
                e.wait_ge(s["x_loaded"], 16)
                e.wait_ge(s["c_loaded"], 16)
                e.wait_ge(s["w_loaded"], 16)
                for b in range(B):
                    if b >= 1:
                        e.wait_ge(s["xT_ready"], b)
                    for t in range(NT):
                        mm = e.transpose(ps[0][:, t * P:(t + 1) * P], x_all[:, NT * b + t, :], C["ident"])
                    mm.then_inc(s["xT_psum"], 1)
                    e.wait_ge(s["xT_ready"], b + 1)
                    for c in range(EC):
                        if b >= 1:
                            e.wait_ge(s["xp_ready"], EC * (b - 1) + c + 1)
                        e.matmul(ps[1 + c][:], W["L0_W_in"][:, c * P:(c + 1) * P], xT[:, b], start=True,
                                 stop=True).then_inc(s["xp_psum"], 1)
                    for c in range(EC):
                        if b >= 1:
                            e.wait_ge(s["sig_ready"], EC * (b - 1) + c + 1)
                        e.matmul(ps[3 + c][:], W["L0_W_in"][:, E0 + c * P:E0 + (c + 1) * P], xT[:, b], start=True,
                                 stop=True).then_inc(s["z_psum"], 1)
                for b in range(B):
                    e.wait_ge(s["conv_ready"], EC * (b + 1))
                    for c in range(EC):
                        mm = e.matmul(u[32 * b:32 * b + 32, :], W["L0_A"][:, 32 * c:32 * c + 32], xconv[:, c, b],
                                      start=(c == 0), stop=(c == EC - 1))
                    mm.then_inc(s["u_ready"], 1)
                e.wait_ge(s["scan_done"], 1)
                for b in range(B):
                    for c in range(EC):
                        if b >= 1:
                            e.wait_ge(s["skip_done"], EC * (b - 1) + c + 1)
                        e.matmul(ps[1 + c][:], W["L0_CT"][32 * b:32 * b + 32, c * P:(c + 1) * P],
                                 h[32 * b:32 * b + 32, 1:], start=True, stop=True).then_inc(s["ch_psum"], 1)
                    e.wait_ge(s["y_ready"], EC * (b + 1))
                    if b >= 2:
                        e.wait_ge(s["out_read"], NT * (b - 1))
                    for t in range(NT):
                        o = ps[6 + b % 2][:, t * P:(t + 1) * P]
                        e.matmul(o, C["ones"][0:1, :], W["L0_b_out"][0:1, :], start=True, stop=False)
                        for c in range(EC):
                            mm = e.matmul(o, xconv[:, c, b, t * P:(t + 1) * P], W["L0_W_out"][:, c * P:(c + 1) * P],
                                          start=False, stop=(c == EC - 1))
                    mm.then_inc(s["out_psum"], 1)

            @block.vector
            def _(e):
                for c in range(EC):
                    e.memset(xp[:, c, :, 0:TAPS - 1], 0.0).then_inc(s["pad_zero"], 1)
                e.memset(h[:, 0:1], 0.0).then_inc(s["h_zero"], 1)
                e.wait_ge(s["pad_zero"], EC)
                e.wait_ge(s["w_loaded"], 16)
                taps = 0
                for b in range(B):
                    e.wait_ge(s["xT_psum"], b + 1)
                    e.tensor_copy(xT[:, b], ps[0][:]).then_inc(s["xT_ready"], 1)
                    for c in range(EC):
                        e.wait_ge(s["xp_psum"], EC * b + c + 1)
                        e.tensor_scalar(xp[:, c, b, TAPS - 1:], ps[1 + c][:], W["L0_b_in"][:, c:c + 1], None,
                                        ALU.add).then_inc(s["xp_ready"], 1)
                    for c in range(EC):
                        cw = W["L0_conv_w"][:, TAPS * c:TAPS * (c + 1)]
                        e.wait_ge(s["xp_ready"], EC * b + c + 1)
                        e.tensor_scalar(xconv[:, c, b], xp[:, c, b, 0:L], cw[:, 0:1], W["L0_conv_b"][:, c:c + 1],
                                        ALU.mult, ALU.add).then_inc(s["tap_done"], 1)
                        taps += 1
                        for k in range(1, TAPS):
                            e.wait_ge(s["tap_done"], taps)
                            i = e.scalar_tensor_tensor(xconv[:, c, b], xp[:, c, b, k:k + L], cw[:, k:k + 1],
                                                       xconv[:, c, b], ALU.mult, ALU.add)
                            i.then_inc(s["tap_done" if k < TAPS - 1 else "conv_ready"], 1)
                            taps += k < TAPS - 1
                for b in range(B):
                    for c in range(EC):
                        e.wait_ge(s["ch_psum"], EC * b + c + 1)
                        e.wait_ge(s["conv_ready"], EC * b + c + 1)
                        e.scalar_tensor_tensor(xconv[:, c, b], xconv[:, c, b], W["L0_Dp"][:, c:c + 1], ps[1 + c][:],
                                               ALU.mult, ALU.add).then_inc(s["skip_done"], 1)
                        e.wait_ge(s["skip_done"], EC * b + c + 1)
                        e.wait_ge(s["sig_ready"], EC * b + c + 1)
                        e.tensor_tensor(xconv[:, c, b], xconv[:, c, b], sig[:, c, b], ALU.mult).then_inc(s["y_ready"], 1)
                    e.wait_ge(s["out_psum"], b + 1)
                    for t in range(NT):
                        e.tensor_tensor(nb.r[:, t], ps[6 + b % 2][:, t * P:(t + 1) * P], x_all[:, NT * b + t, :],
                                        ALU.add).then_inc(s["sum_ready"], 1)
                    e.wait_ge(s["sum_ready"], NT * (b + 1))
                    e.sem_inc(s["out_read"], NT)
                    vector_moments(e, s, nb, lambda t: nb.r[:, t], round_=b)
                    vector_normalize(e, s, nb, lambda t: nb.r[:, t], lambda t: x_all[:, NT * b + t, :], round_=b)

            @block.scalar
            def _(e):
                e.wait_ge(s["w_loaded"], 16)
                for b in range(B):
                    for c in range(EC):
                        e.wait_ge(s["z_psum"], EC * b + c + 1)
                        e.activation(sig[:, c, b], ps[3 + c][:], ACT.Sigmoid,
                                     bias=W["L0_b_in"][:, EC + c:EC + c + 1]).then_inc(s["sig_ready"], 1)
                e.wait_ge(s["h_zero"], 1)
                e.wait_ge(s["u_ready"], B)
                with e.Fori(0, L // SCAN_STEPS) as i:
                    for k in range(SCAN_STEPS):
                        if k:
                            e.wait_ge(s["h_step"], k)
                        e.activation(h[:, ds(i * SCAN_STEPS + k + 1, 1)], u[:, ds(i * SCAN_STEPS + k, 1)], ACT.Tanh,
                                     bias=h[:, ds(i * SCAN_STEPS + k, 1)]).then_inc(s["h_step"], 1)
                    e.wait_ge(s["h_step"], SCAN_STEPS)
                    e.sem_clear(s["h_step"])
                e.sem_inc(s["scan_done"], 1)

            @block.gpsimd
            def _(e):
                for b in range(B):
                    pool_rstd(e, s, nb, half, round_=b)



BATCH_SIGNALS = " x_copied xT_psum xT_ready out_psum" + NORM_SIGNALS


def vector_take(e, s, x_all, b, xc):
    e.tensor_copy(xc[:], x_all[:, ds(NT * b, NT), :]).then_inc(s["x_copied"], 1)


def tensor_turn(e, src, bank, ident, signal):
    for t in range(NT):
        mm = e.transpose(bank[:, t * P:(t + 1) * P], src(t), ident)
    mm.then_inc(signal, 1)


def vector_finish(e, s, nb, y, xc, x_all, b, extra=None):
    e.wait_ge(s["out_psum"], 1)
    for t in range(NT):
        e.tensor_tensor(nb.r[:, t], y(t), xc[:, t], ALU.add).then_inc(s["sum_ready"], 1)
    vector_moments(e, s, nb, lambda t: nb.r[:, t])
    vector_normalize(e, s, nb, lambda t: nb.r[:, t], lambda t: x_all[:, ds(NT * b + t, 1), :])



NE, TOPK = 8, 4
IE = 64
ISH = 256
PAIRS = NE * IE // P
CHUNKS = PAIRS + ISH // P


def experts_stage(nc, ps, x_all, W, C, half, nb, xc, xT):
    with ExitStack() as ctx:
        sbl = lambda n, shape: ctx.enter_context(nc.sbuf_tensor(n, shape, F32))
        g = sbl("moe_silu", [P, 2, L])
        prod = sbl("moe_prod", [P, CHUNKS, L])
        mx = sbl("moe_max", [P, NT])
        lg = sbl("moe_logits", [P, NT, NE])
        ex = sbl("moe_exp", [P, NT, NE])
        sm = sbl("moe_sum", [P, NT])
        rs = sbl("moe_rsum", [P, NT])
        sc = sbl("moe_scores", [P, NT, NE])
        co = sbl("moe_corrected", [P, NT, NE])
        gt = sbl("moe_greater", [P, NT, NE, NE])
        eq = sbl("moe_equal", [P, NT, NE, NE])
        rank = sbl("moe_rank", [P, NT, NE])
        picked = sbl("moe_picked", [P, NT, NE])
        w = sbl("moe_weight", [P, NT, NE])
        wT = sbl("moe_weightT", [NE, L])
        names = ("logits_psum shifted exp_ready route w_ready wT_psum wT_ready spread_psum spread_read "
                 "gate_psum up_psum silu_ready up_read prod_ready" + BATCH_SIGNALS)
        bc = lambda ap, shape: ap.to_broadcast(shape)
        with nc.Fori(0, B) as b:
            with stage(nc, "moe", names) as (block, s):
                @block.tensor
                def _(e):
                    e.wait_ge(s["x_copied"], 1)
                    tensor_turn(e, lambda t: xc[:, t], ps[0], C["ident"], s["xT_psum"])
                    e.wait_ge(s["xT_ready"], 1)
                    for t in range(NT):
                        mm = e.matmul(ps[1][:, t * NE:(t + 1) * NE], xT[:, t * P:(t + 1) * P], W["moe_router"],
                                      start=True, stop=True)
                    mm.then_inc(s["logits_psum"], 1)

                    def expand(c):
                        if c >= 2:
                            e.wait_ge(s["silu_ready"], c - 1)
                            e.wait_ge(s["up_read"], c - 1)
                        e.matmul(ps[2 + c % 2][:], W["moe_gate"][:, c * P:(c + 1) * P], xT[:], start=True,
                                 stop=True).then_inc(s["gate_psum"], 1)
                        e.matmul(ps[4 + c % 2][:], W["moe_up"][:, c * P:(c + 1) * P], xT[:], start=True,
                                 stop=True).then_inc(s["up_psum"], 1)

                    expand(0)
                    expand(1)
                    e.wait_ge(s["w_ready"], 1)
                    for t in range(NT):
                        mm = e.transpose(ps[6][0:NE, t * P:(t + 1) * P], w[:, t, :], C["ident"])
                    mm.then_inc(s["wT_psum"], 1)
                    e.wait_ge(s["wT_ready"], 1)
                    for c in range(CHUNKS):
                        if c >= 2:
                            expand(c)
                        if c < PAIRS:
                            if c >= 1:
                                e.wait_ge(s["spread_read"], c)
                            e.matmul(ps[0][:], C["pair_of_expert"][0:NE, c * P:(c + 1) * P], wT[:], start=True,
                                     stop=True).then_inc(s["spread_psum"], 1)
                    e.wait_ge(s["prod_ready"], CHUNKS)
                    for t in range(NT):
                        for c in range(CHUNKS):
                            mm = e.matmul(ps[7][:, t * P:(t + 1) * P], prod[:, c, t * P:(t + 1) * P],
                                          W["moe_down"][:, c * P:(c + 1) * P], start=(c == 0), stop=(c == CHUNKS - 1))
                    mm.then_inc(s["out_psum"], 1)

                @block.scalar
                def _(e):
                    e.wait_ge(s["xT_psum"], 1)
                    e.activation(xT[:], ps[0][:], ACT.Copy).then_inc(s["xT_ready"], 1)
                    e.wait_ge(s["shifted"], 1)
                    e.activation(ex[:], lg[:], ACT.Exp).then_inc(s["exp_ready"], 1)
                    for c in range(CHUNKS):
                        if c >= 2:
                            e.wait_ge(s["up_read"], c - 1)
                        e.wait_ge(s["gate_psum"], c + 1)
                        e.activation(g[:, c % 2], ps[2 + c % 2][:], ACT.Silu).then_inc(s["silu_ready"], 1)

                @block.vector
                def _(e):
                    vector_take(e, s, x_all, b, xc)
                    n = [0]

                    def routed(i):
                        n[0] += 1
                        i.then_inc(s["route"], 1)
                        e.wait_ge(s["route"], n[0])

                    s3, s4 = [P, NT, NE], [P, NT, NE, NE]
                    logits = ps[1][:, 0:NT * NE].rearrange("p (t e) -> p t e", e=NE)
                    e.wait_ge(s["logits_psum"], 1)
                    routed(e.tensor_reduce(mx[:], logits, AX_X, ALU.max))
                    e.tensor_tensor(lg[:], logits, bc(mx[:].unsqueeze(2), s3), ALU.subtract).then_inc(s["shifted"], 1)
                    e.wait_ge(s["exp_ready"], 1)
                    routed(e.tensor_reduce(sm[:], ex[:], AX_X, ALU.add))
                    routed(e.reciprocal(rs[:], sm[:]))
                    routed(e.tensor_tensor(sc[:], ex[:], bc(rs[:].unsqueeze(2), s3), ALU.mult))
                    routed(e.tensor_scalar(co[:], sc[:], W["moe_router_bias"], None, ALU.add))
                    other, own = bc(co[:].unsqueeze(2), s4), bc(co[:].unsqueeze(3), s4)
                    first = bc(C["comes_first"].rearrange("p (i j) -> p i j", j=NE).unsqueeze(1), s4)
                    e.tensor_tensor(gt[:], other, own, ALU.is_gt)
                    routed(e.tensor_tensor(eq[:], other, own, ALU.is_equal))
                    routed(e.tensor_tensor(eq[:], eq[:], first, ALU.mult))
                    routed(e.tensor_tensor(gt[:], gt[:], eq[:], ALU.add))
                    routed(e.tensor_reduce(rank[:], gt[:], AX_X, ALU.add))
                    routed(e.scalar_tensor_tensor(picked[:], rank[:], TOPK - 0.5, sc[:], ALU.is_lt, ALU.mult))
                    routed(e.tensor_reduce(sm[:], picked[:], AX_X, ALU.add))
                    routed(e.tensor_scalar(sm[:], sm[:], 1e-20, None, ALU.add))
                    routed(e.reciprocal(rs[:], sm[:]))
                    e.tensor_tensor(w[:], picked[:], bc(rs[:].unsqueeze(2), s3), ALU.mult).then_inc(s["w_ready"], 1)
                    e.wait_ge(s["wT_psum"], 1)
                    e.tensor_copy(wT[:], ps[6][0:NE, :]).then_inc(s["wT_ready"], 1)
                    for c in range(CHUNKS):
                        e.wait_ge(s["silu_ready"], c + 1)
                        e.wait_ge(s["up_psum"], c + 1)
                        i = e.tensor_tensor(prod[:, c], g[:, c % 2], ps[4 + c % 2][:], ALU.mult)
                        i.then_inc(s["up_read"], 1)
                        if c >= PAIRS:
                            e.wait_ge(s["up_read"], c + 1)
                            e.sem_inc(s["prod_ready"], 1)
                            continue
                        e.wait_ge(s["up_read"], c + 1)
                        e.wait_ge(s["spread_psum"], c + 1)
                        e.tensor_tensor(prod[:, c], prod[:, c], ps[0][:], ALU.mult).then_inc(s["prod_ready"], 1)
                        e.wait_ge(s["prod_ready"], c + 1)
                        e.sem_inc(s["spread_read"], 1)
                    vector_finish(e, s, nb, lambda t: ps[7][:, t * P:(t + 1) * P], xc, x_all, b)

                @block.gpsimd
                def _(e):
                    pool_rstd(e, s, nb, half)



KS = 64
CH = 64
NCH = L // CH
MLP1 = 512
TWO_PI_1, TWO_PI_2 = 6.28125, 0.0019350051879882812
TWO_PI_3 = 2 * np.pi - TWO_PI_1 - TWO_PI_2
ROUND = 1.5 * 2.0 ** 23


class Eigen:
    def __init__(self, sb):
        self.cos = sb("eig_cos", [P, CH])
        self.sin = sb("eig_sin", [P, CH])
        self.minus_sin = sb("eig_minus_sin", [P, CH])
        self.decay = sb("eig_decay", [P, NCH, CH])
        self.joined = sb("eig_joined", [P, D])


def eigen_tables_stage(nc, ps, W, C, eg):
    with ExitStack() as ctx:
        sbl = lambda n, shape: ctx.enter_context(nc.sbuf_tensor(n, shape, F32))
        ph, n_, r, sh, c2, s1 = (sbl(f"eigt_{k}", [P, CH]) for k in ("phase", "turns", "rest", "half", "sq", "sin"))
        mag, hold = sbl("eigt_mag", [P, 1]), sbl("eigt_hold", [P, CH])
        with stage(nc, "eigt", "vec mag_ready rest_ready sines_ready joined_psum") as (block, s):
            @block.tensor
            def _(e):
                e.matmul(ps[0][:, 0:D], W["L1_coupling"], W["L1_w_out"], start=True, stop=True).then_inc(s["joined_psum"], 1)

            @block.scalar
            def _(e):
                e.activation(mag[:], W["L1_log_decay"], ACT.Sigmoid).then_inc(s["mag_ready"], 1)
                e.wait_ge(s["rest_ready"], 1)
                e.activation(s1[:], r[:], ACT.Sin).then_inc(s["sines_ready"], 1)
                e.activation(sh[:], r[:], ACT.Sin, scale=0.5).then_inc(s["sines_ready"], 1)

            @block.vector
            def _(e):
                n = [0]

                def then(i):
                    n[0] += 1
                    i.then_inc(s["vec"], 1)
                    e.wait_ge(s["vec"], n[0])

                then(e.tensor_scalar(ph[:], C["steps"], W["L1_frequency"], None, ALU.mult))
                then(e.tensor_scalar(n_[:], ph[:], 1 / (2 * np.pi), ROUND, ALU.mult, ALU.add))
                then(e.tensor_scalar(n_[:], n_[:], -ROUND, None, ALU.add))
                then(e.scalar_tensor_tensor(r[:], n_[:], -TWO_PI_1, ph[:], ALU.mult, ALU.add))
                then(e.scalar_tensor_tensor(r[:], n_[:], -TWO_PI_2, r[:], ALU.mult, ALU.add))
                then(e.scalar_tensor_tensor(r[:], n_[:], -TWO_PI_3, r[:], ALU.mult, ALU.add))
                e.tensor_scalar(r[:], r[:], 3.1415925, -3.1415925, ALU.min, ALU.max).then_inc(s["rest_ready"], 1)
                e.wait_ge(s["joined_psum"], 1)
                e.tensor_copy(eg.joined[:], ps[0][:, 0:D])
                e.wait_ge(s["mag_ready"], 1)
                then(e.tensor_scalar(hold[:], C["not_first"], mag[:], None, ALU.mult))
                e.tensor_copy(eg.decay[:], hold[:].unsqueeze(1).to_broadcast([P, NCH, CH]))
                e.wait_ge(s["sines_ready"], 2)
                then(e.tensor_tensor(c2[:], sh[:], sh[:], ALU.mult))
                then(e.tensor_scalar(eg.cos[:], c2[:], -2.0, 1.0, ALU.mult, ALU.add))
                then(e.tensor_scalar(eg.sin[:], s1[:], C["half_sign"], None, ALU.mult))
                e.tensor_scalar(eg.minus_sin[:], eg.sin[:], -1.0, None, ALU.mult)


def eigen_stage(nc, ps, x_all, W, C, half, nb, xc, xT, eg):
    with ExitStack() as ctx:
        sbl = lambda n, shape: ctx.enter_context(nc.sbuf_tensor(n, shape, F32))
        xn = sbl("eig_xn", [P, NT, D])
        z, z2, dd = sbl("eig_z", [P, NCH, CH]), sbl("eig_z2", [P, NCH, CH]), sbl("eig_d", [P, NCH, CH])
        cc = sbl("eig_c", [P, L])
        gate = sbl("eig_gate", [P, NT, D])
        x1 = sbl("eig_x1", [P, NT, D])
        hid = sbl("eig_hid", [P, MLP1 // P, L])
        names = ("x_copied xn_ready xT_psum xT_ready beta_psum turned_in z_ready "
                 "c_whole d_ready swap2_psum c_half c_ready gate_psum gate_ready h_psum gated x1_ready "
                 "mlp_psum mlp_ready out_psum" + NORM_SIGNALS)
        wide = [P, NCH, CH]
        bc = lambda ap: ap.unsqueeze(1).to_broadcast(wide)
        chunked = lambda ap: ap.rearrange("p (n j) -> p n j", j=CH)
        HC = MLP1 // P
        with nc.Fori(0, B) as b:
            with stage(nc, "eig", names) as (block, s):
                @block.tensor
                def _(e):
                    e.wait_ge(s["xn_ready"], NT)
                    tensor_turn(e, lambda t: xn[:, t], ps[0], C["ident"], s["xT_psum"])
                    e.wait_ge(s["xT_ready"], 1)
                    e.matmul(ps[1][:], W["L1_w_in"], xT[:], start=True, stop=True).then_inc(s["beta_psum"], 1)
                    e.matmul(ps[2][:], W["L1_w_in_swapped"], xT[:], start=True, stop=True).then_inc(s["beta_psum"], 1)
                    for t in range(NT):
                        o = ps[3][:, t * P:(t + 1) * P]
                        e.matmul(o, C["ones"][0:1, :], W["L1_b_gate"][0:1, :], start=True, stop=False)
                        mm = e.matmul(o, xT[:, t * P:(t + 1) * P], W["L1_w_gate"], start=False, stop=True)
                    mm.then_inc(s["gate_psum"], 1)
                    e.wait_ge(s["d_ready"], 1)
                    e.matmul(ps[6][:], C["swap"], dd[:].rearrange("p n j -> p (n j)"), start=True,
                             stop=True).then_inc(s["swap2_psum"], 1)
                    e.wait_ge(s["c_ready"], 1)
                    for t in range(NT):
                        mm = e.matmul(ps[7][:, t * P:(t + 1) * P], cc[:, t * P:(t + 1) * P], eg.joined[:], start=True, stop=True)
                    mm.then_inc(s["h_psum"], 1)
                    e.wait_ge(s["xn_ready"], 2 * NT)
                    tensor_turn(e, lambda t: xn[:, t], ps[0], C["ident"], s["xT_psum"])
                    e.wait_ge(s["xT_ready"], 2)
                    for c in range(HC):
                        if c >= 2:
                            e.wait_ge(s["mlp_ready"], c - 1)
                        e.matmul(ps[1 + c % 2][:], W["L1_w_mlp1"][:, c * P:(c + 1) * P], xT[:], start=True,
                                 stop=True).then_inc(s["mlp_psum"], 1)
                    e.wait_ge(s["mlp_ready"], HC)
                    for t in range(NT):
                        o = ps[3][:, t * P:(t + 1) * P]
                        e.matmul(o, C["ones"][0:1, :], W["L1_b_mlp2"][0:1, :], start=True, stop=False)
                        for c in range(HC):
                            mm = e.matmul(o, hid[:, c, t * P:(t + 1) * P], W["L1_w_mlp2"][:, c * P:(c + 1) * P],
                                          start=False, stop=(c == HC - 1))
                    mm.then_inc(s["out_psum"], 1)

                @block.scalar
                def _(e):
                    for r in range(2):
                        ln = W[f"L1_ln{r + 1}"]
                        e.wait_ge(s["xT_psum"], r + 1)
                        e.activation(xT[:], ps[0][:], ACT.Identity, bias=ln[:, 1:2], scale=ln[:, 0:1]).then_inc(s["xT_ready"], 1)
                        if r == 0:
                            e.wait_ge(s["gate_psum"], 1)
                            e.activation(gate[:].rearrange("p t d -> p (t d)"), ps[3][:], ACT.Sigmoid).then_inc(s["gate_ready"], 1)
                    for c in range(HC):
                        e.wait_ge(s["mlp_psum"], c + 1)
                        e.activation(hid[:, c], ps[1 + c % 2][:], ACT.Silu, bias=W["L1_b_mlp1"][:, c:c + 1]).then_inc(s["mlp_ready"], 1)

                @block.vector
                def _(e):
                    vector_take(e, s, x_all, b, xc)
                    e.wait_ge(s["x_copied"], 1)
                    e.sem_inc(s["sum_ready"], NT)
                    vector_moments(e, s, nb, lambda t: xc[:, t])
                    vector_normalize(e, s, nb, lambda t: xc[:, t], lambda t: xn[:, t], signal="xn_ready")
                    e.wait_ge(s["beta_psum"], 1)
                    e.tensor_tensor(z[:], chunked(ps[1][:]), bc(eg.cos[:]), ALU.mult).then_inc(s["turned_in"], 1)
                    e.wait_ge(s["beta_psum"], 2)
                    e.tensor_tensor(z2[:], chunked(ps[2][:]), bc(eg.minus_sin[:]), ALU.mult).then_inc(s["turned_in"], 1)
                    e.wait_ge(s["turned_in"], 2)
                    e.tensor_tensor(z[:], z[:], z2[:], ALU.add).then_inc(s["z_ready"], 1)
                    flat = lambda x: x[:].rearrange("p n j -> p (n j)")
                    e.wait_ge(s["z_ready"], 1)
                    e.tensor_tensor_scan(flat(dd)[:, ::-1], flat(eg.decay), flat(z)[:, ::-1], 0.0, ALU.mult,
                                         ALU.add).then_inc(s["d_ready"], 1)
                    e.wait_ge(s["d_ready"], 1)
                    e.tensor_tensor(z[:], dd[:], bc(eg.cos[:]), ALU.mult).then_inc(s["c_half"], 1)
                    e.wait_ge(s["swap2_psum"], 1)
                    e.tensor_tensor(z2[:], chunked(ps[6][:]), bc(eg.sin[:]), ALU.mult).then_inc(s["c_half"], 1)
                    e.wait_ge(s["c_half"], 2)
                    e.tensor_tensor(cc[:], flat(z), flat(z2), ALU.add).then_inc(s["c_whole"], 1)
                    e.wait_ge(s["c_whole"], 1)
                    first = cc[:].rearrange("p (n j) -> p n j", j=CH)[:, 1:, 0]
                    e.tensor_tensor(first, chunked(ps[1][:])[:, 0:NCH - 1, CH - 1], first, ALU.add).then_inc(s["c_ready"], 1)
                    e.wait_ge(s["h_psum"], 1)
                    e.wait_ge(s["gate_ready"], 1)
                    e.tensor_tensor(gate[:].rearrange("p t d -> p (t d)"), gate[:].rearrange("p t d -> p (t d)"), ps[7][:],
                                    ALU.mult).then_inc(s["gated"], 1)
                    e.wait_ge(s["gated"], 1)
                    e.tensor_tensor(x1[:], gate[:], xc[:], ALU.add).then_inc(s["x1_ready"], 1)
                    e.wait_ge(s["x1_ready"], 1)
                    e.sem_inc(s["sum_ready"], NT)
                    vector_moments(e, s, nb, lambda t: x1[:, t], round_=1)
                    e.wait_ge(s["xT_psum"], 1)
                    vector_normalize(e, s, nb, lambda t: x1[:, t], lambda t: xn[:, t], round_=1, signal="xn_ready")
                    e.wait_ge(s["xn_ready"], 2 * NT)
                    e.tensor_tensor(x1[:], x1[:], xc[:], ALU.add).then_inc(s["x1_ready"], 1)
                    e.wait_ge(s["x1_ready"], 2)
                    e.wait_ge(s["out_psum"], 1)
                    for t in range(NT):
                        e.tensor_tensor(nb.r[:, t], ps[3][:, t * P:(t + 1) * P], x1[:, t], ALU.add).then_inc(s["sum_ready"], 1)
                    vector_moments(e, s, nb, lambda t: nb.r[:, t], round_=2)
                    vector_normalize(e, s, nb, lambda t: nb.r[:, t], lambda t: x_all[:, ds(NT * b + t, 1), :], round_=2)

                @block.gpsimd
                def _(e):
                    for r in range(3):
                        pool_rstd(e, s, nb, half, round_=r)



HID3 = 512
TERNARY_EPS = 1e-6


def ternary_weights_stage(nc, ps, W, C):
    names = ("L1f_W_fc", "L1f_W_proj")
    with ExitStack() as ctx:
        sbl = lambda n, shape: ctx.enter_context(nc.sbuf_tensor(n, shape, F32))
        part = sbl("ter_part", [P, 2, 4])
        gamma, rg = sbl("ter_gamma", [P, 2]), sbl("ter_rgamma", [P, 2])
        above, below = sbl("ter_above", [P, HID3]), sbl("ter_below", [P, HID3])
        with stage(nc, "ter", "vec parts_ready total_psum") as (block, s):
            @block.tensor
            def _(e):
                e.wait_ge(s["parts_ready"], 2)
                e.matmul(ps[0][:, 0:8], C["ones"], part[:].rearrange("p a b -> p (a b)"), start=True,
                         stop=True).then_inc(s["total_psum"], 1)

            @block.vector
            def _(e):
                n = [0]

                def then(i):
                    n[0] += 1
                    i.then_inc(s["vec"], 1)
                    e.wait_ge(s["vec"], n[0])

                for i, w in enumerate(names):
                    e.tensor_reduce(part[:, i], W[w].rearrange("p (a b) -> p a b", a=4), AX_X, ALU.add,
                                    apply_absolute_value=True).then_inc(s["parts_ready"], 1)
                e.wait_ge(s["total_psum"], 1)
                then(e.tensor_reduce(gamma[:], ps[0][:, 0:8].rearrange("p (a b) -> p a b", a=2), AX_X, ALU.add))
                then(e.tensor_scalar(gamma[:], gamma[:], 1.0 / (D * HID3), TERNARY_EPS, ALU.mult, ALU.add))
                then(e.reciprocal(rg[:], gamma[:]))
                for i, w in enumerate(names):
                    then(e.tensor_scalar(above[:], W[w], rg[:, i:i + 1], 0.5, ALU.mult, ALU.is_gt))
                    then(e.tensor_scalar(below[:], W[w], rg[:, i:i + 1], -0.5, ALU.mult, ALU.is_lt))
                    then(e.tensor_tensor(W[w], above[:], below[:], ALU.subtract))


def ternary_stage(nc, ps, x_all, W, C, half, nb, xc, xT):
    HC = HID3 // P
    with ExitStack() as ctx:
        sbl = lambda n, shape: ctx.enter_context(nc.sbuf_tensor(n, shape, F32))
        h = sbl("ter_h", [P, NT, HID3])
        hT = sbl("ter_hT", [P, HC, L])
        names = "h_psum gelu_ready h_normed hT_psum hT_ready" + BATCH_SIGNALS
        with nc.Fori(0, B) as b:
            with stage(nc, "tern", names) as (block, s):
                @block.tensor
                def _(e):
                    e.wait_ge(s["x_copied"], 1)
                    tensor_turn(e, lambda t: xc[:, t], ps[0], C["ident"], s["xT_psum"])
                    e.wait_ge(s["xT_ready"], 1)
                    for t in range(NT):
                        e.matmul(ps[1 + t][:], xT[:, t * P:(t + 1) * P], W["L1f_W_fc"], start=True,
                                 stop=True).then_inc(s["h_psum"], 1)
                    e.wait_ge(s["h_normed"], NT)
                    for c in range(HC):
                        if c >= 2:
                            e.wait_ge(s["hT_ready"], c - 1)
                        tensor_turn(e, lambda t: h[:, t, c * P:(c + 1) * P], ps[5 + c % 2], C["ident"], s["hT_psum"])
                    e.wait_ge(s["hT_ready"], HC)
                    for t in range(NT):
                        for c in range(HC):
                            mm = e.matmul(ps[7][:, t * P:(t + 1) * P], hT[:, c, t * P:(t + 1) * P],
                                          W["L1f_W_proj"][:, c * P:(c + 1) * P], start=(c == 0), stop=(c == HC - 1))
                    mm.then_inc(s["out_psum"], 1)

                @block.scalar
                def _(e):
                    e.wait_ge(s["xT_psum"], 1)
                    e.activation(xT[:], ps[0][:], ACT.Copy).then_inc(s["xT_ready"], 1)
                    for t in range(NT):
                        e.wait_ge(s["h_psum"], t + 1)
                        e.activation(h[:, t], ps[1 + t][:], ACT.Gelu).then_inc(s["sum_ready"], 1)
                    for c in range(HC):
                        e.wait_ge(s["hT_psum"], c + 1)
                        e.activation(hT[:, c], ps[5 + c % 2][:], ACT.Identity, bias=W["L1f_ln_b"][:, c:c + 1],
                                     scale=W["L1f_ln_w"][:, c:c + 1]).then_inc(s["hT_ready"], 1)

                @block.vector
                def _(e):
                    vector_take(e, s, x_all, b, xc)
                    vector_moments(e, s, nb, lambda t: h[:, t])
                    vector_normalize(e, s, nb, lambda t: h[:, t], lambda t: h[:, t], signal="h_normed")
                    e.wait_ge(s["out_psum"], 1)
                    for t in range(NT):
                        e.tensor_tensor(nb.r[:, t], ps[7][:, t * P:(t + 1) * P], xc[:, t], ALU.add).then_inc(s["sum_ready"], 1)
                    e.wait_ge(s["h_normed"], NT)
                    vector_moments(e, s, nb, lambda t: nb.r[:, t], round_=1)
                    vector_normalize(e, s, nb, lambda t: nb.r[:, t], lambda t: x_all[:, ds(NT * b + t, 1), :], round_=1)

                @block.gpsimd
                def _(e):
                    pool_rstd(e, s, nb, half)
                    pool_rstd(e, s, nb, half, round_=1)



H4, DK4 = 16, 64
PAIRS4 = H4 // 2
SCALE4 = DK4 ** -0.5


def causal_stage(nc, ps, x_all, W, C, half, nb, xc, xT, ident_bf, mask_bf):
    UNITS = [(qt, h) for qt in range(NT) for h in range(H4)]
    NU = len(UNITS)
    with ExitStack() as ctx:
        sbl = lambda n, shape: ctx.enter_context(nc.sbuf_tensor(n, shape, F32))
        qT, kT = sbl("att_qT", [P, PAIRS4, L]), sbl("att_kT", [P, PAIRS4, L])
        v = sbl("att_v", [P, NT, H4 * DK4])
        straight, turned = sbl("att_straight", [P, 2, L]), sbl("att_turned", [P, 2, L])
        mx, nmx, sm, rs = (sbl(f"att_{k}", [P, NT * H4]) for k in ("max", "minus_max", "sum", "rsum"))
        prob, probT = sbl("att_prob", [P, 3, L]), sbl("att_probT", [P, 3, NT, P])
        o, oT = sbl("att_o", [P, NT, H4 * DK4]), sbl("att_oT", [P, PAIRS4, L])
        names = ("proj_psum straight_ready turned_ready rope_ready v_psum v_ready s_psum max_ready bias_ready prob_ready "
                 "probT_psum probT_ready pv_psum rsum_ready o_ready oT_psum oT_ready" + BATCH_SIGNALS)
        with nc.Fori(0, B) as b:
            with stage(nc, "att", names) as (block, s):
                S = lambda u: ps[1 + u % 4]
                T = lambda u: ps[5 + u % 2]
                O = lambda h: (ps[7] if h < H4 // 2 else ps[0])[:, (h % 8) * DK4:(h % 8 + 1) * DK4]

                @block.tensor
                def _(e):
                    e.wait_ge(s["x_copied"], 1)
                    tensor_turn(e, lambda t: xc[:, t], ps[0], C["ident"], s["xT_psum"])
                    e.wait_ge(s["xT_ready"], 1)
                    for c in range(2 * PAIRS4):
                        w = "q" if c < PAIRS4 else "k"
                        cc = slice((c % PAIRS4) * P, (c % PAIRS4 + 1) * P)
                        if c >= 2:
                            e.wait_ge(s["straight_ready"], c - 1)
                            e.wait_ge(s["turned_ready"], c - 1)
                        e.matmul(ps[1 + 2 * (c % 2)][:], W[f"L2_w{w}"][:, cc], xT[:], start=True, stop=True).then_inc(s["proj_psum"], 1)
                        e.matmul(ps[2 + 2 * (c % 2)][:], W[f"L2_w{w}_turned"][:, cc], xT[:], start=True, stop=True).then_inc(s["proj_psum"], 1)
                    for i in range(2 * NT):
                        t, hf = divmod(i, 2)
                        if i >= 2:
                            e.wait_ge(s["v_ready"], i - 1)
                        cc = slice(512 * hf, 512 * (hf + 1))
                        e.matmul(ps[5 + i % 2][:], C["ones"][0:1, :], W["L2_bv"][0:1, cc], start=True, stop=False)
                        e.matmul(ps[5 + i % 2][:], xT[:, t * P:(t + 1) * P], W["L2_wv"][:, cc], start=False,
                                 stop=True).then_inc(s["v_psum"], 1)
                    e.wait_ge(s["rope_ready"], 2 * PAIRS4)
                    e.wait_ge(s["v_ready"], 2 * NT)
                    for u in range(NU + 3):
                        if u < NU:
                            qt, h = UNITS[u]
                            if u >= 4:
                                e.wait_ge(s["prob_ready"], u - 3)
                            r = slice(DK4 * (h % 2), DK4 * (h % 2 + 1))
                            e.matmul(S(u)[:, 0:(qt + 1) * P], qT[r, h // 2, qt * P:(qt + 1) * P], kT[r, h // 2, 0:(qt + 1) * P],
                                     start=True, stop=False, skip_group_check=True)
                            e.matmul(S(u)[:, qt * P:(qt + 1) * P], ident_bf[:], mask_bf[:], start=False, stop=True,
                                     skip_group_check=True).then_inc(s["s_psum"], 1)
                        if 2 <= u < NU + 2:
                            qt, h = UNITS[u - 2]
                            e.wait_ge(s["prob_ready"], u - 1)
                            if u >= 4:
                                e.wait_ge(s["probT_ready"], u - 3)
                            for k in range(qt + 1):
                                mm = e.transpose(T(u - 2)[:, k * P:(k + 1) * P], prob[:, (u - 2) % 3, k * P:(k + 1) * P], C["ident"])
                            mm.then_inc(s["probT_psum"], 1)
                        if u >= 3:
                            qt, h = UNITS[u - 3]
                            e.wait_ge(s["probT_ready"], u - 2)
                            if h % (H4 // 2) == 0 and qt >= 1:
                                e.wait_ge(s["o_ready"], 2 * (qt - 1) + 1 + h // (H4 // 2))
                            for k in range(qt + 1):
                                mm = e.matmul(O(h), probT[:, (u - 3) % 3, k], v[:, k, h * DK4:(h + 1) * DK4],
                                              start=(k == 0), stop=(k == qt))
                            mm.then_inc(s["pv_psum"], 1)
                    e.wait_ge(s["o_ready"], 2 * NT)
                    for c in range(PAIRS4):
                        if c >= 2:
                            e.wait_ge(s["oT_ready"], c - 1)
                        tensor_turn(e, lambda t: o[:, t, c * P:(c + 1) * P], ps[5 + c % 2], C["ident"], s["oT_psum"])
                    e.wait_ge(s["oT_ready"], PAIRS4)
                    for t in range(NT):
                        y = ps[1][:, t * P:(t + 1) * P]
                        e.matmul(y, C["ones"][0:1, :], W["L2_bo"][0:1, :], start=True, stop=False)
                        for c in range(PAIRS4):
                            mm = e.matmul(y, oT[:, c, t * P:(t + 1) * P], W["L2_wo"][:, c * P:(c + 1) * P], start=False,
                                          stop=(c == PAIRS4 - 1))
                    mm.then_inc(s["out_psum"], 1)

                @block.scalar
                def _(e):
                    e.wait_ge(s["xT_psum"], 1)
                    e.activation(xT[:], ps[0][:], ACT.Copy).then_inc(s["xT_ready"], 1)
                    for i in range(2 * NT):
                        t, hf = divmod(i, 2)
                        e.wait_ge(s["v_psum"], i + 1)
                        e.activation(v[:, t, 512 * hf:512 * (hf + 1)], ps[5 + i % 2][:], ACT.Copy).then_inc(s["v_ready"], 1)
                    for u, (qt, h) in enumerate(UNITS):
                        e.wait_ge(s["bias_ready"], u + 1)
                        if u >= 3:
                            e.wait_ge(s["probT_psum"], u - 2)
                        e.activation(prob[:, u % 3, 0:(qt + 1) * P], S(u)[:, 0:(qt + 1) * P], ACT.Exp, bias=nmx[:, u:u + 1],
                                     scale=SCALE4, accum_out=sm[:, u:u + 1]).then_inc(s["prob_ready"], 1)
                    for c in range(PAIRS4):
                        e.wait_ge(s["oT_psum"], c + 1)
                        e.activation(oT[:, c], ps[5 + c % 2][:], ACT.Copy).then_inc(s["oT_ready"], 1)

                @block.vector
                def _(e):
                    vector_take(e, s, x_all, b, xc)
                    for c in range(2 * PAIRS4):
                        w = "q" if c < PAIRS4 else "k"
                        bias, bias_turned = W[f"L2_b{w}"], W[f"L2_b{w}_turned"]
                        i = c % PAIRS4
                        if c >= 2:
                            e.wait_ge(s["rope_ready"], c - 1)
                        e.wait_ge(s["proj_psum"], 2 * c + 1)
                        e.scalar_tensor_tensor(straight[:, c % 2], ps[1 + 2 * (c % 2)][:], bias[:, i:i + 1], C["rope4_cos"],
                                               ALU.add, ALU.mult).then_inc(s["straight_ready"], 1)
                        e.wait_ge(s["proj_psum"], 2 * c + 2)
                        e.scalar_tensor_tensor(turned[:, c % 2], ps[2 + 2 * (c % 2)][:], bias_turned[:, i:i + 1], C["rope4_sin"],
                                               ALU.add, ALU.mult).then_inc(s["turned_ready"], 1)
                    for u in range(NU + 3):
                        if u < NU:
                            qt, h = UNITS[u]
                            e.wait_ge(s["s_psum"], u + 1)
                            e.tensor_reduce(mx[:, u:u + 1], S(u)[:, 0:(qt + 1) * P], AX_X, ALU.max).then_inc(s["max_ready"], 1)
                            e.wait_ge(s["max_ready"], u + 1)
                            e.tensor_scalar(nmx[:, u:u + 1], mx[:, u:u + 1], -SCALE4, None, ALU.mult).then_inc(s["bias_ready"], 1)
                        if 2 <= u < NU + 2:
                            qt, h = UNITS[u - 2]
                            e.wait_ge(s["probT_psum"], u - 1)
                            if u >= 5:
                                e.wait_ge(s["pv_psum"], u - 4)
                            e.tensor_copy(probT[:, (u - 2) % 3, 0:qt + 1].rearrange("p k q -> p (k q)"),
                                          T(u - 2)[:, 0:(qt + 1) * P]).then_inc(s["probT_ready"], 1)
                        if u >= 3 and u % (H4 // 2) == 2:
                            j = (u - 2) // (H4 // 2) - 1
                            qt, hf = divmod(j, 2)
                            cols = slice(8 * j, 8 * j + 8)
                            e.wait_ge(s["prob_ready"], 8 * (j + 1))
                            e.reciprocal(rs[:, cols], sm[:, cols]).then_inc(s["rsum_ready"], 1)
                            e.wait_ge(s["rsum_ready"], j + 1)
                            e.wait_ge(s["pv_psum"], 8 * (j + 1))
                            e.tensor_tensor(o[:, qt, 512 * hf:512 * (hf + 1)].rearrange("p (h d) -> p h d", d=DK4),
                                            (ps[0] if hf else ps[7])[:].rearrange("p (h d) -> p h d", d=DK4),
                                            rs[:, cols].unsqueeze(2).to_broadcast([P, 8, DK4]), ALU.mult).then_inc(s["o_ready"], 1)
                    vector_finish(e, s, nb, lambda t: ps[1][:, t * P:(t + 1) * P], xc, x_all, b)

                @block.gpsimd
                def _(e):
                    for c in range(2 * PAIRS4):
                        out = (qT if c < PAIRS4 else kT)[:, c % PAIRS4]
                        e.wait_ge(s["straight_ready"], c + 1)
                        e.wait_ge(s["turned_ready"], c + 1)
                        e.tensor_tensor(out, straight[:, c % 2], turned[:, c % 2], ALU.add).then_inc(s["rope_ready"], 1)
                    pool_rstd(e, s, nb, half)



HID5 = 512


def relu_stage(nc, ps, x_all, W, C, half, nb, xc, xT):
    HC = HID5 // P
    with ExitStack() as ctx:
        hT = ctx.enter_context(nc.sbuf_tensor("mlp_hT", [P, HC, L], F32))
        names = "h_psum h_ready" + BATCH_SIGNALS
        with nc.Fori(0, B) as b:
            with stage(nc, "mlp", names) as (block, s):
                @block.tensor
                def _(e):
                    e.wait_ge(s["x_copied"], 1)
                    tensor_turn(e, lambda t: xc[:, t], ps[0], C["ident"], s["xT_psum"])
                    e.wait_ge(s["xT_ready"], 1)
                    for c in range(HC):
                        e.matmul(ps[1 + c][:], W["L2f_W1"][:, c * P:(c + 1) * P], xT[:], start=True,
                                 stop=True).then_inc(s["h_psum"], 1)
                    e.wait_ge(s["h_ready"], HC)
                    for t in range(NT):
                        y = ps[7][:, t * P:(t + 1) * P]
                        e.matmul(y, C["ones"][0:1, :], W["L2f_b2"][0:1, :], start=True, stop=False)
                        for c in range(HC):
                            mm = e.matmul(y, hT[:, c, t * P:(t + 1) * P], W["L2f_W2"][:, c * P:(c + 1) * P], start=False,
                                          stop=(c == HC - 1))
                    mm.then_inc(s["out_psum"], 1)

                @block.scalar
                def _(e):
                    e.wait_ge(s["xT_psum"], 1)
                    e.activation(xT[:], ps[0][:], ACT.Copy).then_inc(s["xT_ready"], 1)
                    for c in range(HC):
                        e.wait_ge(s["h_psum"], c + 1)
                        e.activation(hT[:, c], ps[1 + c][:], ACT.Relu, bias=W["L2f_b1"][:, c:c + 1]).then_inc(s["h_ready"], 1)

                @block.vector
                def _(e):
                    vector_take(e, s, x_all, b, xc)
                    vector_finish(e, s, nb, lambda t: ps[7][:, t * P:(t + 1) * P], xc, x_all, b)

                @block.gpsimd
                def _(e):
                    pool_rstd(e, s, nb, half)



H6, DH6, M6 = 16, 8, 16
DN6 = DH6 ** -0.25
RATIO6 = M6 ** -0.5
EPS6 = 1e-4
FEATS = H6 * M6


def features_stage(nc, ps, x_all, W, C, half, nb, xc, xT):
    HF = FEATS // P
    with ExitStack() as ctx:
        sbl = lambda n, shape: ctx.enter_context(nc.sbuf_tensor(n, shape, F32))
        t_, sq = sbl("rf_t", [P, 2, L]), sbl("rf_sq", [P, 2, L])
        v1 = sbl("rf_v", [P, NT, D + 1])
        dg = sbl("rf_diag", [P, 2, NT * H6])
        mx = sbl("rf_max", [P, 2, NT * H6])
        kmx, kall, kdiag, kmax = sbl("rf_kmax_tok", [P, H6]), sbl("rf_kmax_h", [H6, 1]), sbl("rf_kmax_d", [H6, H6]), sbl("rf_kmax", [P, NT, H6])
        f = sbl("rf_f", [P, 2, NT, FEATS])
        fT = sbl("rf_fT", [P, HF, L])
        bd = sbl("rf_context", [P, HF, D + H6])
        den = sbl("rf_den", [P, NT, H6])
        o, oT, hT = sbl("rf_o", [P, NT, D]), sbl("rf_oT", [P, L]), sbl("rf_hT", [P, L])
        names = ("proj_psum t_ready sq_ready v_psum v_ready one_ready td_psum diag_psum diag_ready max_ready less_diag "
                 "less_max exp_ready f_ready ktok_ready kT_psum kall_ready kdiag_ready kmax_psum kmax_ready context_psum "
                 "context_ready fT_psum fT_ready ratio_psum den_ready o_ready oT_psum oT_ready h_psum hT_ready"
                 + BATCH_SIGNALS)
        heads = lambda ap: ap.rearrange("p (g m) -> p g m", m=M6)
        wide = [P, 2 * H6, M6]
        WK = D + H6
        with nc.Fori(0, B) as b:
            with stage(nc, "rf", names) as (block, s):
                td = lambda w, j: ps[4 + 2 * w + j]

                @block.tensor
                def _(e):
                    e.wait_ge(s["x_copied"], 1)
                    tensor_turn(e, lambda t: xc[:, t], ps[0], C["ident"], s["xT_psum"])
                    e.wait_ge(s["xT_ready"], 1)
                    e.matmul(ps[1][:], W["L3_Wq"], xT[:], start=True, stop=True).then_inc(s["proj_psum"], 1)
                    e.matmul(ps[2][:], W["L3_Wk"], xT[:], start=True, stop=True).then_inc(s["proj_psum"], 1)
                    for t in range(NT):
                        y = ps[3][:, t * P:(t + 1) * P]
                        e.matmul(y, C["ones"][0:1, :], W["L3_bv"][0:1, :], start=True, stop=False)
                        mm = e.matmul(y, xT[:, t * P:(t + 1) * P], W["L3_Wv"], start=False, stop=True)
                    mm.then_inc(s["v_psum"], 1)
                    for w in (1, 0):
                        e.wait_ge(s["t_ready"], 2 if w == 0 else 1)
                        for t in range(NT):
                            mm = e.matmul(td(w, t // 2)[:, (t % 2) * FEATS:(t % 2 + 1) * FEATS], t_[:, w, t * P:(t + 1) * P],
                                          W["L3_proj"], start=True, stop=True)
                        mm.then_inc(s["td_psum"], 1)
                        e.wait_ge(s["sq_ready"], 2 if w == 0 else 1)
                        for t in range(NT):
                            mm = e.matmul(ps[0][:, (w * NT + t) * H6:(w * NT + t + 1) * H6], sq[:, w, t * P:(t + 1) * P],
                                          C["head_of_feature"], start=True, stop=True)
                        mm.then_inc(s["diag_psum"], 1)
                    e.wait_ge(s["ktok_ready"], 1)
                    e.transpose(ps[1][0:H6, 0:P], kmx[:], C["ident"]).then_inc(s["kT_psum"], 1)
                    e.wait_ge(s["kdiag_ready"], 1)
                    e.matmul(ps[1][:, P:P + H6], C["ones"][0:H6, :], kdiag[:], start=True, stop=True).then_inc(s["kmax_psum"], 1)
                    e.wait_ge(s["v_ready"], 1)
                    e.wait_ge(s["one_ready"], 1)
                    e.wait_ge(s["f_ready"], 4)
                    for m in range(HF):
                        for t in range(NT):
                            mm = e.matmul(ps[2 + m][:, 0:D + 1], f[:, 1, t, m * P:(m + 1) * P], v1[:, t], start=(t == 0),
                                          stop=(t == NT - 1))
                        mm.then_inc(s["context_psum"], 1)
                    for m in range(HF):
                        tensor_turn(e, lambda t: f[:, 0, t, m * P:(m + 1) * P], ps[4 + m], C["ident"], s["fT_psum"])
                    e.wait_ge(s["fT_ready"], HF)
                    e.wait_ge(s["context_ready"], 2 * HF)
                    for t in range(NT):
                        for m in range(HF):
                            mm = e.matmul(ps[6 + t // 2][:, (t % 2) * WK:(t % 2 + 1) * WK], fT[:, m, t * P:(t + 1) * P], bd[:, m],
                                          start=(m == 0), stop=(m == HF - 1))
                    mm.then_inc(s["ratio_psum"], 1)
                    e.wait_ge(s["o_ready"], 2)
                    tensor_turn(e, lambda t: o[:, t], ps[0], C["ident"], s["oT_psum"])
                    e.wait_ge(s["oT_ready"], 1)
                    e.matmul(ps[1][:], W["L3_Wo"], oT[:], start=True, stop=True).then_inc(s["h_psum"], 1)
                    e.wait_ge(s["hT_ready"], 1)
                    for t in range(NT):
                        y = ps[2][:, t * P:(t + 1) * P]
                        e.matmul(y, C["ones"][0:1, :], W["L3_bfc"][0:1, :], start=True, stop=False)
                        mm = e.matmul(y, hT[:, t * P:(t + 1) * P], W["L3_Wfc"], start=False, stop=True)
                    mm.then_inc(s["out_psum"], 1)

                @block.scalar
                def _(e):
                    e.wait_ge(s["xT_psum"], 1)
                    e.activation(xT[:], ps[0][:], ACT.Copy).then_inc(s["xT_ready"], 1)
                    for n, w in enumerate((1, 0)):
                        e.wait_ge(s["t_ready"], n + 1)
                        e.activation(sq[:, w], t_[:, w], ACT.Square).then_inc(s["sq_ready"], 1)
                    e.wait_ge(s["v_psum"], 1)
                    e.activation(v1[:, :, 0:D], ps[3][:].rearrange("p (t d) -> p t d", d=D), ACT.Copy).then_inc(s["v_ready"], 1)
                    for n in range(4):
                        w, j = (0, n) if n < 2 else (1, n - 2)
                        e.wait_ge(s["less_max"], n + 1)
                        x = f[:, w, 2 * j:2 * j + 2]
                        e.activation(x, x, ACT.Exp).then_inc(s["exp_ready"], 1)
                    for m in range(HF):
                        e.wait_ge(s["fT_psum"], m + 1)
                        e.activation(fT[:, m], ps[4 + m][:], ACT.Copy).then_inc(s["fT_ready"], 1)
                    e.wait_ge(s["oT_psum"], 1)
                    e.activation(oT[:], ps[0][:], ACT.Copy).then_inc(s["oT_ready"], 1)
                    e.wait_ge(s["h_psum"], 1)
                    e.activation(hT[:], ps[1][:], ACT.Identity, bias=W["L3_bo"]).then_inc(s["hT_ready"], 1)

                @block.vector
                def _(e):
                    vector_take(e, s, x_all, b, xc)
                    e.memset(v1[:, :, D:], 1.0).then_inc(s["one_ready"], 1)
                    e.wait_ge(s["proj_psum"], 2)
                    for w, name in ((1, "k"), (0, "q")):
                        e.tensor_scalar(t_[:, w], ps[1 + w][:], W[f"L3_b{name}"], DN6, ALU.add, ALU.mult).then_inc(s["t_ready"], 1)
                    for n, w in enumerate((1, 0)):
                        e.wait_ge(s["diag_psum"], 2)
                        e.tensor_scalar(dg[:, w], ps[0][:, w * NT * H6:(w + 1) * NT * H6], 0.5, None,
                                        ALU.mult).then_inc(s["diag_ready"], 1)
                        for j in range(2):
                            e.tensor_reduce(mx[:, w, 2 * H6 * j:2 * H6 * (j + 1)], heads(td(w, j)[:]), AX_X,
                                            ALU.max).then_inc(s["max_ready"], 1)
                        if w == 1:
                            e.wait_ge(s["max_ready"], 2)
                            e.tensor_reduce(kmx[:], mx[:, 1].rearrange("p (t h) -> p h t", h=H6), AX_X,
                                            ALU.max).then_inc(s["ktok_ready"], 1)
                            e.wait_ge(s["kT_psum"], 1)
                            e.tensor_reduce(kall[:], ps[1][0:H6, 0:P], AX_X, ALU.max).then_inc(s["kall_ready"], 1)
                            e.wait_ge(s["kall_ready"], 1)
                            e.tensor_scalar(kdiag[:], C["ident"][0:H6, 0:H6], kall[:], None, ALU.mult).then_inc(s["kdiag_ready"], 1)
                            e.wait_ge(s["kmax_psum"], 1)
                            e.tensor_copy(kmax[:], ps[1][:, P:P + H6].unsqueeze(1).to_broadcast([P, NT, H6])).then_inc(s["kmax_ready"], 1)
                    e.wait_ge(s["diag_ready"], 2)
                    e.wait_ge(s["max_ready"], 4)
                    e.wait_ge(s["kmax_ready"], 1)
                    for n in range(4):
                        w, j = (0, n) if n < 2 else (1, n - 2)
                        x = f[:, w, 2 * j:2 * j + 2].rearrange("p t (h m) -> p (t h) m", m=M6)
                        cols = slice(2 * H6 * j, 2 * H6 * (j + 1))
                        most = mx[:, 0, cols] if w == 0 else kmax[:].rearrange("p t h -> p (t h)")[:, cols]
                        e.tensor_tensor(x, heads(td(w, j)[:]), dg[:, w, cols].unsqueeze(2).to_broadcast(wide),
                                        ALU.subtract).then_inc(s["less_diag"], 1)
                        e.wait_ge(s["less_diag"], n + 1)
                        e.tensor_tensor(x, x, most.unsqueeze(2).to_broadcast(wide), ALU.subtract).then_inc(s["less_max"], 1)
                    for n in range(4):
                        w, j = (0, n) if n < 2 else (1, n - 2)
                        x = f[:, w, 2 * j:2 * j + 2]
                        e.wait_ge(s["exp_ready"], n + 1)
                        e.tensor_scalar(x, x, EPS6, RATIO6, ALU.add, ALU.mult).then_inc(s["f_ready"], 1)
                    for m in range(HF):
                        e.wait_ge(s["context_psum"], m + 1)
                        own = C["own_columns"][:, m * WK:(m + 1) * WK]
                        e.tensor_tensor(bd[:, m, 0:D], ps[2 + m][:, 0:D], own[:, 0:D], ALU.mult).then_inc(s["context_ready"], 1)
                        e.tensor_scalar(bd[:, m, D:], own[:, D:], ps[2 + m][:, D:D + 1], None, ALU.mult).then_inc(s["context_ready"], 1)
                    e.wait_ge(s["ratio_psum"], 1)
                    for j in range(2):
                        r = ps[6 + j][:, 0:2 * WK].rearrange("p (t k) -> p t k", k=WK)
                        e.reciprocal(den[:, 2 * j:2 * j + 2], r[:, :, D:]).then_inc(s["den_ready"], 1)
                    for j in range(2):
                        r = ps[6 + j][:, 0:2 * WK].rearrange("p (t k) -> p t k", k=WK)
                        e.wait_ge(s["den_ready"], j + 1)
                        for t in range(2):
                            i = e.tensor_tensor(o[:, 2 * j + t].rearrange("p (h d) -> p h d", d=DH6),
                                                r[:, t, 0:D].rearrange("p (h d) -> p h d", d=DH6),
                                                den[:, 2 * j + t].unsqueeze(2).to_broadcast([P, H6, DH6]), ALU.mult)
                        i.then_inc(s["o_ready"], 1)
                    e.wait_ge(s["out_psum"], 1)
                    for t in range(NT):
                        e.scalar_tensor_tensor(nb.r[:, t], ps[2][:, t * P:(t + 1) * P], 0.0, xc[:, t], ALU.max,
                                               ALU.add).then_inc(s["sum_ready"], 1)
                    vector_moments(e, s, nb, lambda t: nb.r[:, t])
                    vector_normalize(e, s, nb, lambda t: nb.r[:, t], lambda t: x_all[:, ds(NT * b + t, 1), :])

                @block.gpsimd
                def _(e):
                    pool_rstd(e, s, nb, half)



DEPTH = 6
H7, DK7 = 16, 64
INNER7 = H7 * DK7
PAIRS7 = H7 // 2
WIN = 32
SPAN = WIN + P
HALF = D // 2
QK_SCALE = 8.0
GROUP = 4
NG = H7 // GROUP
HID7 = 384
LAYER_COLUMNS = (("qkv", 3 * INNER7), ("wo", PAIRS7 * D), ("w1", 2 * HID7), ("w2", HID7), ("b1", 2 * HID7 // P),
                 ("ln", 2), ("b2", D), ("q_scale", DK7), ("q_scale_rolled", DK7), ("k_scale", DK7), ("k_scale_rolled", DK7))


class LayerBuffers:
    def __init__(self, nc, ctx):
        sbl = lambda n, shape, dtype=F32: ctx.enter_context(nc.sbuf_tensor(n, shape, dtype))
        width = sum(w for _, w in LAYER_COLUMNS)
        self.weights = [sbl(f"lay_weights{i}", [P, width]) for i in range(2)]
        self.at, o = {}, 0
        for n, w in LAYER_COLUMNS:
            self.at[n] = slice(o, o + w)
            o += w
        self.table = sbl("lay_table", [P, 4, NT, DK7])
        self.raw = sbl("lay_raw", [P, 2, 2 * INNER7])
        self.sq = sbl("lay_sq", [P, 2 * INNER7])
        self.part = sbl("lay_turned", [P, 2 * INNER7])
        self.qk = sbl("lay_qk", [P, NT, 2 * INNER7])
        self.v = sbl("lay_v", [P, NT, INNER7])
        self.vb = sbl("lay_v_before", [P, 2, NG, GROUP * DK7])
        self.qT = sbl("lay_qT", [P, PAIRS7, L])
        self.kT = sbl("lay_kT", [P, PAIRS7, WIN + L])
        self.ss = sbl("lay_squares", [P, NT, 2 * H7])
        self.norm = sbl("lay_norm", [P, NT, 2 * H7])
        self.rn = sbl("lay_rnorm", [P, NT, 2 * H7])
        self.q8 = sbl("lay_q8", [P, NT, H7])
        self.mx = sbl("lay_max", [P, NT * NG, GROUP])
        self.nmx = sbl("lay_minus_max", [P, NT * NG, GROUP])
        self.sm = sbl("lay_sum", [P, NT * NG, GROUP])
        self.rs = sbl("lay_rsum", [P, NT * NG, GROUP])
        raw = self.raw[:].rearrange("p a b -> p (a b)")
        o = 2 * GROUP * SPAN
        self.prob = raw[:, 0:o].rearrange("p (a j k) -> p a j k", a=2, j=GROUP)
        self.probT = raw[:, o:o + 2 * GROUP * P].rearrange("p (a j q) -> p a j q", a=2, j=GROUP)
        self.probTb = raw[:, o + 2 * GROUP * P:o + 2 * GROUP * P + 2 * P].rearrange("p (a q) -> p a q", a=2)
        o += 2 * GROUP * P + 2 * P
        self.probb = raw[:, o:o + 2 * P].rearrange("p (a q) -> p a q", a=2)
        self.mask = sbl("lay_mask", [P, 2, SPAN], BF16)
        self.ident = sbl("lay_ident", [P, P], BF16)

    def w(self, parity, name):
        return self.weights[parity][:, self.at[name]]


def layers_start_stage(nc, lb, late, late_dram, layers_dram, arrived):
    with stage(nc, "lays", "late_loaded zeroed masks") as (block, s):
        @block.sync
        def _(e):
            e.dma_start(late.all[:], late_dram).then_inc(s["late_loaded"], 16)
            e.dma_start(lb.weights[0][:], layers_dram[0]).then_inc(arrived, 16)

        @block.vector
        def _(e):
            e.memset(lb.kT[:, :, 0:WIN], 0.0).then_inc(s["zeroed"], 1)
            e.memset(lb.vb[:], 0.0).then_inc(s["zeroed"], 1)
            e.wait_ge(s["late_loaded"], 16)
            e.tensor_copy(lb.mask[:], late["band_masks"].rearrange("p (a b) -> p a b", a=2)).then_inc(s["masks"], 1)
            e.tensor_copy(lb.ident[:], late["ident_late"]).then_inc(s["masks"], 1)


def layer_prepare_stage(nc, lb, late, layers_dram, arrived, parity, following):
    with stage(nc, f"layp{parity}", "weights_ready table_ready") as (block, s):
        @block.sync
        def _(e):
            e.wait_ge(arrived, 16)
            e.sem_inc(s["weights_ready"], 1)
            e.sem_clear(arrived)
            e.dma_start(lb.weights[1 - parity][:], layers_dram[ds(following, 1)].rearrange("a p w -> (a p) w")).then_inc(arrived, 16)

        @block.vector
        def _(e):
            e.wait_ge(s["weights_ready"], 1)
            for i, n in enumerate(("q_scale", "q_scale_rolled", "k_scale", "k_scale_rolled")):
                e.tensor_tensor(lb.table[:, i], late["rope7"][:, i * NT * DK7:(i + 1) * NT * DK7].rearrange("p (t d) -> p t d", d=DK7),
                                lb.w(parity, n).unsqueeze(1).to_broadcast([P, NT, DK7]), ALU.mult).then_inc(s["table_ready"], 1)


def local_attention_stage(nc, ps, x_all, C, xc, xT, lb, parity):
    NU = NT * NG
    names = ("x_copied first_zero xT_psum xT_ready qk_psum v_psum raw_ready v_ready sq_ready squares_ready straight_ready "
             "turned_ready rotated norm_ready norm_floored rnorm_ready q8_ready k_normed qkT_psum qkT_ready v_before "
             "s_psum max_ready bias_ready prob_ready before_ready probT_psum probT_ready probTb_ready pv_psum rsum_ready o_ready "
             "oT_psum oT_ready out_psum")
    heads = lambda ap: ap.rearrange("p (h d) -> p h d", d=DK7)
    W = lambda n: lb.w(parity, n)
    with nc.Fori(0, B) as b:
        with stage(nc, f"loc{parity}", names) as (block, s):
            S = lambda u, odd: ps[2 + 2 * (u % 2) + odd]

            @block.tensor
            def _(e):
                e.wait_ge(s["x_copied"], 1)
                tensor_turn(e, lambda t: xc[:, t], ps[0], C["ident"], s["xT_psum"])
                e.wait_ge(s["xT_ready"], 2)
                e.wait_ge(s["first_zero"], 1)
                for t in range(NT):
                    for c in range(6):
                        if t >= 1:
                            e.wait_ge(s["raw_ready"] if c < 4 else s["v_ready"], 4 * (t - 1) + c + 1 if c < 4 else 2 * (t - 1) + c - 3)
                        e.matmul(ps[1 + c][:], xT[:, t * P:(t + 1) * P], W("qkv")[:, 512 * c:512 * (c + 1)], start=True,
                                 stop=True).then_inc(s["qk_psum"] if c < 4 else s["v_psum"], 1)

                def turn_tile(t):
                    for i in range(4):
                        j = 4 * t + i
                        if i < 2:
                            e.wait_ge(s["rotated"], 2 * t + 2)
                        else:
                            e.wait_ge(s["k_normed"], t + 1)
                        if j >= 1:
                            e.wait_ge(s["qkT_ready"], j)
                        for c in range(4):
                            mm = e.transpose(ps[1][:, c * P:(c + 1) * P], lb.qk[:, t, i * 512 + c * P:i * 512 + (c + 1) * P], C["ident"])
                        mm.then_inc(s["qkT_psum"], 1)
                    e.wait_ge(s["qkT_ready"], 4 * (t + 1))

                def scores(u):
                    t, g = divmod(u, NG)
                    if u >= 2:
                        e.wait_ge(s["prob_ready"], u - 1)
                    for j in range(2):
                        for odd in range(2):
                            r = slice(DK7 * odd, DK7 * (odd + 1))
                            e.matmul(S(u, odd)[:, j * SPAN:(j + 1) * SPAN], lb.qT[r, 2 * g + j, t * P:(t + 1) * P],
                                     lb.kT[r, 2 * g + j, t * P:t * P + SPAN], start=(j == 0), stop=False, skip_group_check=True)
                    for j in range(2):
                        for odd in range(2):
                            mm = e.matmul(S(u, odd)[:, j * SPAN:(j + 1) * SPAN], lb.ident[:], lb.mask[:, min(t, 1)], start=False,
                                          stop=(j == 1), skip_group_check=True)
                    mm.then_inc(s["s_psum"], 1)

                def turn_probabilities(u):
                    e.wait_ge(s["prob_ready"], u + 1)
                    if u >= 1:
                        e.wait_ge(s["probT_ready"], u)
                        e.wait_ge(s["probTb_ready"], u)
                    for j in range(GROUP):
                        e.transpose(ps[6][:, j * P:(j + 1) * P], lb.prob[:, u % 2, j, WIN:], C["ident"])
                    e.wait_ge(s["before_ready"], u + 1)
                    e.transpose(ps[7][:, 0:P], lb.probb[:, u % 2], C["ident"]).then_inc(s["probT_psum"], 1)

                def values(u):
                    t, g = divmod(u, NG)
                    e.wait_ge(s["probT_ready"], u + 1)
                    e.wait_ge(s["probTb_ready"], u + 1)
                    if u >= 1:
                        e.wait_ge(s["o_ready"], u)
                    if t >= 1:
                        e.wait_ge(s["v_before"], GROUP * t)
                        e.matmul(ps[0][:, 0:GROUP * DK7], lb.probTb[:, u % 2], lb.vb[:, (t - 1) % 2, g], start=True, stop=False,
                                 skip_group_check=True)
                    for j in range(GROUP):
                        h = GROUP * g + j
                        mm = e.matmul(ps[0][:, j * DK7:(j + 1) * DK7], lb.probT[:, u % 2, j], lb.v[:, t, h * DK7:(h + 1) * DK7],
                                      start=(t == 0), stop=True, skip_group_check=True)
                    mm.then_inc(s["pv_psum"], 1)

                e.wait_ge(s["raw_ready"], 4 * NT)
                e.wait_ge(s["v_ready"], 2 * NT)
                for u in range(NU + 2):
                    if u < NU:
                        if u % NG == 0:
                            turn_tile(u // NG)
                        scores(u)
                    if 1 <= u < NU + 1:
                        turn_probabilities(u - 1)
                    if u >= 2:
                        values(u - 2)
                e.wait_ge(s["o_ready"], NU)
                for c in range(PAIRS7):
                    if c >= 2:
                        e.wait_ge(s["oT_ready"], c - 1)
                    tensor_turn(e, lambda t: lb.qk[:, t, c * P:(c + 1) * P], ps[1 + c % 2], C["ident"], s["oT_psum"])
                e.wait_ge(s["oT_ready"], PAIRS7)
                for t in range(NT):
                    for c in range(PAIRS7):
                        mm = e.matmul(ps[3][:, t * P:(t + 1) * P], lb.qT[:, c, t * P:(t + 1) * P], W("wo")[:, c * D:(c + 1) * D],
                                      start=(c == 0), stop=(c == PAIRS7 - 1))
                mm.then_inc(s["out_psum"], 1)

            @block.scalar
            def _(e):
                e.wait_ge(s["xT_psum"], 1)
                e.activation(xT[0:HALF, :], ps[0][0:HALF, :], ACT.Copy).then_inc(s["xT_ready"], 1)
                e.activation(xT[HALF:, 1:], ps[0][HALF:, 0:L - 1], ACT.Copy).then_inc(s["xT_ready"], 1)
                for t in range(NT):
                    for c in range(4):
                        if c == 0 and t >= 2:
                            e.wait_ge(s["turned_ready"], 4 * (t - 1))
                            e.wait_ge(s["straight_ready"], 2 * (t - 1))
                            e.wait_ge(s["sq_ready"], t - 1)
                        e.wait_ge(s["qk_psum"], 4 * t + c + 1)
                        e.activation(lb.raw[:, t % 2, 512 * c:512 * (c + 1)], ps[1 + c][:], ACT.Copy).then_inc(s["raw_ready"], 1)
                    for c in range(2):
                        e.wait_ge(s["v_psum"], 2 * t + c + 1)
                        e.activation(lb.v[:, t, 512 * c:512 * (c + 1)], ps[5 + c][:], ACT.Copy).then_inc(s["v_ready"], 1)
                    e.wait_ge(s["raw_ready"], 4 * (t + 1))
                    if t >= 1:
                        e.wait_ge(s["squares_ready"], t)
                    e.activation(lb.sq[:], lb.raw[:, t % 2], ACT.Square).then_inc(s["sq_ready"], 1)
                e.wait_ge(s["squares_ready"], NT)
                e.activation(lb.norm[:], lb.ss[:], ACT.Sqrt).then_inc(s["norm_ready"], 1)
                for u in range(NU + 2):
                    if u < NU:
                        t, g = divmod(u, NG)
                        if g == 0:
                            for i in range(4):
                                e.wait_ge(s["qkT_psum"], 4 * t + i + 1)
                                dst = (lb.qT[:, 4 * i:4 * i + 4, t * P:(t + 1) * P] if i < 2 else
                                       lb.kT[:, 4 * (i - 2):4 * (i - 2) + 4, WIN + t * P:WIN + (t + 1) * P])
                                e.activation(dst, ps[1][:].rearrange("p (c q) -> p c q", q=P), ACT.Copy).then_inc(s["qkT_ready"], 1)
                        if g == 2 and t + 1 < NT:
                            if t >= 2:
                                e.wait_ge(s["pv_psum"], NG * t)
                            e.wait_ge(s["v_ready"], 2 * NT)
                            for j in range(GROUP):
                                e.activation(lb.vb[WIN * j:WIN * (j + 1), t % 2, :, j * DK7:(j + 1) * DK7],
                                             lb.v[P - WIN:, t].rearrange("p (g j d) -> p g j d", g=NG, j=GROUP)[:, :, j],
                                             ACT.Copy).then_inc(s["v_before"], 1)
                        e.wait_ge(s["bias_ready"], u + 1)
                        if u >= 2:
                            e.wait_ge(s["probT_psum"], u - 1)
                        for j in range(GROUP):
                            h = GROUP * g + j
                            i = e.activation(lb.prob[:, u % 2, j], S(u, j % 2)[:, (j // 2) * SPAN:(j // 2 + 1) * SPAN], ACT.Exp,
                                             bias=lb.nmx[:, u, j:j + 1], scale=lb.q8[:, t, h:h + 1],
                                             accum_out=lb.sm[:, u, j:j + 1])
                        i.then_inc(s["prob_ready"], 1)
                    if 1 <= u < NU + 1:
                        e.wait_ge(s["probT_psum"], u)
                        if u >= 3:
                            e.wait_ge(s["pv_psum"], u - 2)
                        e.activation(lb.probTb[:, (u - 1) % 2], ps[7][:, 0:P], ACT.Copy).then_inc(s["probTb_ready"], 1)
                for c in range(PAIRS7):
                    e.wait_ge(s["oT_psum"], c + 1)
                    e.activation(lb.qT[:, c], ps[1 + c % 2][:], ACT.Copy).then_inc(s["oT_ready"], 1)

            @block.vector
            def _(e):
                vector_take(e, s, x_all, b, xc)
                e.memset(xT[HALF:, 0:1], 0.0).then_inc(s["first_zero"], 1)
                for t in range(NT):
                    e.wait_ge(s["raw_ready"], 4 * (t + 1))
                    for i in range(2):
                        src = heads(lb.raw[:, t % 2, i * INNER7:(i + 1) * INNER7])
                        cos = lb.table[:, 2 * i, t].unsqueeze(1).to_broadcast([P, H7, DK7])
                        e.tensor_tensor(heads(lb.qk[:, t, i * INNER7:(i + 1) * INNER7]), src, cos, ALU.mult).then_inc(s["straight_ready"], 1)
                        if t >= 1:
                            e.wait_ge(s["rotated"], 2 * (t - 1) + i + 1)
                        part = heads(lb.part[:, i * INNER7:(i + 1) * INNER7])
                        for hf in range(2):
                            to, of = slice(32 * hf, 32 * hf + 32), slice(32 - 32 * hf, 64 - 32 * hf)
                            sin = lb.table[:, 2 * i + 1, t, to].unsqueeze(1).to_broadcast([P, H7, DK7 // 2])
                            e.tensor_tensor(part[:, :, to], src[:, :, of], sin, ALU.mult).then_inc(s["turned_ready"], 1)
                    e.wait_ge(s["sq_ready"], t + 1)
                    e.tensor_reduce(lb.ss[:, t], heads(lb.sq[:]), AX_X, ALU.add).then_inc(s["squares_ready"], 1)
                e.wait_ge(s["norm_ready"], 1)
                e.tensor_scalar(lb.norm[:], lb.norm[:], 1e-12, None, ALU.max).then_inc(s["norm_floored"], 1)
                e.wait_ge(s["norm_floored"], 1)
                e.reciprocal(lb.rn[:], lb.norm[:]).then_inc(s["rnorm_ready"], 1)
                e.wait_ge(s["rnorm_ready"], 1)
                e.tensor_scalar(lb.q8[:], lb.rn[:, :, 0:H7], QK_SCALE, None, ALU.mult).then_inc(s["q8_ready"], 1)
                for t in range(NT):
                    e.wait_ge(s["rotated"], 2 * (t + 1))
                    k = heads(lb.qk[:, t, INNER7:])
                    e.tensor_tensor(k, k, lb.rn[:, t, H7:].unsqueeze(2).to_broadcast([P, H7, DK7]), ALU.mult).then_inc(s["k_normed"], 1)
                e.wait_ge(s["q8_ready"], 1)
                for u in range(NU + 3):
                    if u < NU:
                        t, g = divmod(u, NG)
                        e.wait_ge(s["s_psum"], u + 1)
                        for odd in range(2):
                            e.tensor_reduce(lb.mx[:, u, odd::2], S(u, odd)[:, 0:2 * SPAN].rearrange("p (j k) -> p j k", k=SPAN), AX_X,
                                            ALU.max).then_inc(s["max_ready"], 1)
                        e.wait_ge(s["max_ready"], 2 * (u + 1))
                        e.scalar_tensor_tensor(lb.nmx[:, u], lb.mx[:, u], -1.0, lb.q8[:, t, GROUP * g:GROUP * (g + 1)], ALU.mult,
                                               ALU.mult).then_inc(s["bias_ready"], 1)
                    if 1 <= u < NU + 1:
                        e.wait_ge(s["probT_psum"], u)
                        if u >= 3:
                            e.wait_ge(s["pv_psum"], u - 2)
                        e.tensor_copy(lb.probT[:, (u - 1) % 2].rearrange("p j q -> p (j q)"), ps[6][:]).then_inc(s["probT_ready"], 1)
                    if 2 <= u < NU + 2:
                        t, g = divmod(u - 2, NG)
                        e.wait_ge(s["prob_ready"], u - 1)
                        e.reciprocal(lb.rs[:, u - 2], lb.sm[:, u - 2]).then_inc(s["rsum_ready"], 1)
                        e.wait_ge(s["rsum_ready"], u - 1)
                        e.wait_ge(s["pv_psum"], u - 1)
                        e.tensor_tensor(heads(lb.qk[:, t, GROUP * DK7 * g:GROUP * DK7 * (g + 1)]), heads(ps[0][:, 0:GROUP * DK7]),
                                        lb.rs[:, u - 2].unsqueeze(2).to_broadcast([P, GROUP, DK7]), ALU.mult).then_inc(s["o_ready"], 1)
                e.wait_ge(s["out_psum"], 1)
                e.tensor_tensor(x_all[:, ds(NT * b, NT), :], ps[3][:].rearrange("p (t d) -> p t d", d=D), xc[:], ALU.add)

            @block.gpsimd
            def _(e):
                for t in range(NT):
                    for i in range(2):
                        e.wait_ge(s["straight_ready"], 2 * t + i + 1)
                        e.wait_ge(s["turned_ready"], 4 * t + 2 * i + 2)
                        qk = lb.qk[:, t, i * INNER7:(i + 1) * INNER7]
                        e.tensor_tensor(qk, qk, lb.part[:, i * INNER7:(i + 1) * INNER7], ALU.add).then_inc(s["rotated"], 1)
                for u in range(NU):
                    e.wait_ge(s["prob_ready"], u + 1)
                    if u >= 2:
                        e.wait_ge(s["probT_psum"], u - 1)
                    e.tensor_copy(lb.probb[:, u % 2].rearrange("p (j k) -> p j k", k=WIN), lb.prob[:, u % 2, :, 0:WIN]).then_inc(s["before_ready"], 1)


def gated_mlp_stage(nc, ps, x_all, C, late, half, nb, xc, xT, xs, hid, gl, lb, parity):
    HC = HID7 // P
    W = lambda n: lb.w(parity, n)
    names = ("x_copied shift_psum first_half second_half xs_ready normed xT_psum xT_ready a_psum gate_psum gelu_ready "
             "hid_ready out_psum" + NORM_SIGNALS)
    with nc.Fori(0, B) as b:
        with stage(nc, f"glu{parity}", names) as (block, s):
            @block.tensor
            def _(e):
                e.wait_ge(s["x_copied"], 1)
                e.matmul(ps[0][:, 0:NT * HALF], late["next_token"], xc[:, :, HALF:], start=True, stop=False, skip_group_check=True)
                e.matmul(ps[0][:, HALF:NT * HALF], late["last_to_first"], xc[:, 0:NT - 1, HALF:], start=False, stop=True,
                         skip_group_check=True).then_inc(s["shift_psum"], 1)
                e.wait_ge(s["normed"], NT)
                tensor_turn(e, lambda t: xs[:, t], ps[1], C["ident"], s["xT_psum"])
                e.wait_ge(s["xT_ready"], 1)
                for c in range(HC):
                    e.matmul(ps[2 + c % 2][:] if c < 2 else ps[0][:], W("w1")[:, HID7 + c * P:HID7 + (c + 1) * P], xT[:], start=True,
                             stop=True).then_inc(s["gate_psum"], 1)
                    e.matmul(ps[4 + c][:], W("w1")[:, c * P:(c + 1) * P], xT[:], start=True, stop=True).then_inc(s["a_psum"], 1)
                e.wait_ge(s["hid_ready"], HC)
                for t in range(NT):
                    y = ps[7][:, t * P:(t + 1) * P]
                    e.matmul(y, C["ones"][0:1, :], W("b2")[0:1, :], start=True, stop=False)
                    for c in range(HC):
                        mm = e.matmul(y, hid[:, c, t * P:(t + 1) * P], W("w2")[:, c * P:(c + 1) * P], start=False, stop=(c == HC - 1))
                mm.then_inc(s["out_psum"], 1)

            @block.scalar
            def _(e):
                e.wait_ge(s["x_copied"], 1)
                e.activation(xs[:, :, 0:HALF], xc[:, :, 0:HALF], ACT.Copy).then_inc(s["first_half"], 1)
                e.wait_ge(s["xT_psum"], 1)
                e.activation(xT[:], ps[1][:], ACT.Identity, bias=W("ln")[:, 1:2], scale=W("ln")[:, 0:1]).then_inc(s["xT_ready"], 1)
                for c in range(HC):
                    e.wait_ge(s["gate_psum"], c + 1)
                    e.activation(gl[:, c], ps[2 + c][:] if c < 2 else ps[0][:], ACT.Gelu,
                                 bias=W("b1")[:, HC + c:HC + c + 1]).then_inc(s["gelu_ready"], 1)

            @block.vector
            def _(e):
                vector_take(e, s, x_all, b, xc)
                e.wait_ge(s["shift_psum"], 1)
                e.tensor_copy(xs[:, :, HALF:], ps[0][:, 0:NT * HALF].rearrange("p (t d) -> p t d", d=HALF)).then_inc(s["second_half"], 1)
                e.wait_ge(s["second_half"], 1)
                e.wait_ge(s["first_half"], 1)
                e.sem_inc(s["sum_ready"], NT)
                vector_moments(e, s, nb, lambda t: xs[:, t])
                vector_normalize(e, s, nb, lambda t: xs[:, t], lambda t: xs[:, t], signal="normed")
                for c in range(HC):
                    e.wait_ge(s["a_psum"], c + 1)
                    e.wait_ge(s["gelu_ready"], c + 1)
                    e.scalar_tensor_tensor(hid[:, c], ps[4 + c][:], W("b1")[:, c:c + 1], gl[:, c], ALU.add,
                                           ALU.mult).then_inc(s["hid_ready"], 1)
                e.wait_ge(s["out_psum"], 1)
                e.tensor_tensor(x_all[:, ds(NT * b, NT), :], ps[7][:].rearrange("p (t d) -> p t d", d=D), xc[:], ALU.add)

            @block.gpsimd
            def _(e):
                pool_rstd(e, s, nb, half)


def layers(nc, ctx, ps, x_all, C, half, nb, xc, xT, late_layout, late_dram, layers_dram, arrived):
    sbl = lambda n, shape: ctx.enter_context(nc.sbuf_tensor(n, shape, F32))
    late = Packed(nc, ctx, "late", late_layout, late_dram)
    lb = LayerBuffers(nc, ctx)
    layers_start_stage(nc, lb, late, late_dram, layers_dram, arrived)
    xs = lb.raw[:, 0, 0:NT * D].rearrange("p (t d) -> p t d", d=D)
    hid = lb.qk[:, 0, 0:HID7 // P * L].rearrange("p (c t) -> p c t", t=L)
    gl = lb.qk[:, 1, 0:HID7 // P * L].rearrange("p (c t) -> p c t", t=L)
    with nc.Fori(0, DEPTH // 2) as i:
        for parity in range(2):
            layer_prepare_stage(nc, lb, late, layers_dram, arrived, parity, 2 * i + parity + 1)
            local_attention_stage(nc, ps, x_all, C, xc, xT, lb, parity)
            gated_mlp_stage(nc, ps, x_all, C, late, half, nb, xc, xT, xs, hid, gl, lb, parity)
    with stage(nc, "laye", "none") as (block, s):
        @block.sync
        def _(e):
            e.wait_ge(arrived, 16)


def last_norm_stage(nc, x_all, x_in, half, nb, xc):
    with nc.Fori(0, B) as b:
        with stage(nc, "fin", "x_copied" + NORM_SIGNALS) as (block, s):
            @block.vector
            def _(e):
                e.tensor_tensor(nb.r[:], x_in[:, ds(NT * b, NT), :], x_all[:, ds(NT * b, NT), :], ALU.add).then_inc(s["sum_ready"], NT)
                vector_moments(e, s, nb, lambda t: nb.r[:, t])
                vector_normalize(e, s, nb, lambda t: nb.r[:, t], lambda t: x_all[:, ds(NT * b + t, 1), :])

            @block.gpsimd
            def _(e):
                pool_rstd(e, s, nb, half)



class Packed:

    def __init__(self, nc, ctx, name, layout, dram, first=0, dtype=F32):
        self.width = sum(w for _, w in layout)
        self.all = ctx.enter_context(nc.sbuf_tensor(name + "_sb", [P, self.width], dtype))
        self.dram = dram
        self.at = {}
        self.first = 0
        o = 0
        for n, w in layout:
            self.at[n] = (o, w)
            o += w
            if n == first:
                self.first = o

    def __getitem__(self, name):
        o, w = self.at[name]
        return self.all[:, o:o + w]


class Names:

    def __init__(self, *packs):
        self.packs = packs

    def __getitem__(self, name):
        return next(p for p in self.packs if name in p.at)[name]


def build(nc, a, layouts):
    with ExitStack() as ctx:
        def sb(name, shape, dtype=F32):
            return ctx.enter_context(nc.sbuf_tensor(name, shape, dtype))

        ps = [ctx.enter_context(nc.psum_tensor(f"bank{i}", [P, 512], F32)) for i in range(8)]
        arrived = ctx.enter_context(nc.semaphore("layer_weights_arrived"))
        x_all = sb("x_all", [P, B * NT, D])
        C = Packed(nc, ctx, "constants", layouts["constants"], a["constants"])
        nb = NormBuffers(sb)
        half = C["minus_half"]
        xc = sb("x_batch", [P, NT, D])
        xT = sb("x_batchT", [P, L])
        with ExitStack() as early:
            sbe = lambda n, shape, dtype=F32: early.enter_context(nc.sbuf_tensor(n, shape, dtype))
            W = Packed(nc, early, "weights", layouts["weights"], a["weights"], first="L0_b_out")
            CE = Packed(nc, early, "early", layouts["early"], a["early"])
            CC = Names(C, CE)
            recurrence_stage(nc, ps, a["L0_attn_x"], x_all, W, C, CE, half, nb)
            args = (nc, ps, x_all, W, CC, half, nb, xc, xT)
            experts_stage(*args)
            eg = Eigen(sbe)
            eigen_tables_stage(nc, ps, W, CC, eg)
            eigen_stage(*args, eg)
            ternary_weights_stage(nc, ps, W, CC)
            ternary_stage(*args)
            ident_bf, mask_bf = sbe("ident_bf", [P, P], BF16), sbe("mask_bf", [P, P], BF16)
            with stage(nc, "masks", "copied") as (block, s):
                @block.vector
                def _(e):
                    e.tensor_copy(ident_bf[:], C["ident"]).then_inc(s["copied"], 1)
                    e.tensor_copy(mask_bf[:], CE["causal_mask"]).then_inc(s["copied"], 1)
            causal_stage(*args, ident_bf, mask_bf)
            relu_stage(*args)
            features_stage(*args)
        x_in = sb("x_in", [P, B * NT, D])
        with stage(nc, "keep", "kept") as (block, s):
            @block.vector
            def _(e):
                e.tensor_copy(x_in[:], x_all[:]).then_inc(s["kept"], 1)
        with ExitStack() as last:
            layers(nc, last, ps, x_all, C, half, nb, xc, xT, layouts["late"], a["late"], a["layers"], arrived)
        last_norm_stage(nc, x_all, x_in, half, nb, xc)
        with stage(nc, "end", "stored") as (block, s):
            @block.sync
            def _(e):
                e.dma_start(a["out"].rearrange("b (j p) d -> p (b j) d", p=P), x_all[:]).then_inc(s["stored"], 16)
                e.wait_ge(s["stored"], 16)


def host_layouts(v):
    def rows(w):
        w = np.asarray(w)
        k, m = w.shape
        return w.reshape(k // P, P, m).transpose(1, 0, 2).reshape(P, -1)

    def cols(b):
        return np.asarray(b).reshape(-1, P).T

    def row(b):
        b = np.asarray(b).reshape(1, -1)
        return np.repeat(b, P, 0)

    z = np.zeros
    weights = []
    add = lambda n, w: weights.append((n, np.ascontiguousarray(w, dtype=np.float32)))
    A = np.asarray(v["L0_attn_A"])
    A_pad = z((E0, 32), np.float32)
    A_pad[:, :NS] = A
    CT = z((P, E0), np.float32)
    for b in range(B):
        CT[32 * b:32 * b + NS] = np.asarray(v["L0_attn_C"]).T
    add("L0_W_in", np.asarray(v["L0_attn_W_in"]))
    add("L0_b_in", cols(v["L0_attn_b_in"]))
    cw = np.asarray(v["L0_attn_conv_w"]).reshape(E0 // P, P, TAPS).transpose(1, 0, 2).reshape(P, -1)
    add("L0_conv_w", cw)
    add("L0_conv_b", cols(v["L0_attn_conv_b"]))
    add("L0_A", rows(A_pad))
    add("L0_CT", CT)
    add("L0_Dp", cols(v["L0_attn_Dp"]))
    add("L0_W_out", rows(v["L0_attn_W_out"]))
    add("L0_b_out", row(v["L0_attn_b_out"]))

    add("moe_router", np.asarray(v["L0_ffn_router_w"]))
    pairs = lambda w: np.asarray(w).transpose(1, 0, 2).reshape(D, NE * IE)
    add("moe_router_bias", row(v["L0_ffn_router_bias"]))
    add("moe_gate", np.concatenate([pairs(v["L0_ffn_gate_w"]), np.asarray(v["L0_ffn_s_gate_w"])], 1))
    add("moe_up", np.concatenate([pairs(v["L0_ffn_up_w"]), np.asarray(v["L0_ffn_s_up_w"])], 1))
    add("moe_down", rows(np.concatenate([np.asarray(v["L0_ffn_down_w"]).reshape(NE * IE, D), np.asarray(v["L0_ffn_s_down_w"])], 0)))
    w_in = np.asarray(v["L1_attn_w_in"])
    twice = lambda c: np.concatenate([np.asarray(c)] * 2).reshape(P, 1)
    coupling = z((P, P), np.float32)
    for i in range(P // 16):
        coupling[16 * i:16 * i + 16, 16 * i:16 * i + 16] = np.asarray(v["L1_attn_coupling"])[i % 4]
    add("L1_w_in", w_in.T)
    add("L1_w_in_swapped", np.concatenate([w_in[KS:], w_in[:KS]]).T)
    add("L1_coupling", coupling)
    add("L1_w_out", np.asarray(v["L1_attn_w_out"]).T)
    add("L1_w_gate", np.asarray(v["L1_attn_w_gate"]).T)
    add("L1_b_gate", row(v["L1_attn_b_gate"]))
    add("L1_log_decay", twice(v["L1_attn_log_decay"]))
    add("L1_frequency", twice(v["L1_attn_frequency"]))
    add("L1_w_mlp1", np.asarray(v["L1_attn_w_mlp1"]).T)
    add("L1_b_mlp1", cols(v["L1_attn_b_mlp1"]))
    add("L1_w_mlp2", rows(np.asarray(v["L1_attn_w_mlp2"]).T))
    add("L1_b_mlp2", row(v["L1_attn_b_mlp2"]))
    add("L1_ln1", np.stack([np.asarray(v["L1_attn_ln1_g"]), np.asarray(v["L1_attn_ln1_b"])], 1))
    add("L1_ln2", np.stack([np.asarray(v["L1_attn_ln2_g"]), np.asarray(v["L1_attn_ln2_b"])], 1))
    add("L1f_W_fc", np.asarray(v["L1_ffn_W_fc"]).T)
    add("L1f_W_proj", rows(np.asarray(v["L1_ffn_W_proj"]).T))
    add("L1f_ln_w", cols(v["L1_ffn_ln_w"]))
    add("L1f_ln_b", cols(v["L1_ffn_ln_b"]))
    partner = np.arange(H4 * DK4) ^ 1
    for w in "qk":
        wt, bt = np.asarray(v[f"L2_attn_w{w}"]), np.asarray(v[f"L2_attn_b{w}"])
        add(f"L2_w{w}", wt.T)
        add(f"L2_w{w}_turned", wt[partner].T)
        add(f"L2_b{w}", cols(bt))
        add(f"L2_b{w}_turned", cols(bt[partner]))
    add("L2_wv", np.asarray(v["L2_attn_wv"]).T)
    add("L2_bv", row(v["L2_attn_bv"]))
    add("L2_wo", rows(np.asarray(v["L2_attn_wo"]).T))
    add("L2_bo", row(v["L2_attn_bo"]))
    add("L2f_W1", np.asarray(v["L2_ffn_W1"]))
    add("L2f_b1", cols(v["L2_ffn_b1"]))
    add("L2f_W2", rows(v["L2_ffn_W2"]))
    add("L2f_b2", row(v["L2_ffn_b2"]))
    for w in ("Wq", "Wk", "Wv", "Wo", "Wfc"):
        add("L3_" + w, np.asarray(v["L3_attn_" + w]).T)
    for w in ("bq", "bk", "bo"):
        add("L3_" + w, cols(v["L3_attn_" + w]))
    add("L3_bv", row(v["L3_attn_bv"]))
    add("L3_bfc", row(v["L3_attn_bfc"]))
    proj = z((D, FEATS), np.float32)
    for h in range(H6):
        proj[DH6 * h:DH6 * (h + 1), M6 * h:M6 * (h + 1)] = np.asarray(v["L3_attn_proj"]).T
    add("L3_proj", proj)
    constants = []
    addc = lambda n, w: constants.append((n, np.ascontiguousarray(w, dtype=np.float32)))
    addc("ident", np.eye(P))
    addc("ones", np.ones((P, P)))
    addc("minus_half", np.full((P, 1), -0.5))
    early = []
    adde = lambda n, w: early.append((n, np.ascontiguousarray(w, dtype=np.float32)))
    spread = np.zeros((P, PAIRS * P))
    for i in range(NE):
        spread[i, IE * i:IE * (i + 1)] = 1
    adde("pair_of_expert", spread)
    adde("comes_first", np.repeat((np.arange(NE)[None] < np.arange(NE)[:, None]).reshape(1, -1), P, 0))
    adde("steps", np.repeat(np.arange(CH).reshape(1, -1), P, 0))
    adde("not_first", np.repeat((np.arange(CH) > 0).reshape(1, -1), P, 0))
    adde("half_sign", np.where(np.arange(P) < KS, 1.0, -1.0).reshape(P, 1))
    adde("swap", np.roll(np.eye(P), KS, 0))
    f32 = np.float32
    i, j = np.arange(P)[:, None], np.arange(P)[None]
    adde("causal_mask", np.where(j > i, MASKED, 0.0))
    theta = f32(10000.0) ** (np.arange(0, DK4, 2, dtype=f32) / f32(DK4))
    freqs = np.arange(L, dtype=f32)[:, None] * (f32(1) / theta)[None]
    emb = np.concatenate([freqs, freqs], 1).T
    sign = np.where(np.arange(DK4) % 2 == 0, -1.0, 1.0)[:, None]
    adde("rope4_cos", np.tile(np.cos(emb), (2, 1)))
    adde("rope4_sin", np.tile(np.sin(emb) * sign, (2, 1)))
    adde("head_of_feature", np.arange(P)[:, None] // DH6 == np.arange(H6)[None])
    own = np.zeros((P, FEATS // P, D + H6))
    for m in range(FEATS // P):
        h = (m * P + np.arange(P)) // M6
        own[:, m, :D] = h[:, None] == np.arange(D)[None] // DH6
        own[:, m, D:] = h[:, None] == np.arange(H6)[None]
    adde("own_columns", own.reshape(P, -1))

    late = []
    addl = lambda n, w: late.append((n, np.ascontiguousarray(w, dtype=np.float32)))
    back = np.arange(P)[:, None] - (np.arange(SPAN)[None] - WIN)
    band = np.where((back >= 0) & (back <= WIN), 0.0, MASKED)
    first = np.where(np.arange(SPAN)[None] < WIN, MASKED, band)
    addl("band_masks", np.concatenate([first, band], 1))
    addl("ident_late", np.eye(P))
    addl("next_token", np.eye(P, k=1))
    last_to_first = np.zeros((P, P))
    last_to_first[P - 1, 0] = 1
    addl("last_to_first", last_to_first)
    hw = np.arange(0, DK7, 2, dtype=f32)
    inv = f32(1.0) / f32(10000.0) ** (hw / f32(DK7))
    tt = np.arange(L, dtype=f32)
    fr = tt[:, None] * inv[None]
    base = (hw + f32(0.4 * DK7)) / f32(1.4 * DK7)
    power = (tt - L // 2) / f32(WIN // 2)
    sc = (base[None] ** power[:, None]).astype(f32)
    fr, sc = np.concatenate([fr, fr], 1), np.concatenate([sc, sc], 1)
    sg = np.where(np.arange(DK7) < DK7 // 2, -1.0, 1.0)[None]
    tok = lambda x: x.reshape(NT, P, DK7).transpose(1, 0, 2).reshape(P, -1)
    addl("rope7", np.concatenate([tok(np.cos(fr) * sc), tok(np.sin(fr) * sg * sc), tok(np.cos(fr) / sc), tok(np.sin(fr) * sg / sc)], 1))

    g = lambda n: np.asarray(v["L3_ffn_" + n])
    inner = g("W2").shape[1]
    layers_ = np.zeros((DEPTH + 1, P, sum(w for _, w in LAYER_COLUMNS)), np.float32)
    for d in range(DEPTH):
        w1, b1 = z((D, 2, HID7), np.float32), z((2, HID7), np.float32)
        w1[:, :, :inner] = g("W1")[d].reshape(D, 2, inner)
        b1[:, :inner] = g("b1")[d].reshape(2, inner)
        w2 = z((HID7, D), np.float32)
        w2[:inner] = g("W2")[d]
        part = {"qkv": g("Wqkv")[d], "wo": rows(g("Wo")[d]), "w1": w1.reshape(D, -1), "w2": rows(w2), "b1": cols(b1),
                "ln": np.stack([g("ln_g")[d], g("ln_b")[d]], 1), "b2": row(g("b2")[d]),
                "q_scale": row(g("q_scale")[d]), "q_scale_rolled": row(np.roll(g("q_scale")[d], DK7 // 2)),
                "k_scale": row(g("k_scale")[d]), "k_scale_rolled": row(np.roll(g("k_scale")[d], DK7 // 2))}
        layers_[d] = np.concatenate([part[n] for n, _ in LAYER_COLUMNS], 1)
    packs = {"weights": weights, "constants": constants, "early": early, "late": late}
    out = {k: np.concatenate([w for _, w in p], 1) for k, p in packs.items()}
    out["layers"] = layers_
    return out, {k: [(n, w.shape[1]) for n, w in p] for k, p in packs.items()}


def kernel(**v):
    import concourse.bacc as bacc
    from concourse.bass_utils import run_bass_kernel_spmd as run

    arrays, lay = host_layouts(v)
    arrays["L0_attn_x"] = np.asarray(v["L0_attn_x"])
    nc = bacc.Bacc("TRN2", target_bir_lowering=False, num_devices=1)
    aps = {n: nc.dram_tensor(n, x.shape, mybir.dt.from_np(x.dtype), kind="ExternalInput").ap() for n, x in arrays.items()}
    aps["out"] = nc.dram_tensor("out", (B, L, D), F32, kind="ExternalOutput").ap()
    build(nc, aps, lay)
    return run(nc, [arrays], core_ids=[0]).results[0]["out"]
```

```python
from contextlib import ExitStack, contextmanager

import numpy as np

import concourse.bass as bass
from concourse import mybir

F32 = mybir.dt.float32
BF16 = mybir.dt.bfloat16
ALU = mybir.AluOpType
ACT = mybir.ActivationFunctionType
AX_X = mybir.AxisListType.X
ds = bass.ds

P = 128
B, L, D = 4, 512, 128
NT = L // P
LN_EPS = 1e-5
FIRST_SEMAPHORE = 110
MASKED = -1e30


class Signals:

    def __init__(self, nc, ctx, stage, names):
        self.nums = []
        self.of = {}
        for i, n in enumerate(names.split()):
            s = ctx.enter_context(nc.semaphore(f"{stage}_{n}", num=FIRST_SEMAPHORE + i))
            self.nums.append(s.num)
            self.of[n] = s

    def __getitem__(self, name):
        return self.of[name]


@contextmanager
def stage(nc, name, signals):
    with ExitStack() as ctx:
        s = Signals(nc, ctx, name, signals)
        with nc.Block(no_gpsimd_drain=True) as block:
            yield block, s
        nc.all_engine_barrier(sems_to_clear=range(min(s.nums), max(s.nums) + 1))



NORM_SIGNALS = " sum_ready stats_ready moments_ready eps_added rstd_ready"


class NormBuffers:
    def __init__(self, sb):
        self.r = sb("norm_sum", [P, NT, D])
        self.stats = sb("norm_stats", [P, NT, 6])
        self.moments = sb("norm_moments", [P, NT, 2])
        self.veps = sb("norm_veps", [P, NT])
        self.rstd = sb("norm_rstd", [P, NT])


def vector_moments(e, s, nb, value, round_=0):
    for t in range(NT):
        e.wait_ge(s["sum_ready"], NT * round_ + t + 1)
        e.bn_stats(nb.stats[:, t], value(t)).then_inc(s["stats_ready"], 1)
    for t in range(NT):
        e.wait_ge(s["stats_ready"], NT * round_ + t + 1)
        e.bn_aggr(nb.moments[:, t], nb.stats[:, t]).then_inc(s["moments_ready"], 1)


def pool_rstd(e, s, nb, half, eps=LN_EPS, round_=0):
    e.wait_ge(s["moments_ready"], NT * (round_ + 1))
    e.tensor_scalar(nb.veps[:], nb.moments[:, :, 1], eps, None, ALU.add).then_inc(s["eps_added"], 1)
    e.wait_ge(s["eps_added"], round_ + 1)
    e.tensor_tensor(nb.rstd[:], nb.veps[:], half.to_broadcast([P, NT]), ALU.pow).then_inc(s["rstd_ready"], 1)


def vector_normalize(e, s, nb, value, out, round_=0, signal=None):
    e.wait_ge(s["rstd_ready"], round_ + 1)
    for t in range(NT):
        i = e.tensor_scalar(out(t), value(t), nb.moments[:, t, 0:1], nb.rstd[:, t:t + 1],
                            ALU.subtract, ALU.mult)
        if signal is not None:
            i.then_inc(s[signal], 1)



E0 = 256
NS = 16
TAPS = 4
SCAN_STEPS = 8


def recurrence_stage(nc, ps, x_dram, x_all, W, C, CE, half, nb):
    EC = E0 // P
    with ExitStack() as ctx:
        sbl = lambda n, shape: ctx.enter_context(nc.sbuf_tensor(n, shape, F32))
        xT = sbl("r_xT", [P, B, L])
        xp = sbl("r_xp", [P, EC, B, TAPS - 1 + L])
        xconv = sbl("r_xconv", [P, EC, B, L])
        sig = sbl("r_sig", [P, EC, B, L])
        h = sbl("r_h", [P, 1 + L])
        u = ps[5]
        names = ("x_loaded w_rest early_loaded w_loaded c_loaded xT_psum xT_ready xp_psum xp_ready z_psum sig_ready pad_zero tap_done "
                 "conv_ready u_ready h_zero h_step scan_done ch_psum skip_done y_ready out_psum out_read" + NORM_SIGNALS)
        with stage(nc, "rec", names) as (block, s):
            @block.sync
            def _(e):
                e.dma_start(C.all[:], C.dram).then_inc(s["c_loaded"], 16)
                e.dma_start(x_all[:], x_dram.rearrange("b (j p) d -> p (b j) d", p=P)).then_inc(s["x_loaded"], 16)
                e.dma_start(W.all[:, 0:W.first], W.dram[:, 0:W.first]).then_inc(s["w_loaded"], 16)
                e.dma_start(W.all[:, W.first:], W.dram[:, W.first:]).then_inc(s["w_rest"], 16)
                e.dma_start(CE.all[:], CE.dram).then_inc(s["early_loaded"], 16)
                e.wait_ge(s["w_rest"], 16)
                e.wait_ge(s["early_loaded"], 16)

            @block.tensor
            def _(e):
                e.wait_ge(s["x_loaded"], 16)
                e.wait_ge(s["c_loaded"], 16)
                e.wait_ge(s["w_loaded"], 16)
                for b in range(B):
                    if b >= 1:
                        e.wait_ge(s["xT_ready"], b)
                    for t in range(NT):
                        mm = e.transpose(ps[0][:, t * P:(t + 1) * P], x_all[:, NT * b + t, :], C["ident"])
                    mm.then_inc(s["xT_psum"], 1)
                    e.wait_ge(s["xT_ready"], b + 1)
                    for c in range(EC):
                        if b >= 1:
                            e.wait_ge(s["xp_ready"], EC * (b - 1) + c + 1)
                        e.matmul(ps[1 + c][:], W["L0_W_in"][:, c * P:(c + 1) * P], xT[:, b], start=True,
                                 stop=True).then_inc(s["xp_psum"], 1)
                    for c in range(EC):
                        if b >= 1:
                            e.wait_ge(s["sig_ready"], EC * (b - 1) + c + 1)
                        e.matmul(ps[3 + c][:], W["L0_W_in"][:, E0 + c * P:E0 + (c + 1) * P], xT[:, b], start=True,
                                 stop=True).then_inc(s["z_psum"], 1)
                for b in range(B):
                    e.wait_ge(s["conv_ready"], EC * (b + 1))
                    for c in range(EC):
                        mm = e.matmul(u[32 * b:32 * b + 32, :], W["L0_A"][:, 32 * c:32 * c + 32], xconv[:, c, b],
                                      start=(c == 0), stop=(c == EC - 1))
                    mm.then_inc(s["u_ready"], 1)
                e.wait_ge(s["scan_done"], 1)
                for b in range(B):
                    for c in range(EC):
                        if b >= 1:
                            e.wait_ge(s["skip_done"], EC * (b - 1) + c + 1)
                        e.matmul(ps[1 + c][:], W["L0_CT"][32 * b:32 * b + 32, c * P:(c + 1) * P],
                                 h[32 * b:32 * b + 32, 1:], start=True, stop=True).then_inc(s["ch_psum"], 1)
                    e.wait_ge(s["y_ready"], EC * (b + 1))
                    if b >= 2:
                        e.wait_ge(s["out_read"], NT * (b - 1))
                    for t in range(NT):
                        o = ps[6 + b % 2][:, t * P:(t + 1) * P]
                        e.matmul(o, C["ones"][0:1, :], W["L0_b_out"][0:1, :], start=True, stop=False)
                        for c in range(EC):
                            mm = e.matmul(o, xconv[:, c, b, t * P:(t + 1) * P], W["L0_W_out"][:, c * P:(c + 1) * P],
                                          start=False, stop=(c == EC - 1))
                    mm.then_inc(s["out_psum"], 1)

            @block.vector
            def _(e):
                for c in range(EC):
                    e.memset(xp[:, c, :, 0:TAPS - 1], 0.0).then_inc(s["pad_zero"], 1)
                e.memset(h[:, 0:1], 0.0).then_inc(s["h_zero"], 1)
                e.wait_ge(s["pad_zero"], EC)
                e.wait_ge(s["w_loaded"], 16)
                taps = 0
                for b in range(B):
                    e.wait_ge(s["xT_psum"], b + 1)
                    e.tensor_copy(xT[:, b], ps[0][:]).then_inc(s["xT_ready"], 1)
                    for c in range(EC):
                        e.wait_ge(s["xp_psum"], EC * b + c + 1)
                        e.tensor_scalar(xp[:, c, b, TAPS - 1:], ps[1 + c][:], W["L0_b_in"][:, c:c + 1], None,
                                        ALU.add).then_inc(s["xp_ready"], 1)
                    for c in range(EC):
                        cw = W["L0_conv_w"][:, TAPS * c:TAPS * (c + 1)]
                        e.wait_ge(s["xp_ready"], EC * b + c + 1)
                        e.tensor_scalar(xconv[:, c, b], xp[:, c, b, 0:L], cw[:, 0:1], W["L0_conv_b"][:, c:c + 1],
                                        ALU.mult, ALU.add).then_inc(s["tap_done"], 1)
                        taps += 1
                        for k in range(1, TAPS):
                            e.wait_ge(s["tap_done"], taps)
                            i = e.scalar_tensor_tensor(xconv[:, c, b], xp[:, c, b, k:k + L], cw[:, k:k + 1],
                                                       xconv[:, c, b], ALU.mult, ALU.add)
                            i.then_inc(s["tap_done" if k < TAPS - 1 else "conv_ready"], 1)
                            taps += k < TAPS - 1
                for b in range(B):
                    for c in range(EC):
                        e.wait_ge(s["ch_psum"], EC * b + c + 1)
                        e.wait_ge(s["conv_ready"], EC * b + c + 1)
                        e.scalar_tensor_tensor(xconv[:, c, b], xconv[:, c, b], W["L0_Dp"][:, c:c + 1], ps[1 + c][:],
                                               ALU.mult, ALU.add).then_inc(s["skip_done"], 1)
                        e.wait_ge(s["skip_done"], EC * b + c + 1)
                        e.wait_ge(s["sig_ready"], EC * b + c + 1)
                        e.tensor_tensor(xconv[:, c, b], xconv[:, c, b], sig[:, c, b], ALU.mult).then_inc(s["y_ready"], 1)
                    e.wait_ge(s["out_psum"], b + 1)
                    for t in range(NT):
                        e.tensor_tensor(nb.r[:, t], ps[6 + b % 2][:, t * P:(t + 1) * P], x_all[:, NT * b + t, :],
                                        ALU.add).then_inc(s["sum_ready"], 1)
                    e.wait_ge(s["sum_ready"], NT * (b + 1))
                    e.sem_inc(s["out_read"], NT)
                    vector_moments(e, s, nb, lambda t: nb.r[:, t], round_=b)
                    vector_normalize(e, s, nb, lambda t: nb.r[:, t], lambda t: x_all[:, NT * b + t, :], round_=b)

            @block.scalar
            def _(e):
                e.wait_ge(s["w_loaded"], 16)
                for b in range(B):
                    for c in range(EC):
                        e.wait_ge(s["z_psum"], EC * b + c + 1)
                        e.activation(sig[:, c, b], ps[3 + c][:], ACT.Sigmoid,
                                     bias=W["L0_b_in"][:, EC + c:EC + c + 1]).then_inc(s["sig_ready"], 1)
                e.wait_ge(s["h_zero"], 1)
                e.wait_ge(s["u_ready"], B)
                with e.Fori(0, L // SCAN_STEPS) as i:
                    for k in range(SCAN_STEPS):
                        if k:
                            e.wait_ge(s["h_step"], k)
                        e.activation(h[:, ds(i * SCAN_STEPS + k + 1, 1)], u[:, ds(i * SCAN_STEPS + k, 1)], ACT.Tanh,
                                     bias=h[:, ds(i * SCAN_STEPS + k, 1)]).then_inc(s["h_step"], 1)
                    e.wait_ge(s["h_step"], SCAN_STEPS)
                    e.sem_clear(s["h_step"])
                e.sem_inc(s["scan_done"], 1)

            @block.gpsimd
            def _(e):
                for b in range(B):
                    pool_rstd(e, s, nb, half, round_=b)



BATCH_SIGNALS = " x_copied xT_psum xT_ready out_psum" + NORM_SIGNALS


def vector_take(e, s, x_all, b, xc):
    e.tensor_copy(xc[:], x_all[:, ds(NT * b, NT), :]).then_inc(s["x_copied"], 1)


def tensor_turn(e, src, bank, ident, signal):
    for t in range(NT):
        mm = e.transpose(bank[:, t * P:(t + 1) * P], src(t), ident)
    mm.then_inc(signal, 1)


def vector_finish(e, s, nb, y, xc, x_all, b, extra=None):
    e.wait_ge(s["out_psum"], 1)
    for t in range(NT):
        e.tensor_tensor(nb.r[:, t], y(t), xc[:, t], ALU.add).then_inc(s["sum_ready"], 1)
    vector_moments(e, s, nb, lambda t: nb.r[:, t])
    vector_normalize(e, s, nb, lambda t: nb.r[:, t], lambda t: x_all[:, ds(NT * b + t, 1), :])



NE, TOPK = 8, 4
IE = 64
ISH = 256
PAIRS = NE * IE // P
CHUNKS = PAIRS + ISH // P


def experts_stage(nc, ps, x_all, W, C, half, nb, xc, xT):
    with ExitStack() as ctx:
        sbl = lambda n, shape: ctx.enter_context(nc.sbuf_tensor(n, shape, F32))
        g = sbl("moe_silu", [P, 2, L])
        prod = sbl("moe_prod", [P, CHUNKS, L])
        mx = sbl("moe_max", [P, NT])
        lg = sbl("moe_logits", [P, NT, NE])
        ex = sbl("moe_exp", [P, NT, NE])
        sm = sbl("moe_sum", [P, NT])
        rs = sbl("moe_rsum", [P, NT])
        sc = sbl("moe_scores", [P, NT, NE])
        co = sbl("moe_corrected", [P, NT, NE])
        gt = sbl("moe_greater", [P, NT, NE, NE])
        eq = sbl("moe_equal", [P, NT, NE, NE])
        rank = sbl("moe_rank", [P, NT, NE])
        picked = sbl("moe_picked", [P, NT, NE])
        w = sbl("moe_weight", [P, NT, NE])
        wT = sbl("moe_weightT", [NE, L])
        names = ("logits_psum shifted exp_ready route w_ready wT_psum wT_ready spread_psum spread_read "
                 "gate_psum up_psum silu_ready up_read prod_ready" + BATCH_SIGNALS)
        bc = lambda ap, shape: ap.to_broadcast(shape)
        with nc.Fori(0, B) as b:
            with stage(nc, "moe", names) as (block, s):
                @block.tensor
                def _(e):
                    e.wait_ge(s["x_copied"], 1)
                    tensor_turn(e, lambda t: xc[:, t], ps[0], C["ident"], s["xT_psum"])
                    e.wait_ge(s["xT_ready"], 1)
                    for t in range(NT):
                        mm = e.matmul(ps[1][:, t * NE:(t + 1) * NE], xT[:, t * P:(t + 1) * P], W["moe_router"],
                                      start=True, stop=True)
                    mm.then_inc(s["logits_psum"], 1)

                    def expand(c):
                        if c >= 2:
                            e.wait_ge(s["silu_ready"], c - 1)
                            e.wait_ge(s["up_read"], c - 1)
                        e.matmul(ps[2 + c % 2][:], W["moe_gate"][:, c * P:(c + 1) * P], xT[:], start=True,
                                 stop=True).then_inc(s["gate_psum"], 1)
                        e.matmul(ps[4 + c % 2][:], W["moe_up"][:, c * P:(c + 1) * P], xT[:], start=True,
                                 stop=True).then_inc(s["up_psum"], 1)

                    expand(0)
                    expand(1)
                    e.wait_ge(s["w_ready"], 1)
                    for t in range(NT):
                        mm = e.transpose(ps[6][0:NE, t * P:(t + 1) * P], w[:, t, :], C["ident"])
                    mm.then_inc(s["wT_psum"], 1)
                    e.wait_ge(s["wT_ready"], 1)
                    for c in range(CHUNKS):
                        if c >= 2:
                            expand(c)
                        if c < PAIRS:
                            if c >= 1:
                                e.wait_ge(s["spread_read"], c)
                            e.matmul(ps[0][:], C["pair_of_expert"][0:NE, c * P:(c + 1) * P], wT[:], start=True,
                                     stop=True).then_inc(s["spread_psum"], 1)
                    e.wait_ge(s["prod_ready"], CHUNKS)
                    for t in range(NT):
                        for c in range(CHUNKS):
                            mm = e.matmul(ps[7][:, t * P:(t + 1) * P], prod[:, c, t * P:(t + 1) * P],
                                          W["moe_down"][:, c * P:(c + 1) * P], start=(c == 0), stop=(c == CHUNKS - 1))
                    mm.then_inc(s["out_psum"], 1)

                @block.scalar
                def _(e):
                    e.wait_ge(s["xT_psum"], 1)
                    e.activation(xT[:], ps[0][:], ACT.Copy).then_inc(s["xT_ready"], 1)
                    e.wait_ge(s["shifted"], 1)
                    e.activation(ex[:], lg[:], ACT.Exp).then_inc(s["exp_ready"], 1)
                    for c in range(CHUNKS):
                        if c >= 2:
                            e.wait_ge(s["up_read"], c - 1)
                        e.wait_ge(s["gate_psum"], c + 1)
                        e.activation(g[:, c % 2], ps[2 + c % 2][:], ACT.Silu).then_inc(s["silu_ready"], 1)

                @block.vector
                def _(e):
                    vector_take(e, s, x_all, b, xc)
                    n = [0]

                    def routed(i):
                        n[0] += 1
                        i.then_inc(s["route"], 1)
                        e.wait_ge(s["route"], n[0])

                    s3, s4 = [P, NT, NE], [P, NT, NE, NE]
                    logits = ps[1][:, 0:NT * NE].rearrange("p (t e) -> p t e", e=NE)
                    e.wait_ge(s["logits_psum"], 1)
                    routed(e.tensor_reduce(mx[:], logits, AX_X, ALU.max))
                    e.tensor_tensor(lg[:], logits, bc(mx[:].unsqueeze(2), s3), ALU.subtract).then_inc(s["shifted"], 1)
                    e.wait_ge(s["exp_ready"], 1)
                    routed(e.tensor_reduce(sm[:], ex[:], AX_X, ALU.add))
                    routed(e.reciprocal(rs[:], sm[:]))
                    routed(e.tensor_tensor(sc[:], ex[:], bc(rs[:].unsqueeze(2), s3), ALU.mult))
                    routed(e.tensor_scalar(co[:], sc[:], W["moe_router_bias"], None, ALU.add))
                    other, own = bc(co[:].unsqueeze(2), s4), bc(co[:].unsqueeze(3), s4)
                    first = bc(C["comes_first"].rearrange("p (i j) -> p i j", j=NE).unsqueeze(1), s4)
                    e.tensor_tensor(gt[:], other, own, ALU.is_gt)
                    routed(e.tensor_tensor(eq[:], other, own, ALU.is_equal))
                    routed(e.tensor_tensor(eq[:], eq[:], first, ALU.mult))
                    routed(e.tensor_tensor(gt[:], gt[:], eq[:], ALU.add))
                    routed(e.tensor_reduce(rank[:], gt[:], AX_X, ALU.add))
                    routed(e.scalar_tensor_tensor(picked[:], rank[:], TOPK - 0.5, sc[:], ALU.is_lt, ALU.mult))
                    routed(e.tensor_reduce(sm[:], picked[:], AX_X, ALU.add))
                    routed(e.tensor_scalar(sm[:], sm[:], 1e-20, None, ALU.add))
                    routed(e.reciprocal(rs[:], sm[:]))
                    e.tensor_tensor(w[:], picked[:], bc(rs[:].unsqueeze(2), s3), ALU.mult).then_inc(s["w_ready"], 1)
                    e.wait_ge(s["wT_psum"], 1)
                    e.tensor_copy(wT[:], ps[6][0:NE, :]).then_inc(s["wT_ready"], 1)
                    for c in range(CHUNKS):
                        e.wait_ge(s["silu_ready"], c + 1)
                        e.wait_ge(s["up_psum"], c + 1)
                        i = e.tensor_tensor(prod[:, c], g[:, c % 2], ps[4 + c % 2][:], ALU.mult)
                        i.then_inc(s["up_read"], 1)
                        if c >= PAIRS:
                            e.wait_ge(s["up_read"], c + 1)
                            e.sem_inc(s["prod_ready"], 1)
                            continue
                        e.wait_ge(s["up_read"], c + 1)
                        e.wait_ge(s["spread_psum"], c + 1)
                        e.tensor_tensor(prod[:, c], prod[:, c], ps[0][:], ALU.mult).then_inc(s["prod_ready"], 1)
                        e.wait_ge(s["prod_ready"], c + 1)
                        e.sem_inc(s["spread_read"], 1)
                    vector_finish(e, s, nb, lambda t: ps[7][:, t * P:(t + 1) * P], xc, x_all, b)

                @block.gpsimd
                def _(e):
                    pool_rstd(e, s, nb, half)



KS = 64
CH = 64
NCH = L // CH
MLP1 = 512
TWO_PI_1, TWO_PI_2 = 6.28125, 0.0019350051879882812
TWO_PI_3 = 2 * np.pi - TWO_PI_1 - TWO_PI_2
ROUND = 1.5 * 2.0 ** 23


class Eigen:
    def __init__(self, sb):
        self.cos = sb("eig_cos", [P, CH])
        self.sin = sb("eig_sin", [P, CH])
        self.minus_sin = sb("eig_minus_sin", [P, CH])
        self.decay = sb("eig_decay", [P, NCH, CH])
        self.joined = sb("eig_joined", [P, D])


def eigen_tables_stage(nc, ps, W, C, eg):
    with ExitStack() as ctx:
        sbl = lambda n, shape: ctx.enter_context(nc.sbuf_tensor(n, shape, F32))
        ph, n_, r, sh, c2, s1 = (sbl(f"eigt_{k}", [P, CH]) for k in ("phase", "turns", "rest", "half", "sq", "sin"))
        mag, hold = sbl("eigt_mag", [P, 1]), sbl("eigt_hold", [P, CH])
        with stage(nc, "eigt", "vec mag_ready rest_ready sines_ready joined_psum") as (block, s):
            @block.tensor
            def _(e):
                e.matmul(ps[0][:, 0:D], W["L1_coupling"], W["L1_w_out"], start=True, stop=True).then_inc(s["joined_psum"], 1)

            @block.scalar
            def _(e):
                e.activation(mag[:], W["L1_log_decay"], ACT.Sigmoid).then_inc(s["mag_ready"], 1)
                e.wait_ge(s["rest_ready"], 1)
                e.activation(s1[:], r[:], ACT.Sin).then_inc(s["sines_ready"], 1)
                e.activation(sh[:], r[:], ACT.Sin, scale=0.5).then_inc(s["sines_ready"], 1)

            @block.vector
            def _(e):
                n = [0]

                def then(i):
                    n[0] += 1
                    i.then_inc(s["vec"], 1)
                    e.wait_ge(s["vec"], n[0])

                then(e.tensor_scalar(ph[:], C["steps"], W["L1_frequency"], None, ALU.mult))
                then(e.tensor_scalar(n_[:], ph[:], 1 / (2 * np.pi), ROUND, ALU.mult, ALU.add))
                then(e.tensor_scalar(n_[:], n_[:], -ROUND, None, ALU.add))
                then(e.scalar_tensor_tensor(r[:], n_[:], -TWO_PI_1, ph[:], ALU.mult, ALU.add))
                then(e.scalar_tensor_tensor(r[:], n_[:], -TWO_PI_2, r[:], ALU.mult, ALU.add))
                then(e.scalar_tensor_tensor(r[:], n_[:], -TWO_PI_3, r[:], ALU.mult, ALU.add))
                e.tensor_scalar(r[:], r[:], 3.1415925, -3.1415925, ALU.min, ALU.max).then_inc(s["rest_ready"], 1)
                e.wait_ge(s["joined_psum"], 1)
                e.tensor_copy(eg.joined[:], ps[0][:, 0:D])
                e.wait_ge(s["mag_ready"], 1)
                then(e.tensor_scalar(hold[:], C["not_first"], mag[:], None, ALU.mult))
                e.tensor_copy(eg.decay[:], hold[:].unsqueeze(1).to_broadcast([P, NCH, CH]))
                e.wait_ge(s["sines_ready"], 2)
                then(e.tensor_tensor(c2[:], sh[:], sh[:], ALU.mult))
                then(e.tensor_scalar(eg.cos[:], c2[:], -2.0, 1.0, ALU.mult, ALU.add))
                then(e.tensor_scalar(eg.sin[:], s1[:], C["half_sign"], None, ALU.mult))
                e.tensor_scalar(eg.minus_sin[:], eg.sin[:], -1.0, None, ALU.mult)


def eigen_stage(nc, ps, x_all, W, C, half, nb, xc, xT, eg):
    with ExitStack() as ctx:
        sbl = lambda n, shape: ctx.enter_context(nc.sbuf_tensor(n, shape, F32))
        xn = sbl("eig_xn", [P, NT, D])
        z, z2, dd = sbl("eig_z", [P, NCH, CH]), sbl("eig_z2", [P, NCH, CH]), sbl("eig_d", [P, NCH, CH])
        cc = sbl("eig_c", [P, L])
        gate = sbl("eig_gate", [P, NT, D])
        x1 = sbl("eig_x1", [P, NT, D])
        hid = sbl("eig_hid", [P, MLP1 // P, L])
        names = ("x_copied xn_ready xT_psum xT_ready beta_psum turned_in z_ready "
                 "c_whole d_ready swap2_psum c_half c_ready gate_psum gate_ready h_psum gated x1_ready "
                 "mlp_psum mlp_ready out_psum" + NORM_SIGNALS)
        wide = [P, NCH, CH]
        bc = lambda ap: ap.unsqueeze(1).to_broadcast(wide)
        chunked = lambda ap: ap.rearrange("p (n j) -> p n j", j=CH)
        HC = MLP1 // P
        with nc.Fori(0, B) as b:
            with stage(nc, "eig", names) as (block, s):
                @block.tensor
                def _(e):
                    e.wait_ge(s["xn_ready"], NT)
                    tensor_turn(e, lambda t: xn[:, t], ps[0], C["ident"], s["xT_psum"])
                    e.wait_ge(s["xT_ready"], 1)
                    e.matmul(ps[1][:], W["L1_w_in"], xT[:], start=True, stop=True).then_inc(s["beta_psum"], 1)
                    e.matmul(ps[2][:], W["L1_w_in_swapped"], xT[:], start=True, stop=True).then_inc(s["beta_psum"], 1)
                    for t in range(NT):
                        o = ps[3][:, t * P:(t + 1) * P]
                        e.matmul(o, C["ones"][0:1, :], W["L1_b_gate"][0:1, :], start=True, stop=False)
                        mm = e.matmul(o, xT[:, t * P:(t + 1) * P], W["L1_w_gate"], start=False, stop=True)
                    mm.then_inc(s["gate_psum"], 1)
                    e.wait_ge(s["d_ready"], 1)
                    e.matmul(ps[6][:], C["swap"], dd[:].rearrange("p n j -> p (n j)"), start=True,
                             stop=True).then_inc(s["swap2_psum"], 1)
                    e.wait_ge(s["c_ready"], 1)
                    for t in range(NT):
                        mm = e.matmul(ps[7][:, t * P:(t + 1) * P], cc[:, t * P:(t + 1) * P], eg.joined[:], start=True, stop=True)
                    mm.then_inc(s["h_psum"], 1)
                    e.wait_ge(s["xn_ready"], 2 * NT)
                    tensor_turn(e, lambda t: xn[:, t], ps[0], C["ident"], s["xT_psum"])
                    e.wait_ge(s["xT_ready"], 2)
                    for c in range(HC):
                        if c >= 2:
                            e.wait_ge(s["mlp_ready"], c - 1)
                        e.matmul(ps[1 + c % 2][:], W["L1_w_mlp1"][:, c * P:(c + 1) * P], xT[:], start=True,
                                 stop=True).then_inc(s["mlp_psum"], 1)
                    e.wait_ge(s["mlp_ready"], HC)
                    for t in range(NT):
                        o = ps[3][:, t * P:(t + 1) * P]
                        e.matmul(o, C["ones"][0:1, :], W["L1_b_mlp2"][0:1, :], start=True, stop=False)
                        for c in range(HC):
                            mm = e.matmul(o, hid[:, c, t * P:(t + 1) * P], W["L1_w_mlp2"][:, c * P:(c + 1) * P],
                                          start=False, stop=(c == HC - 1))
                    mm.then_inc(s["out_psum"], 1)

                @block.scalar
                def _(e):
                    for r in range(2):
                        ln = W[f"L1_ln{r + 1}"]
                        e.wait_ge(s["xT_psum"], r + 1)
                        e.activation(xT[:], ps[0][:], ACT.Identity, bias=ln[:, 1:2], scale=ln[:, 0:1]).then_inc(s["xT_ready"], 1)
                        if r == 0:
                            e.wait_ge(s["gate_psum"], 1)
                            e.activation(gate[:].rearrange("p t d -> p (t d)"), ps[3][:], ACT.Sigmoid).then_inc(s["gate_ready"], 1)
                    for c in range(HC):
                        e.wait_ge(s["mlp_psum"], c + 1)
                        e.activation(hid[:, c], ps[1 + c % 2][:], ACT.Silu, bias=W["L1_b_mlp1"][:, c:c + 1]).then_inc(s["mlp_ready"], 1)

                @block.vector
                def _(e):
                    vector_take(e, s, x_all, b, xc)
                    e.wait_ge(s["x_copied"], 1)
                    e.sem_inc(s["sum_ready"], NT)
                    vector_moments(e, s, nb, lambda t: xc[:, t])
                    vector_normalize(e, s, nb, lambda t: xc[:, t], lambda t: xn[:, t], signal="xn_ready")
                    e.wait_ge(s["beta_psum"], 1)
                    e.tensor_tensor(z[:], chunked(ps[1][:]), bc(eg.cos[:]), ALU.mult).then_inc(s["turned_in"], 1)
                    e.wait_ge(s["beta_psum"], 2)
                    e.tensor_tensor(z2[:], chunked(ps[2][:]), bc(eg.minus_sin[:]), ALU.mult).then_inc(s["turned_in"], 1)
                    e.wait_ge(s["turned_in"], 2)
                    e.tensor_tensor(z[:], z[:], z2[:], ALU.add).then_inc(s["z_ready"], 1)
                    flat = lambda x: x[:].rearrange("p n j -> p (n j)")
                    e.wait_ge(s["z_ready"], 1)
                    e.tensor_tensor_scan(flat(dd)[:, ::-1], flat(eg.decay), flat(z)[:, ::-1], 0.0, ALU.mult,
                                         ALU.add).then_inc(s["d_ready"], 1)
                    e.wait_ge(s["d_ready"], 1)
                    e.tensor_tensor(z[:], dd[:], bc(eg.cos[:]), ALU.mult).then_inc(s["c_half"], 1)
                    e.wait_ge(s["swap2_psum"], 1)
                    e.tensor_tensor(z2[:], chunked(ps[6][:]), bc(eg.sin[:]), ALU.mult).then_inc(s["c_half"], 1)
                    e.wait_ge(s["c_half"], 2)
                    e.tensor_tensor(cc[:], flat(z), flat(z2), ALU.add).then_inc(s["c_whole"], 1)
                    e.wait_ge(s["c_whole"], 1)
                    first = cc[:].rearrange("p (n j) -> p n j", j=CH)[:, 1:, 0]
                    e.tensor_tensor(first, chunked(ps[1][:])[:, 0:NCH - 1, CH - 1], first, ALU.add).then_inc(s["c_ready"], 1)
                    e.wait_ge(s["h_psum"], 1)
                    e.wait_ge(s["gate_ready"], 1)
                    e.tensor_tensor(gate[:].rearrange("p t d -> p (t d)"), gate[:].rearrange("p t d -> p (t d)"), ps[7][:],
                                    ALU.mult).then_inc(s["gated"], 1)
                    e.wait_ge(s["gated"], 1)
                    e.tensor_tensor(x1[:], gate[:], xc[:], ALU.add).then_inc(s["x1_ready"], 1)
                    e.wait_ge(s["x1_ready"], 1)
                    e.sem_inc(s["sum_ready"], NT)
                    vector_moments(e, s, nb, lambda t: x1[:, t], round_=1)
                    e.wait_ge(s["xT_psum"], 1)
                    vector_normalize(e, s, nb, lambda t: x1[:, t], lambda t: xn[:, t], round_=1, signal="xn_ready")
                    e.wait_ge(s["xn_ready"], 2 * NT)
                    e.tensor_tensor(x1[:], x1[:], xc[:], ALU.add).then_inc(s["x1_ready"], 1)
                    e.wait_ge(s["x1_ready"], 2)
                    e.wait_ge(s["out_psum"], 1)
                    for t in range(NT):
                        e.tensor_tensor(nb.r[:, t], ps[3][:, t * P:(t + 1) * P], x1[:, t], ALU.add).then_inc(s["sum_ready"], 1)
                    vector_moments(e, s, nb, lambda t: nb.r[:, t], round_=2)
                    vector_normalize(e, s, nb, lambda t: nb.r[:, t], lambda t: x_all[:, ds(NT * b + t, 1), :], round_=2)

                @block.gpsimd
                def _(e):
                    for r in range(3):
                        pool_rstd(e, s, nb, half, round_=r)



HID3 = 512
TERNARY_EPS = 1e-6


def ternary_weights_stage(nc, ps, W, C):
    names = ("L1f_W_fc", "L1f_W_proj")
    with ExitStack() as ctx:
        sbl = lambda n, shape: ctx.enter_context(nc.sbuf_tensor(n, shape, F32))
        part = sbl("ter_part", [P, 2, 4])
        gamma, rg = sbl("ter_gamma", [P, 2]), sbl("ter_rgamma", [P, 2])
        above, below = sbl("ter_above", [P, HID3]), sbl("ter_below", [P, HID3])
        with stage(nc, "ter", "vec parts_ready total_psum") as (block, s):
            @block.tensor
            def _(e):
                e.wait_ge(s["parts_ready"], 2)
                e.matmul(ps[0][:, 0:8], C["ones"], part[:].rearrange("p a b -> p (a b)"), start=True,
                         stop=True).then_inc(s["total_psum"], 1)

            @block.vector
            def _(e):
                n = [0]

                def then(i):
                    n[0] += 1
                    i.then_inc(s["vec"], 1)
                    e.wait_ge(s["vec"], n[0])

                for i, w in enumerate(names):
                    e.tensor_reduce(part[:, i], W[w].rearrange("p (a b) -> p a b", a=4), AX_X, ALU.add,
                                    apply_absolute_value=True).then_inc(s["parts_ready"], 1)
                e.wait_ge(s["total_psum"], 1)
                then(e.tensor_reduce(gamma[:], ps[0][:, 0:8].rearrange("p (a b) -> p a b", a=2), AX_X, ALU.add))
                then(e.tensor_scalar(gamma[:], gamma[:], 1.0 / (D * HID3), TERNARY_EPS, ALU.mult, ALU.add))
                then(e.reciprocal(rg[:], gamma[:]))
                for i, w in enumerate(names):
                    then(e.tensor_scalar(above[:], W[w], rg[:, i:i + 1], 0.5, ALU.mult, ALU.is_gt))
                    then(e.tensor_scalar(below[:], W[w], rg[:, i:i + 1], -0.5, ALU.mult, ALU.is_lt))
                    then(e.tensor_tensor(W[w], above[:], below[:], ALU.subtract))


def ternary_stage(nc, ps, x_all, W, C, half, nb, xc, xT):
    HC = HID3 // P
    with ExitStack() as ctx:
        sbl = lambda n, shape: ctx.enter_context(nc.sbuf_tensor(n, shape, F32))
        h = sbl("ter_h", [P, NT, HID3])
        hT = sbl("ter_hT", [P, HC, L])
        names = "h_psum gelu_ready h_normed hT_psum hT_ready" + BATCH_SIGNALS
        with nc.Fori(0, B) as b:
            with stage(nc, "tern", names) as (block, s):
                @block.tensor
                def _(e):
                    e.wait_ge(s["x_copied"], 1)
                    tensor_turn(e, lambda t: xc[:, t], ps[0], C["ident"], s["xT_psum"])
                    e.wait_ge(s["xT_ready"], 1)
                    for t in range(NT):
                        e.matmul(ps[1 + t][:], xT[:, t * P:(t + 1) * P], W["L1f_W_fc"], start=True,
                                 stop=True).then_inc(s["h_psum"], 1)
                    e.wait_ge(s["h_normed"], NT)
                    for c in range(HC):
                        if c >= 2:
                            e.wait_ge(s["hT_ready"], c - 1)
                        tensor_turn(e, lambda t: h[:, t, c * P:(c + 1) * P], ps[5 + c % 2], C["ident"], s["hT_psum"])
                    e.wait_ge(s["hT_ready"], HC)
                    for t in range(NT):
                        for c in range(HC):
                            mm = e.matmul(ps[7][:, t * P:(t + 1) * P], hT[:, c, t * P:(t + 1) * P],
                                          W["L1f_W_proj"][:, c * P:(c + 1) * P], start=(c == 0), stop=(c == HC - 1))
                    mm.then_inc(s["out_psum"], 1)

                @block.scalar
                def _(e):
                    e.wait_ge(s["xT_psum"], 1)
                    e.activation(xT[:], ps[0][:], ACT.Copy).then_inc(s["xT_ready"], 1)
                    for t in range(NT):
                        e.wait_ge(s["h_psum"], t + 1)
                        e.activation(h[:, t], ps[1 + t][:], ACT.Gelu).then_inc(s["sum_ready"], 1)
                    for c in range(HC):
                        e.wait_ge(s["hT_psum"], c + 1)
                        e.activation(hT[:, c], ps[5 + c % 2][:], ACT.Identity, bias=W["L1f_ln_b"][:, c:c + 1],
                                     scale=W["L1f_ln_w"][:, c:c + 1]).then_inc(s["hT_ready"], 1)

                @block.vector
                def _(e):
                    vector_take(e, s, x_all, b, xc)
                    vector_moments(e, s, nb, lambda t: h[:, t])
                    vector_normalize(e, s, nb, lambda t: h[:, t], lambda t: h[:, t], signal="h_normed")
                    e.wait_ge(s["out_psum"], 1)
                    for t in range(NT):
                        e.tensor_tensor(nb.r[:, t], ps[7][:, t * P:(t + 1) * P], xc[:, t], ALU.add).then_inc(s["sum_ready"], 1)
                    e.wait_ge(s["h_normed"], NT)
                    vector_moments(e, s, nb, lambda t: nb.r[:, t], round_=1)
                    vector_normalize(e, s, nb, lambda t: nb.r[:, t], lambda t: x_all[:, ds(NT * b + t, 1), :], round_=1)

                @block.gpsimd
                def _(e):
                    pool_rstd(e, s, nb, half)
                    pool_rstd(e, s, nb, half, round_=1)



H4, DK4 = 16, 64
PAIRS4 = H4 // 2
SCALE4 = DK4 ** -0.5


def causal_stage(nc, ps, x_all, W, C, half, nb, xc, xT, ident_bf, mask_bf):
    UNITS = [(qt, h) for qt in range(NT) for h in range(H4)]
    NU = len(UNITS)
    with ExitStack() as ctx:
        sbl = lambda n, shape: ctx.enter_context(nc.sbuf_tensor(n, shape, F32))
        qT, kT = sbl("att_qT", [P, PAIRS4, L]), sbl("att_kT", [P, PAIRS4, L])
        v = sbl("att_v", [P, NT, H4 * DK4])
        straight, turned = sbl("att_straight", [P, 2, L]), sbl("att_turned", [P, 2, L])
        mx, nmx, sm, rs = (sbl(f"att_{k}", [P, NT * H4]) for k in ("max", "minus_max", "sum", "rsum"))
        prob, probT = sbl("att_prob", [P, 3, L]), sbl("att_probT", [P, 3, NT, P])
        o, oT = sbl("att_o", [P, NT, H4 * DK4]), sbl("att_oT", [P, PAIRS4, L])
        names = ("proj_psum straight_ready turned_ready rope_ready v_psum v_ready s_psum max_ready bias_ready prob_ready "
                 "probT_psum probT_ready pv_psum rsum_ready o_ready oT_psum oT_ready" + BATCH_SIGNALS)
        with nc.Fori(0, B) as b:
            with stage(nc, "att", names) as (block, s):
                S = lambda u: ps[1 + u % 4]
                T = lambda u: ps[5 + u % 2]
                O = lambda h: (ps[7] if h < H4 // 2 else ps[0])[:, (h % 8) * DK4:(h % 8 + 1) * DK4]

                @block.tensor
                def _(e):
                    e.wait_ge(s["x_copied"], 1)
                    tensor_turn(e, lambda t: xc[:, t], ps[0], C["ident"], s["xT_psum"])
                    e.wait_ge(s["xT_ready"], 1)
                    for c in range(2 * PAIRS4):
                        w = "q" if c < PAIRS4 else "k"
                        cc = slice((c % PAIRS4) * P, (c % PAIRS4 + 1) * P)
                        if c >= 2:
                            e.wait_ge(s["straight_ready"], c - 1)
                            e.wait_ge(s["turned_ready"], c - 1)
                        e.matmul(ps[1 + 2 * (c % 2)][:], W[f"L2_w{w}"][:, cc], xT[:], start=True, stop=True).then_inc(s["proj_psum"], 1)
                        e.matmul(ps[2 + 2 * (c % 2)][:], W[f"L2_w{w}_turned"][:, cc], xT[:], start=True, stop=True).then_inc(s["proj_psum"], 1)
                    for i in range(2 * NT):
                        t, hf = divmod(i, 2)
                        if i >= 2:
                            e.wait_ge(s["v_ready"], i - 1)
                        cc = slice(512 * hf, 512 * (hf + 1))
                        e.matmul(ps[5 + i % 2][:], C["ones"][0:1, :], W["L2_bv"][0:1, cc], start=True, stop=False)
                        e.matmul(ps[5 + i % 2][:], xT[:, t * P:(t + 1) * P], W["L2_wv"][:, cc], start=False,
                                 stop=True).then_inc(s["v_psum"], 1)
                    e.wait_ge(s["rope_ready"], 2 * PAIRS4)
                    e.wait_ge(s["v_ready"], 2 * NT)
                    for u in range(NU + 3):
                        if u < NU:
                            qt, h = UNITS[u]
                            if u >= 4:
                                e.wait_ge(s["prob_ready"], u - 3)
                            r = slice(DK4 * (h % 2), DK4 * (h % 2 + 1))
                            e.matmul(S(u)[:, 0:(qt + 1) * P], qT[r, h // 2, qt * P:(qt + 1) * P], kT[r, h // 2, 0:(qt + 1) * P],
                                     start=True, stop=False, skip_group_check=True)
                            e.matmul(S(u)[:, qt * P:(qt + 1) * P], ident_bf[:], mask_bf[:], start=False, stop=True,
                                     skip_group_check=True).then_inc(s["s_psum"], 1)
                        if 2 <= u < NU + 2:
                            qt, h = UNITS[u - 2]
                            e.wait_ge(s["prob_ready"], u - 1)
                            if u >= 4:
                                e.wait_ge(s["probT_ready"], u - 3)
                            for k in range(qt + 1):
                                mm = e.transpose(T(u - 2)[:, k * P:(k + 1) * P], prob[:, (u - 2) % 3, k * P:(k + 1) * P], C["ident"])
                            mm.then_inc(s["probT_psum"], 1)
                        if u >= 3:
                            qt, h = UNITS[u - 3]
                            e.wait_ge(s["probT_ready"], u - 2)
                            if h % (H4 // 2) == 0 and qt >= 1:
                                e.wait_ge(s["o_ready"], 2 * (qt - 1) + 1 + h // (H4 // 2))
                            for k in range(qt + 1):
                                mm = e.matmul(O(h), probT[:, (u - 3) % 3, k], v[:, k, h * DK4:(h + 1) * DK4],
                                              start=(k == 0), stop=(k == qt))
                            mm.then_inc(s["pv_psum"], 1)
                    e.wait_ge(s["o_ready"], 2 * NT)
                    for c in range(PAIRS4):
                        if c >= 2:
                            e.wait_ge(s["oT_ready"], c - 1)
                        tensor_turn(e, lambda t: o[:, t, c * P:(c + 1) * P], ps[5 + c % 2], C["ident"], s["oT_psum"])
                    e.wait_ge(s["oT_ready"], PAIRS4)
                    for t in range(NT):
                        y = ps[1][:, t * P:(t + 1) * P]
                        e.matmul(y, C["ones"][0:1, :], W["L2_bo"][0:1, :], start=True, stop=False)
                        for c in range(PAIRS4):
                            mm = e.matmul(y, oT[:, c, t * P:(t + 1) * P], W["L2_wo"][:, c * P:(c + 1) * P], start=False,
                                          stop=(c == PAIRS4 - 1))
                    mm.then_inc(s["out_psum"], 1)

                @block.scalar
                def _(e):
                    e.wait_ge(s["xT_psum"], 1)
                    e.activation(xT[:], ps[0][:], ACT.Copy).then_inc(s["xT_ready"], 1)
                    for i in range(2 * NT):
                        t, hf = divmod(i, 2)
                        e.wait_ge(s["v_psum"], i + 1)
                        e.activation(v[:, t, 512 * hf:512 * (hf + 1)], ps[5 + i % 2][:], ACT.Copy).then_inc(s["v_ready"], 1)
                    for u, (qt, h) in enumerate(UNITS):
                        e.wait_ge(s["bias_ready"], u + 1)
                        if u >= 3:
                            e.wait_ge(s["probT_psum"], u - 2)
                        e.activation(prob[:, u % 3, 0:(qt + 1) * P], S(u)[:, 0:(qt + 1) * P], ACT.Exp, bias=nmx[:, u:u + 1],
                                     scale=SCALE4, accum_out=sm[:, u:u + 1]).then_inc(s["prob_ready"], 1)
                    for c in range(PAIRS4):
                        e.wait_ge(s["oT_psum"], c + 1)
                        e.activation(oT[:, c], ps[5 + c % 2][:], ACT.Copy).then_inc(s["oT_ready"], 1)

                @block.vector
                def _(e):
                    vector_take(e, s, x_all, b, xc)
                    for c in range(2 * PAIRS4):
                        w = "q" if c < PAIRS4 else "k"
                        bias, bias_turned = W[f"L2_b{w}"], W[f"L2_b{w}_turned"]
                        i = c % PAIRS4
                        if c >= 2:
                            e.wait_ge(s["rope_ready"], c - 1)
                        e.wait_ge(s["proj_psum"], 2 * c + 1)
                        e.scalar_tensor_tensor(straight[:, c % 2], ps[1 + 2 * (c % 2)][:], bias[:, i:i + 1], C["rope4_cos"],
                                               ALU.add, ALU.mult).then_inc(s["straight_ready"], 1)
                        e.wait_ge(s["proj_psum"], 2 * c + 2)
                        e.scalar_tensor_tensor(turned[:, c % 2], ps[2 + 2 * (c % 2)][:], bias_turned[:, i:i + 1], C["rope4_sin"],
                                               ALU.add, ALU.mult).then_inc(s["turned_ready"], 1)
                    for u in range(NU + 3):
                        if u < NU:
                            qt, h = UNITS[u]
                            e.wait_ge(s["s_psum"], u + 1)
                            e.tensor_reduce(mx[:, u:u + 1], S(u)[:, 0:(qt + 1) * P], AX_X, ALU.max).then_inc(s["max_ready"], 1)
                            e.wait_ge(s["max_ready"], u + 1)
                            e.tensor_scalar(nmx[:, u:u + 1], mx[:, u:u + 1], -SCALE4, None, ALU.mult).then_inc(s["bias_ready"], 1)
                        if 2 <= u < NU + 2:
                            qt, h = UNITS[u - 2]
                            e.wait_ge(s["probT_psum"], u - 1)
                            if u >= 5:
                                e.wait_ge(s["pv_psum"], u - 4)
                            e.tensor_copy(probT[:, (u - 2) % 3, 0:qt + 1].rearrange("p k q -> p (k q)"),
                                          T(u - 2)[:, 0:(qt + 1) * P]).then_inc(s["probT_ready"], 1)
                        if u >= 3 and u % (H4 // 2) == 2:
                            j = (u - 2) // (H4 // 2) - 1
                            qt, hf = divmod(j, 2)
                            cols = slice(8 * j, 8 * j + 8)
                            e.wait_ge(s["prob_ready"], 8 * (j + 1))
                            e.reciprocal(rs[:, cols], sm[:, cols]).then_inc(s["rsum_ready"], 1)
                            e.wait_ge(s["rsum_ready"], j + 1)
                            e.wait_ge(s["pv_psum"], 8 * (j + 1))
                            e.tensor_tensor(o[:, qt, 512 * hf:512 * (hf + 1)].rearrange("p (h d) -> p h d", d=DK4),
                                            (ps[0] if hf else ps[7])[:].rearrange("p (h d) -> p h d", d=DK4),
                                            rs[:, cols].unsqueeze(2).to_broadcast([P, 8, DK4]), ALU.mult).then_inc(s["o_ready"], 1)
                    vector_finish(e, s, nb, lambda t: ps[1][:, t * P:(t + 1) * P], xc, x_all, b)

                @block.gpsimd
                def _(e):
                    for c in range(2 * PAIRS4):
                        out = (qT if c < PAIRS4 else kT)[:, c % PAIRS4]
                        e.wait_ge(s["straight_ready"], c + 1)
                        e.wait_ge(s["turned_ready"], c + 1)
                        e.tensor_tensor(out, straight[:, c % 2], turned[:, c % 2], ALU.add).then_inc(s["rope_ready"], 1)
                    pool_rstd(e, s, nb, half)



HID5 = 512


def relu_stage(nc, ps, x_all, W, C, half, nb, xc, xT):
    HC = HID5 // P
    with ExitStack() as ctx:
        hT = ctx.enter_context(nc.sbuf_tensor("mlp_hT", [P, HC, L], F32))
        names = "h_psum h_ready" + BATCH_SIGNALS
        with nc.Fori(0, B) as b:
            with stage(nc, "mlp", names) as (block, s):
                @block.tensor
                def _(e):
                    e.wait_ge(s["x_copied"], 1)
                    tensor_turn(e, lambda t: xc[:, t], ps[0], C["ident"], s["xT_psum"])
                    e.wait_ge(s["xT_ready"], 1)
                    for c in range(HC):
                        e.matmul(ps[1 + c][:], W["L2f_W1"][:, c * P:(c + 1) * P], xT[:], start=True,
                                 stop=True).then_inc(s["h_psum"], 1)
                    e.wait_ge(s["h_ready"], HC)
                    for t in range(NT):
                        y = ps[7][:, t * P:(t + 1) * P]
                        e.matmul(y, C["ones"][0:1, :], W["L2f_b2"][0:1, :], start=True, stop=False)
                        for c in range(HC):
                            mm = e.matmul(y, hT[:, c, t * P:(t + 1) * P], W["L2f_W2"][:, c * P:(c + 1) * P], start=False,
                                          stop=(c == HC - 1))
                    mm.then_inc(s["out_psum"], 1)

                @block.scalar
                def _(e):
                    e.wait_ge(s["xT_psum"], 1)
                    e.activation(xT[:], ps[0][:], ACT.Copy).then_inc(s["xT_ready"], 1)
                    for c in range(HC):
                        e.wait_ge(s["h_psum"], c + 1)
                        e.activation(hT[:, c], ps[1 + c][:], ACT.Relu, bias=W["L2f_b1"][:, c:c + 1]).then_inc(s["h_ready"], 1)

                @block.vector
                def _(e):
                    vector_take(e, s, x_all, b, xc)
                    vector_finish(e, s, nb, lambda t: ps[7][:, t * P:(t + 1) * P], xc, x_all, b)

                @block.gpsimd
                def _(e):
                    pool_rstd(e, s, nb, half)



H6, DH6, M6 = 16, 8, 16
DN6 = DH6 ** -0.25
RATIO6 = M6 ** -0.5
EPS6 = 1e-4
FEATS = H6 * M6


def features_stage(nc, ps, x_all, W, C, half, nb, xc, xT):
    HF = FEATS // P
    with ExitStack() as ctx:
        sbl = lambda n, shape: ctx.enter_context(nc.sbuf_tensor(n, shape, F32))
        t_, sq = sbl("rf_t", [P, 2, L]), sbl("rf_sq", [P, 2, L])
        v1 = sbl("rf_v", [P, NT, D + 1])
        dg = sbl("rf_diag", [P, 2, NT * H6])
        mx = sbl("rf_max", [P, 2, NT * H6])
        kmx, kall, kdiag, kmax = sbl("rf_kmax_tok", [P, H6]), sbl("rf_kmax_h", [H6, 1]), sbl("rf_kmax_d", [H6, H6]), sbl("rf_kmax", [P, NT, H6])
        f = sbl("rf_f", [P, 2, NT, FEATS])
        fT = sbl("rf_fT", [P, HF, L])
        bd = sbl("rf_context", [P, HF, D + H6])
        den = sbl("rf_den", [P, NT, H6])
        o, oT, hT = sbl("rf_o", [P, NT, D]), sbl("rf_oT", [P, L]), sbl("rf_hT", [P, L])
        names = ("proj_psum t_ready sq_ready v_psum v_ready one_ready td_psum diag_psum diag_ready max_ready less_diag "
                 "less_max exp_ready f_ready ktok_ready kT_psum kall_ready kdiag_ready kmax_psum kmax_ready context_psum "
                 "context_ready fT_psum fT_ready ratio_psum den_ready o_ready oT_psum oT_ready h_psum hT_ready"
                 + BATCH_SIGNALS)
        heads = lambda ap: ap.rearrange("p (g m) -> p g m", m=M6)
        wide = [P, 2 * H6, M6]
        WK = D + H6
        with nc.Fori(0, B) as b:
            with stage(nc, "rf", names) as (block, s):
                td = lambda w, j: ps[4 + 2 * w + j]

                @block.tensor
                def _(e):
                    e.wait_ge(s["x_copied"], 1)
                    tensor_turn(e, lambda t: xc[:, t], ps[0], C["ident"], s["xT_psum"])
                    e.wait_ge(s["xT_ready"], 1)
                    e.matmul(ps[1][:], W["L3_Wq"], xT[:], start=True, stop=True).then_inc(s["proj_psum"], 1)
                    e.matmul(ps[2][:], W["L3_Wk"], xT[:], start=True, stop=True).then_inc(s["proj_psum"], 1)
                    for t in range(NT):
                        y = ps[3][:, t * P:(t + 1) * P]
                        e.matmul(y, C["ones"][0:1, :], W["L3_bv"][0:1, :], start=True, stop=False)
                        mm = e.matmul(y, xT[:, t * P:(t + 1) * P], W["L3_Wv"], start=False, stop=True)
                    mm.then_inc(s["v_psum"], 1)
                    for w in (1, 0):
                        e.wait_ge(s["t_ready"], 2 if w == 0 else 1)
                        for t in range(NT):
                            mm = e.matmul(td(w, t // 2)[:, (t % 2) * FEATS:(t % 2 + 1) * FEATS], t_[:, w, t * P:(t + 1) * P],
                                          W["L3_proj"], start=True, stop=True)
                        mm.then_inc(s["td_psum"], 1)
                        e.wait_ge(s["sq_ready"], 2 if w == 0 else 1)
                        for t in range(NT):
                            mm = e.matmul(ps[0][:, (w * NT + t) * H6:(w * NT + t + 1) * H6], sq[:, w, t * P:(t + 1) * P],
                                          C["head_of_feature"], start=True, stop=True)
                        mm.then_inc(s["diag_psum"], 1)
                    e.wait_ge(s["ktok_ready"], 1)
                    e.transpose(ps[1][0:H6, 0:P], kmx[:], C["ident"]).then_inc(s["kT_psum"], 1)
                    e.wait_ge(s["kdiag_ready"], 1)
                    e.matmul(ps[1][:, P:P + H6], C["ones"][0:H6, :], kdiag[:], start=True, stop=True).then_inc(s["kmax_psum"], 1)
                    e.wait_ge(s["v_ready"], 1)
                    e.wait_ge(s["one_ready"], 1)
                    e.wait_ge(s["f_ready"], 4)
                    for m in range(HF):
                        for t in range(NT):
                            mm = e.matmul(ps[2 + m][:, 0:D + 1], f[:, 1, t, m * P:(m + 1) * P], v1[:, t], start=(t == 0),
                                          stop=(t == NT - 1))
                        mm.then_inc(s["context_psum"], 1)
                    for m in range(HF):
                        tensor_turn(e, lambda t: f[:, 0, t, m * P:(m + 1) * P], ps[4 + m], C["ident"], s["fT_psum"])
                    e.wait_ge(s["fT_ready"], HF)
                    e.wait_ge(s["context_ready"], 2 * HF)
                    for t in range(NT):
                        for m in range(HF):
                            mm = e.matmul(ps[6 + t // 2][:, (t % 2) * WK:(t % 2 + 1) * WK], fT[:, m, t * P:(t + 1) * P], bd[:, m],
                                          start=(m == 0), stop=(m == HF - 1))
                    mm.then_inc(s["ratio_psum"], 1)
                    e.wait_ge(s["o_ready"], 2)
                    tensor_turn(e, lambda t: o[:, t], ps[0], C["ident"], s["oT_psum"])
                    e.wait_ge(s["oT_ready"], 1)
                    e.matmul(ps[1][:], W["L3_Wo"], oT[:], start=True, stop=True).then_inc(s["h_psum"], 1)
                    e.wait_ge(s["hT_ready"], 1)
                    for t in range(NT):
                        y = ps[2][:, t * P:(t + 1) * P]
                        e.matmul(y, C["ones"][0:1, :], W["L3_bfc"][0:1, :], start=True, stop=False)
                        mm = e.matmul(y, hT[:, t * P:(t + 1) * P], W["L3_Wfc"], start=False, stop=True)
                    mm.then_inc(s["out_psum"], 1)

                @block.scalar
                def _(e):
                    e.wait_ge(s["xT_psum"], 1)
                    e.activation(xT[:], ps[0][:], ACT.Copy).then_inc(s["xT_ready"], 1)
                    for n, w in enumerate((1, 0)):
                        e.wait_ge(s["t_ready"], n + 1)
                        e.activation(sq[:, w], t_[:, w], ACT.Square).then_inc(s["sq_ready"], 1)
                    e.wait_ge(s["v_psum"], 1)
                    e.activation(v1[:, :, 0:D], ps[3][:].rearrange("p (t d) -> p t d", d=D), ACT.Copy).then_inc(s["v_ready"], 1)
                    for n in range(4):
                        w, j = (0, n) if n < 2 else (1, n - 2)
                        e.wait_ge(s["less_max"], n + 1)
                        x = f[:, w, 2 * j:2 * j + 2]
                        e.activation(x, x, ACT.Exp).then_inc(s["exp_ready"], 1)
                    for m in range(HF):
                        e.wait_ge(s["fT_psum"], m + 1)
                        e.activation(fT[:, m], ps[4 + m][:], ACT.Copy).then_inc(s["fT_ready"], 1)
                    e.wait_ge(s["oT_psum"], 1)
                    e.activation(oT[:], ps[0][:], ACT.Copy).then_inc(s["oT_ready"], 1)
                    e.wait_ge(s["h_psum"], 1)
                    e.activation(hT[:], ps[1][:], ACT.Identity, bias=W["L3_bo"]).then_inc(s["hT_ready"], 1)

                @block.vector
                def _(e):
                    vector_take(e, s, x_all, b, xc)
                    e.memset(v1[:, :, D:], 1.0).then_inc(s["one_ready"], 1)
                    e.wait_ge(s["proj_psum"], 2)
                    for w, name in ((1, "k"), (0, "q")):
                        e.tensor_scalar(t_[:, w], ps[1 + w][:], W[f"L3_b{name}"], DN6, ALU.add, ALU.mult).then_inc(s["t_ready"], 1)
                    for n, w in enumerate((1, 0)):
                        e.wait_ge(s["diag_psum"], 2)
                        e.tensor_scalar(dg[:, w], ps[0][:, w * NT * H6:(w + 1) * NT * H6], 0.5, None,
                                        ALU.mult).then_inc(s["diag_ready"], 1)
                        for j in range(2):
                            e.tensor_reduce(mx[:, w, 2 * H6 * j:2 * H6 * (j + 1)], heads(td(w, j)[:]), AX_X,
                                            ALU.max).then_inc(s["max_ready"], 1)
                        if w == 1:
                            e.wait_ge(s["max_ready"], 2)
                            e.tensor_reduce(kmx[:], mx[:, 1].rearrange("p (t h) -> p h t", h=H6), AX_X,
                                            ALU.max).then_inc(s["ktok_ready"], 1)
                            e.wait_ge(s["kT_psum"], 1)
                            e.tensor_reduce(kall[:], ps[1][0:H6, 0:P], AX_X, ALU.max).then_inc(s["kall_ready"], 1)
                            e.wait_ge(s["kall_ready"], 1)
                            e.tensor_scalar(kdiag[:], C["ident"][0:H6, 0:H6], kall[:], None, ALU.mult).then_inc(s["kdiag_ready"], 1)
                            e.wait_ge(s["kmax_psum"], 1)
                            e.tensor_copy(kmax[:], ps[1][:, P:P + H6].unsqueeze(1).to_broadcast([P, NT, H6])).then_inc(s["kmax_ready"], 1)
                    e.wait_ge(s["diag_ready"], 2)
                    e.wait_ge(s["max_ready"], 4)
                    e.wait_ge(s["kmax_ready"], 1)
                    for n in range(4):
                        w, j = (0, n) if n < 2 else (1, n - 2)
                        x = f[:, w, 2 * j:2 * j + 2].rearrange("p t (h m) -> p (t h) m", m=M6)
                        cols = slice(2 * H6 * j, 2 * H6 * (j + 1))
                        most = mx[:, 0, cols] if w == 0 else kmax[:].rearrange("p t h -> p (t h)")[:, cols]
                        e.tensor_tensor(x, heads(td(w, j)[:]), dg[:, w, cols].unsqueeze(2).to_broadcast(wide),
                                        ALU.subtract).then_inc(s["less_diag"], 1)
                        e.wait_ge(s["less_diag"], n + 1)
                        e.tensor_tensor(x, x, most.unsqueeze(2).to_broadcast(wide), ALU.subtract).then_inc(s["less_max"], 1)
                    for n in range(4):
                        w, j = (0, n) if n < 2 else (1, n - 2)
                        x = f[:, w, 2 * j:2 * j + 2]
                        e.wait_ge(s["exp_ready"], n + 1)
                        e.tensor_scalar(x, x, EPS6, RATIO6, ALU.add, ALU.mult).then_inc(s["f_ready"], 1)
                    for m in range(HF):
                        e.wait_ge(s["context_psum"], m + 1)
                        own = C["own_columns"][:, m * WK:(m + 1) * WK]
                        e.tensor_tensor(bd[:, m, 0:D], ps[2 + m][:, 0:D], own[:, 0:D], ALU.mult).then_inc(s["context_ready"], 1)
                        e.tensor_scalar(bd[:, m, D:], own[:, D:], ps[2 + m][:, D:D + 1], None, ALU.mult).then_inc(s["context_ready"], 1)
                    e.wait_ge(s["ratio_psum"], 1)
                    for j in range(2):
                        r = ps[6 + j][:, 0:2 * WK].rearrange("p (t k) -> p t k", k=WK)
                        e.reciprocal(den[:, 2 * j:2 * j + 2], r[:, :, D:]).then_inc(s["den_ready"], 1)
                    for j in range(2):
                        r = ps[6 + j][:, 0:2 * WK].rearrange("p (t k) -> p t k", k=WK)
                        e.wait_ge(s["den_ready"], j + 1)
                        for t in range(2):
                            i = e.tensor_tensor(o[:, 2 * j + t].rearrange("p (h d) -> p h d", d=DH6),
                                                r[:, t, 0:D].rearrange("p (h d) -> p h d", d=DH6),
                                                den[:, 2 * j + t].unsqueeze(2).to_broadcast([P, H6, DH6]), ALU.mult)
                        i.then_inc(s["o_ready"], 1)
                    e.wait_ge(s["out_psum"], 1)
                    for t in range(NT):
                        e.scalar_tensor_tensor(nb.r[:, t], ps[2][:, t * P:(t + 1) * P], 0.0, xc[:, t], ALU.max,
                                               ALU.add).then_inc(s["sum_ready"], 1)
                    vector_moments(e, s, nb, lambda t: nb.r[:, t])
                    vector_normalize(e, s, nb, lambda t: nb.r[:, t], lambda t: x_all[:, ds(NT * b + t, 1), :])

                @block.gpsimd
                def _(e):
                    pool_rstd(e, s, nb, half)



DEPTH = 6
H7, DK7 = 16, 64
INNER7 = H7 * DK7
PAIRS7 = H7 // 2
WIN = 32
SPAN = WIN + P
HALF = D // 2
QK_SCALE = 8.0
GROUP = 4
NG = H7 // GROUP
HID7 = 384
LAYER_COLUMNS = (("qkv", 3 * INNER7), ("wo", PAIRS7 * D), ("w1", 2 * HID7), ("w2", HID7), ("b1", 2 * HID7 // P),
                 ("ln", 2), ("b2", D), ("q_scale", DK7), ("q_scale_rolled", DK7), ("k_scale", DK7), ("k_scale_rolled", DK7))


class LayerBuffers:
    def __init__(self, nc, ctx):
        sbl = lambda n, shape, dtype=F32: ctx.enter_context(nc.sbuf_tensor(n, shape, dtype))
        width = sum(w for _, w in LAYER_COLUMNS)
        self.weights = [sbl(f"lay_weights{i}", [P, width]) for i in range(2)]
        self.at, o = {}, 0
        for n, w in LAYER_COLUMNS:
            self.at[n] = slice(o, o + w)
            o += w
        self.table = sbl("lay_table", [P, 4, NT, DK7])
        self.raw = sbl("lay_raw", [P, 2 * INNER7])
        self.sq = sbl("lay_sq", [P, 2 * INNER7])
        self.part = sbl("lay_turned", [P, 2 * INNER7])
        self.qk = sbl("lay_qk", [P, 2 * INNER7])
        self.v = sbl("lay_v", [P, 3, INNER7])
        self.o = sbl("lay_o", [P, 2, INNER7])
        self.oT = sbl("lay_oT", [P, PAIRS7, P])
        self.qT = sbl("lay_qT", [P, PAIRS7, 2, P])
        self.kT = sbl("lay_kT", [P, PAIRS7, WIN + L])
        self.ss = sbl("lay_squares", [P, NT, 2 * H7])
        self.norm2 = sbl("lay_norm2", [P, NT, 2 * H7])
        self.rn = sbl("lay_rnorm", [P, NT, 2 * H7])
        self.q8 = sbl("lay_q8", [P, NT, H7])
        self.mx = sbl("lay_max", [P, NT * NG, GROUP])
        self.nmx = sbl("lay_minus_max", [P, NT * NG, GROUP])
        self.sm = sbl("lay_sum", [P, NT * NG, GROUP])
        self.rs = sbl("lay_rsum", [P, NT * NG, GROUP])
        self.mask = sbl("lay_mask", [P, 2, SPAN], BF16)
        self.ident = sbl("lay_ident", [P, P], BF16)
        HC = HID7 // P
        shared = sbl("lay_shared", [P, 2 * HC * L])[:]
        self.hid, self.gl = (shared[:, i * HC * L:(i + 1) * HC * L].rearrange("p (c t) -> p c t", t=L) for i in range(2))
        o = 2 * GROUP * SPAN
        self.prob = shared[:, 0:o].rearrange("p (a j k) -> p a j k", a=2, j=GROUP)
        self.probT = shared[:, o:o + 2 * GROUP * P].rearrange("p (a j q) -> p a j q", a=2, j=GROUP)
        o += 2 * GROUP * P
        self.probTb = shared[:, o:o + 2 * GROUP * WIN].rearrange("p (a j q) -> p a j q", a=2, j=GROUP)
        self.xg = sbl("lay_x_mlp", [P, NT, D])
        self.xs = sbl("lay_x_shifted", [P, NT, D])
        self.xgT = sbl("lay_x_mlpT", [P, L])

    def w(self, parity, name):
        return self.weights[parity][:, self.at[name]]


def layers_start_stage(nc, lb, late, late_dram, layers_dram, arrived):
    with stage(nc, "lays", "late_loaded zeroed masks") as (block, s):
        @block.sync
        def _(e):
            e.dma_start(late.all[:], late_dram).then_inc(s["late_loaded"], 16)
            e.dma_start(lb.weights[0][:], layers_dram[0]).then_inc(arrived, 16)

        @block.vector
        def _(e):
            e.memset(lb.kT[:, :, 0:WIN], 0.0).then_inc(s["zeroed"], 1)
            e.wait_ge(s["late_loaded"], 16)
            e.tensor_copy(lb.mask[:], late["band_masks"].rearrange("p (a b) -> p a b", a=2)).then_inc(s["masks"], 1)
            e.tensor_copy(lb.ident[:], late["ident_late"]).then_inc(s["masks"], 1)


def layer_prepare_stage(nc, lb, late, parity, arrived):
    with stage(nc, f"layp{parity}", "weights_ready table_ready") as (block, s):
        @block.sync
        def _(e):
            e.wait_ge(arrived, 16)
            e.sem_inc(s["weights_ready"], 1)
            e.sem_clear(arrived)

        @block.vector
        def _(e):
            e.wait_ge(s["weights_ready"], 1)
            for i, n in enumerate(("q_scale", "q_scale_rolled", "k_scale", "k_scale_rolled")):
                e.tensor_tensor(lb.table[:, i], late["rope7"][:, i * NT * DK7:(i + 1) * NT * DK7].rearrange("p (t d) -> p t d", d=DK7),
                                lb.w(parity, n).unsqueeze(1).to_broadcast([P, NT, DK7]), ALU.mult).then_inc(s["table_ready"], 1)


def layer_fetch_stage(nc, lb, layers_dram, arrived, parity, following):
    with stage(nc, f"layf{parity}", "none") as (block, s):
        @block.sync
        def _(e):
            e.dma_start(lb.weights[1 - parity][:], layers_dram[ds(following, 1)].rearrange("a p w -> (a p) w")).then_inc(arrived, 16)


HC7 = HID7 // P
MLP_SIGNALS = (" xg_copied shift_psum first_half second_half normed xgT_psum xgT_ready a_psum gate_psum gelu_ready "
               "hid_ready mlp_psum mlp_added" + NORM_SIGNALS)


class GatedMLP:

    def __init__(self, s, ps, x_all, C, late, half, nb, lb, parity, batch):
        self.s, self.ps, self.x_all, self.C, self.late, self.half, self.nb, self.lb = s, ps, x_all, C, late, half, nb, lb
        self.W = lambda n: lb.w(parity, n)
        self.b = batch
        self.gates = (ps[2], ps[6], ps[7])
        self.values = (ps[4], ps[5], ps[3])

    def tensor_shift(self, e):
        s, xg, bank = self.s, self.lb.xg, self.ps[2]
        e.wait_ge(s["xg_copied"], 1)
        e.matmul(bank[:, 0:NT * HALF], self.late["next_token"], xg[:, :, HALF:], start=True, stop=False, skip_group_check=True)
        e.matmul(bank[:, HALF:NT * HALF], self.late["last_to_first"], xg[:, 0:NT - 1, HALF:], start=False, stop=True,
                 skip_group_check=True).then_inc(s["shift_psum"], 1)

    def tensor_inner(self, e):
        s = self.s
        e.wait_ge(s["normed"], NT)
        tensor_turn(e, lambda t: self.lb.xs[:, t], self.ps[3], self.C["ident"], s["xgT_psum"])
        e.wait_ge(s["xgT_ready"], 1)
        for c in range(HC7):
            e.matmul(self.gates[c][:], self.W("w1")[:, HID7 + c * P:HID7 + (c + 1) * P], self.lb.xgT[:], start=True,
                     stop=True).then_inc(s["gate_psum"], 1)
            e.matmul(self.values[c][:], self.W("w1")[:, c * P:(c + 1) * P], self.lb.xgT[:], start=True,
                     stop=True).then_inc(s["a_psum"], 1)

    def tensor_out(self, e):
        s = self.s
        e.wait_ge(s["hid_ready"], HC7)
        for t in range(NT):
            y = self.ps[7][:, t * P:(t + 1) * P]
            e.matmul(y, self.C["ones"][0:1, :], self.W("b2")[0:1, :], start=True, stop=False)
            for c in range(HC7):
                mm = e.matmul(y, self.lb.hid[:, c, t * P:(t + 1) * P], self.W("w2")[:, c * P:(c + 1) * P], start=False,
                              stop=(c == HC7 - 1))
        mm.then_inc(s["mlp_psum"], 1)

    def scalar_first_half(self, e):
        e.wait_ge(self.s["xg_copied"], 1)
        e.activation(self.lb.xs[:, :, 0:HALF], self.lb.xg[:, :, 0:HALF], ACT.Copy).then_inc(self.s["first_half"], 1)

    def scalar_turned(self, e):
        e.wait_ge(self.s["xgT_psum"], 1)
        e.activation(self.lb.xgT[:], self.ps[3][:], ACT.Identity, bias=self.W("ln")[:, 1:2],
                     scale=self.W("ln")[:, 0:1]).then_inc(self.s["xgT_ready"], 1)

    def scalar_gelu(self, e):
        for c in range(HC7):
            e.wait_ge(self.s["gate_psum"], c + 1)
            e.activation(self.lb.gl[:, c], self.gates[c][:], ACT.Gelu,
                         bias=self.W("b1")[:, HC7 + c:HC7 + c + 1]).then_inc(self.s["gelu_ready"], 1)

    def vector_copy(self, e):
        e.tensor_copy(self.lb.xg[:], self.x_all[:, ds(NT * self.b, NT), :]).then_inc(self.s["xg_copied"], 1)

    def vector_norm(self, e):
        s, xs = self.s, self.lb.xs
        e.wait_ge(s["shift_psum"], 1)
        e.tensor_copy(xs[:, :, HALF:], self.ps[2][:, 0:NT * HALF].rearrange("p (t d) -> p t d", d=HALF)).then_inc(s["second_half"], 1)
        e.wait_ge(s["second_half"], 1)
        e.wait_ge(s["first_half"], 1)
        e.sem_inc(s["sum_ready"], NT)
        vector_moments(e, s, self.nb, lambda t: xs[:, t])
        vector_normalize(e, s, self.nb, lambda t: xs[:, t], lambda t: xs[:, t], signal="normed")

    def pool_norm(self, e):
        pool_rstd(e, self.s, self.nb, self.half)

    def vector_hidden(self, e):
        s, lb = self.s, self.lb
        for c in range(HC7):
            e.wait_ge(s["a_psum"], c + 1)
            e.wait_ge(s["gelu_ready"], c + 1)
            e.scalar_tensor_tensor(lb.hid[:, c], self.values[c][:], self.W("b1")[:, c:c + 1], lb.gl[:, c], ALU.add,
                                   ALU.mult).then_inc(s["hid_ready"], 1)

    def vector_add(self, e):
        e.wait_ge(self.s["mlp_psum"], 1)
        e.tensor_tensor(self.x_all[:, ds(NT * self.b, NT), :], self.ps[7][:].rearrange("p (t d) -> p t d", d=D), self.lb.xg[:],
                        ALU.add).then_inc(self.s["mlp_added"], 1)


NU = NT * NG
NEXT_TILE = {
    0: ([("k", 0), ("k", 1)], [("q", 0)], [("q", 1)]),
    1: ([], [], [("v", 0), ("v", 1)]),
    2: ([], [], [("kT", 0)]),
    3: ([("qT", 0)], [], [("kT", 1), ("qT", 1)]),
}
TILE_BEFORE = {
    0: ([], [], []),
    1: ([], [], []),
    2: ([("oT", 0)], [("oT", 1)], []),
    3: ([], [("out", 0)], []),
}
FIRST_PROJECTIONS = [("k", 0, 0), ("k", 1, 0), ("q", 0, 0), ("q", 1, 0), ("v", 0, 0), ("v", 1, 0)]
FIRST_TURNS = [("kT", 0, 0), ("qT", 0, 0), ("kT", 1, 0), ("qT", 1, 0)]
LAST_OUTPUTS = [("oT", 0, NT - 1), ("oT", 1, NT - 1), ("out", 0, NT - 1)]


def step_slots(u, point):
    if u >= NU:
        return []
    t, g = divmod(u, NG)
    before = [(what, i, t - 1) for what, i in TILE_BEFORE[g][point]] if t >= 1 else []
    after = [(what, i, t + 1) for what, i in NEXT_TILE[g][point]] if t + 1 < NT else []
    return before + after


def slot_order():
    order = FIRST_PROJECTIONS + FIRST_TURNS
    for u in range(NU + 2):
        order = order + step_slots(u, 0) + step_slots(u, 1)
        if u >= 2:
            order = order + [("pv", 0, u - 2)]
        order = order + step_slots(u, 2)
    return order + LAST_OUTPUTS


SLOT = {slot: i for i, slot in enumerate(slot_order())}


def layer_stage(nc, ps, x_all, C, late, half, nb, xc, xT, lb, name, parity, b, mlp_parity=None, mlp_batch=None):
    names = ("x_copied first_zero xT_psum xT_ready slot_full slot0_read slot1_read raw_ready sq_ready squares_ready "
             "straight_ready turned_ready rotated norm2_ready rnorm_ready q8_ready k_normed s_psum max_ready bias_ready "
             "prob_ready probT_psum probT_ready probTb_ready rsum_ready o_ready")
    heads = lambda ap: ap.rearrange("p (h d) -> p h d", d=DK7)
    W = lambda n: lb.w(parity, n)
    part_of = {"q": slice(0, INNER7), "k": slice(INNER7, 2 * INNER7)}
    heads_of = {"q": slice(0, H7), "k": slice(H7, 2 * H7)}
    with stage(nc, name, names + (MLP_SIGNALS if mlp_parity is not None else "")) as (block, s):
        mlp = GatedMLP(s, ps, x_all, C, late, half, nb, lb, mlp_parity, mlp_batch) if mlp_parity is not None else None
        S = lambda u, odd: ps[2 + 2 * (u % 2) + odd]

        def bank(slot):
            return ps[SLOT[slot] % 2]

        def wait_free(e, slot):
            if SLOT[slot] >= 2:
                e.wait_ge(s[f"slot{SLOT[slot] % 2}_read"], SLOT[slot] // 2)

        def wait_full(e, slot):
            e.wait_ge(s["slot_full"], SLOT[slot] + 1)

        def wait_read(e, slot):
            e.wait_ge(s[f"slot{SLOT[slot] % 2}_read"], SLOT[slot] // 2 + 1)

        def read_signal(slot):
            return s[f"slot{SLOT[slot] % 2}_read"]

        @block.tensor
        def _(e):
            def fill(slot):
                what, i, t = slot
                out = bank(slot)
                wait_free(e, slot)
                if what in ("q", "k", "v"):
                    c = 2 * "qkv".index(what) + i
                    mm = e.matmul(out[:], xT[:, t * P:(t + 1) * P], W("qkv")[:, 512 * c:512 * (c + 1)], start=True, stop=True)
                elif what in ("qT", "kT"):
                    if what == "kT":
                        e.wait_ge(s["k_normed"], t + 1)
                    else:
                        e.wait_ge(s["rotated"], 2 * t + 2)
                    src = lb.qk[:, part_of[what[0]]]
                    for c in range(4):
                        mm = e.transpose(out[:, c * P:(c + 1) * P], src[:, (4 * i + c) * P:(4 * i + c + 1) * P], C["ident"])
                elif what == "oT":
                    e.wait_ge(s["o_ready"], NG * (t + 1))
                    for c in range(4):
                        mm = e.transpose(out[:, c * P:(c + 1) * P], lb.o[:, t % 2, (4 * i + c) * P:(4 * i + c + 1) * P], C["ident"])
                elif what == "out":
                    for half_ in range(2):
                        wait_read(e, ("oT", half_, t))
                    for c in range(PAIRS7):
                        mm = e.matmul(out[:, 0:D], lb.oT[:, c], W("wo")[:, c * D:(c + 1) * D], start=(c == 0), stop=(c == PAIRS7 - 1))
                mm.then_inc(s["slot_full"], 1)

            def scores(u):
                t, g = divmod(u, NG)
                if u >= 2:
                    e.wait_ge(s["prob_ready"], u - 1)
                wait_read(e, ("kT", g // 2, t))
                wait_read(e, ("qT", g // 2, t))
                for j in range(2):
                    for odd in range(2):
                        r = slice(DK7 * odd, DK7 * (odd + 1))
                        e.matmul(S(u, odd)[:, j * SPAN:(j + 1) * SPAN], lb.qT[r, 2 * g + j, t % 2],
                                 lb.kT[r, 2 * g + j, t * P:t * P + SPAN], start=(j == 0), stop=False, skip_group_check=True)
                for odd in range(2):
                    mm = e.matmul(S(u, odd)[:, 0:2 * SPAN], lb.ident[:], lb.mask[:, min(t, 1)].unsqueeze(1).to_broadcast([P, 2, SPAN]),
                                  start=False, stop=True, skip_group_check=True)
                mm.then_inc(s["s_psum"], 1)

            def turn_probabilities(u):
                e.wait_ge(s["prob_ready"], u + 1)
                if u >= 1:
                    e.wait_ge(s["probT_ready"], u)
                for j in range(GROUP):
                    mm = e.transpose(ps[6][:, j * P:(j + 1) * P], lb.prob[:, u % 2, j, WIN:], C["ident"])
                if u // NG >= 1:
                    if u > NG:
                        e.wait_ge(s["probTb_ready"], u - NG)
                    for j in range(GROUP):
                        mm = e.transpose(ps[7][0:WIN, j * WIN:(j + 1) * WIN], lb.prob[0:WIN, u % 2, j, 0:WIN], C["ident"][0:WIN, 0:WIN])
                mm.then_inc(s["probT_psum"], 1)

            def values(u):
                t, g = divmod(u, NG)
                slot = ("pv", 0, u)
                wait_free(e, slot)
                e.wait_ge(s["probT_ready"], u + 1)
                if t >= 1:
                    e.wait_ge(s["probTb_ready"], u - NG + 1)
                for i in range(2):
                    wait_read(e, ("v", i, t))
                for j in range(GROUP):
                    cols = slice((GROUP * g + j) * DK7, (GROUP * g + j + 1) * DK7)
                    mm = e.matmul(bank(slot)[:, j * DK7:(j + 1) * DK7], lb.probT[:, u % 2, j], lb.v[:, t % 3, cols],
                                  start=True, stop=(t == 0), skip_group_check=True)
                    if t >= 1:
                        mm = e.matmul(bank(slot)[0:WIN, j * DK7:(j + 1) * DK7], lb.probTb[P - WIN:, u % 2, j],
                                      lb.v[P - WIN:, (t - 1) % 3, cols], start=False, stop=True, skip_group_check=True)
                mm.then_inc(s["slot_full"], 1)

            if mlp:
                mlp.tensor_shift(e)
            e.wait_ge(s["x_copied"], 1)
            tensor_turn(e, lambda t: xc[:, t], ps[6], C["ident"], s["xT_psum"])
            e.wait_ge(s["xT_ready"], 2)
            e.wait_ge(s["first_zero"], 1)
            for slot in FIRST_PROJECTIONS:
                fill(slot)
            if mlp:
                mlp.tensor_inner(e)
            for slot in FIRST_TURNS:
                fill(slot)
            if mlp:
                mlp.tensor_out(e)
            for u in range(NU + 2):
                if u < NU:
                    scores(u)
                for slot in step_slots(u, 0):
                    fill(slot)
                if 1 <= u < NU + 1:
                    if mlp and u == 1:
                        e.wait_ge(s["mlp_added"], 1)
                    turn_probabilities(u - 1)
                for slot in step_slots(u, 1):
                    fill(slot)
                if u >= 2:
                    values(u - 2)
                for slot in step_slots(u, 2):
                    fill(slot)
            for slot in LAST_OUTPUTS:
                fill(slot)

        @block.scalar
        def _(e):
            def take(slot):
                what, i, t = slot
                if what not in ("q", "k", "v", "qT", "kT"):
                    return
                src = bank(slot)
                if what in ("q", "k"):
                    second = what == "q"
                    if t >= 1 and i == 0:
                        e.wait_ge(s["straight_ready"], 2 * (t - 1) + 1 + second)
                        e.wait_ge(s["turned_ready"], 4 * (t - 1) + 2 + 2 * second)
                        e.wait_ge(s["sq_ready"], 2 * (t - 1) + 1 + second)
                    o = part_of[what].start + 512 * i
                    wait_full(e, slot)
                    e.activation(lb.raw[:, o:o + 512], src[:], ACT.Copy).then_inc(read_signal(slot), 1)
                    if i == 1:
                        wait_read(e, (what, 0, t))
                        wait_read(e, (what, 1, t))
                        e.sem_inc(s["raw_ready"], 1)
                elif what == "v":
                    wait_full(e, slot)
                    e.activation(lb.v[:, t % 3, 512 * i:512 * (i + 1)], src[:], ACT.Copy).then_inc(read_signal(slot), 1)
                else:
                    wait_full(e, slot)
                    dst = (lb.qT[:, 4 * i:4 * i + 4, t % 2] if what == "qT" else
                           lb.kT[:, 4 * i:4 * i + 4, WIN + t * P:WIN + (t + 1) * P])
                    e.activation(dst, src[:].rearrange("p (c q) -> p c q", q=P), ACT.Copy).then_inc(read_signal(slot), 1)

            def square(what, t):
                n = 2 * t + (what == "q")
                e.wait_ge(s["raw_ready"], n + 1)
                if t >= 1:
                    e.wait_ge(s["squares_ready"], n - 1)
                part = part_of[what]
                e.activation(lb.sq[:, part], lb.raw[:, part], ACT.Square).then_inc(s["sq_ready"], 1)

            if mlp:
                mlp.scalar_first_half(e)
            e.wait_ge(s["xT_psum"], 1)
            e.activation(xT[0:HALF, :], ps[6][0:HALF, :], ACT.Copy).then_inc(s["xT_ready"], 1)
            e.activation(xT[HALF:, 1:], ps[6][HALF:, 0:L - 1], ACT.Copy).then_inc(s["xT_ready"], 1)
            for i, slot in enumerate(FIRST_PROJECTIONS):
                take(slot)
                if i == 2:
                    square("k", 0)
                if i == 4:
                    square("q", 0)
            if mlp:
                mlp.scalar_turned(e)
                mlp.scalar_gelu(e)
            for slot in FIRST_TURNS:
                take(slot)
            for u in range(NU + 1):
                t, g = divmod(u, NG)
                for slot in step_slots(u, 0):
                    take(slot)
                if u < NU:
                    e.wait_ge(s["bias_ready"], u + 1)
                    if g == 0:
                        e.wait_ge(s["q8_ready"], t + 1)
                    if u >= 2:
                        e.wait_ge(s["probT_psum"], u - 1)
                    for j in range(GROUP):
                        h = GROUP * g + j
                        i = e.activation(lb.prob[:, u % 2, j], S(u, j % 2)[:, (j // 2) * SPAN:(j // 2 + 1) * SPAN], ACT.Exp,
                                         bias=lb.nmx[:, u, j:j + 1], scale=lb.q8[:, t, h:h + 1],
                                         accum_out=lb.sm[:, u, j:j + 1])
                    i.then_inc(s["prob_ready"], 1)
                for slot in step_slots(u, 1):
                    take(slot)
                if u - 1 >= NG:
                    e.wait_ge(s["probT_psum"], u)
                    if u - 1 >= NG + 2:
                        wait_full(e, ("pv", 0, u - 3))
                    e.activation(lb.probTb[P - WIN:, (u - 1) % 2].rearrange("p j q -> p (j q)"), ps[7][0:WIN, 0:GROUP * WIN],
                                 ACT.Copy).then_inc(s["probTb_ready"], 1)
                if g == 0 and t + 1 < NT:
                    square("k", t + 1)
                for slot in step_slots(u, 2):
                    take(slot)
                if g == 0 and t + 1 < NT:
                    square("q", t + 1)

        @block.vector
        def _(e):
            def rotate(what, t):
                n = 2 * t + (what == "q")
                table = 0 if what == "q" else 2
                e.wait_ge(s["raw_ready"], n + 1)
                if t >= 1:
                    wait_full(e, (what + "T", 1, t - 1))
                src = heads(lb.raw[:, part_of[what]])
                cos = lb.table[:, table, t].unsqueeze(1).to_broadcast([P, H7, DK7])
                e.tensor_tensor(heads(lb.qk[:, part_of[what]]), src, cos, ALU.mult).then_inc(s["straight_ready"], 1)
                if t >= 1:
                    e.wait_ge(s["rotated"], n - 1)
                part = heads(lb.part[:, part_of[what]])
                for hf in range(2):
                    to, of = slice(32 * hf, 32 * hf + 32), slice(32 - 32 * hf, 64 - 32 * hf)
                    sin = lb.table[:, table + 1, t, to].unsqueeze(1).to_broadcast([P, H7, DK7 // 2])
                    e.tensor_tensor(part[:, :, to], src[:, :, of], sin, ALU.mult).then_inc(s["turned_ready"], 1)

            def squares(what, t):
                e.wait_ge(s["sq_ready"], 2 * t + (what == "q") + 1)
                e.tensor_reduce(lb.ss[:, t, heads_of[what]], heads(lb.sq[:, part_of[what]]), AX_X, ALU.add).then_inc(s["squares_ready"], 1)

            def normalize_k(t):
                e.wait_ge(s["rotated"], 2 * t + 1)
                e.wait_ge(s["rnorm_ready"], 2 * t + 1)
                k = heads(lb.qk[:, part_of["k"]])
                e.tensor_tensor(k, k, lb.rn[:, t, heads_of["k"]].unsqueeze(2).to_broadcast([P, H7, DK7]), ALU.mult).then_inc(s["k_normed"], 1)

            def take(slot):
                what, i, t = slot
                if what == "oT":
                    wait_full(e, slot)
                    e.tensor_copy(lb.oT[:, 4 * i:4 * i + 4].rearrange("p c q -> p (c q)"), bank(slot)[:]).then_inc(read_signal(slot), 1)
                elif what == "out":
                    wait_full(e, slot)
                    e.tensor_tensor(x_all[:, ds(NT * b + t, 1), :], bank(slot)[:, 0:D].unsqueeze(1), xc[:, t:t + 1], ALU.add).then_inc(read_signal(slot), 1)

            vector_take(e, s, x_all, b, xc)
            if mlp:
                mlp.vector_copy(e)
            e.memset(xT[HALF:, 0:1], 0.0).then_inc(s["first_zero"], 1)
            if mlp:
                mlp.vector_norm(e)
            rotate("k", 0)
            squares("k", 0)
            rotate("q", 0)
            squares("q", 0)
            normalize_k(0)
            if mlp:
                mlp.vector_hidden(e)
                mlp.vector_add(e)
            for u in range(NU + 3):
                t, g = divmod(u, NG)
                if u < NU:
                    e.wait_ge(s["s_psum"], u + 1)
                    for odd in range(2):
                        e.tensor_reduce(lb.mx[:, u, odd::2], S(u, odd)[:, 0:2 * SPAN].rearrange("p (j k) -> p j k", k=SPAN), AX_X,
                                        ALU.max).then_inc(s["max_ready"], 1)
                    e.wait_ge(s["max_ready"], 2 * (u + 1))
                    if g == 0:
                        e.wait_ge(s["q8_ready"], t + 1)
                    e.scalar_tensor_tensor(lb.nmx[:, u], lb.mx[:, u], -1.0, lb.q8[:, t, GROUP * g:GROUP * (g + 1)], ALU.mult,
                                           ALU.mult).then_inc(s["bias_ready"], 1)
                for slot in step_slots(u, 0):
                    take(slot)
                if 1 <= u < NU + 1:
                    e.wait_ge(s["probT_psum"], u)
                    if u >= 3:
                        wait_full(e, ("pv", 0, u - 3))
                    e.tensor_copy(lb.probT[:, (u - 1) % 2].rearrange("p j q -> p (j q)"), ps[6][:]).then_inc(s["probT_ready"], 1)
                for slot in step_slots(u, 1):
                    take(slot)
                if 2 <= u < NU + 2:
                    w = u - 2
                    tw, gw = divmod(w, NG)
                    e.wait_ge(s["prob_ready"], w + 1)
                    e.reciprocal(lb.rs[:, w], lb.sm[:, w]).then_inc(s["rsum_ready"], 1)
                    e.wait_ge(s["rsum_ready"], w + 1)
                    slot = ("pv", 0, w)
                    wait_full(e, slot)
                    e.tensor_tensor(heads(lb.o[:, tw % 2, GROUP * DK7 * gw:GROUP * DK7 * (gw + 1)]), heads(bank(slot)[:, 0:GROUP * DK7]),
                                    lb.rs[:, w].unsqueeze(2).to_broadcast([P, GROUP, DK7]), ALU.mult).then_inc(read_signal(slot), 1)
                    wait_read(e, slot)
                    e.sem_inc(s["o_ready"], 1)
                for slot in step_slots(u, 2):
                    take(slot)
                if t + 1 < NT:
                    if g == 0:
                        rotate("k", t + 1)
                    if g == 1:
                        squares("k", t + 1)
                        rotate("q", t + 1)
                    if g == 2:
                        normalize_k(t + 1)
                        squares("q", t + 1)
            for slot in LAST_OUTPUTS:
                take(slot)

        @block.gpsimd
        def _(e):
            if mlp:
                mlp.pool_norm(e)
            for t in range(NT):
                for i, what in enumerate("kq"):
                    n = 2 * t + i
                    e.wait_ge(s["straight_ready"], n + 1)
                    e.wait_ge(s["turned_ready"], 2 * n + 2)
                    qk = lb.qk[:, part_of[what]]
                    e.tensor_tensor(qk, qk, lb.part[:, part_of[what]], ALU.add).then_inc(s["rotated"], 1)
                    e.wait_ge(s["squares_ready"], n + 1)
                    h = heads_of[what]
                    e.tensor_scalar(lb.norm2[:, t, h], lb.ss[:, t, h], 1e-24, None, ALU.max).then_inc(s["norm2_ready"], 1)
                    e.wait_ge(s["norm2_ready"], n + 1)
                    e.tensor_tensor(lb.rn[:, t, h], lb.norm2[:, t, h], half.to_broadcast([P, H7]), ALU.pow).then_inc(s["rnorm_ready"], 1)
                e.wait_ge(s["rnorm_ready"], 2 * t + 2)
                e.tensor_scalar(lb.q8[:, t], lb.rn[:, t, heads_of["q"]], QK_SCALE, None, ALU.mult).then_inc(s["q8_ready"], 1)


def last_mlp_stage(nc, ps, x_all, C, late, half, nb, lb, parity):
    with stage(nc, f"glu{parity}", MLP_SIGNALS) as (block, s):
        mlp = GatedMLP(s, ps, x_all, C, late, half, nb, lb, parity, B - 1)

        @block.tensor
        def _(e):
            mlp.tensor_shift(e)
            mlp.tensor_inner(e)
            mlp.tensor_out(e)

        @block.scalar
        def _(e):
            mlp.scalar_first_half(e)
            mlp.scalar_turned(e)
            mlp.scalar_gelu(e)

        @block.vector
        def _(e):
            mlp.vector_copy(e)
            mlp.vector_norm(e)
            mlp.vector_hidden(e)
            mlp.vector_add(e)

        @block.gpsimd
        def _(e):
            mlp.pool_norm(e)


def layers(nc, ctx, ps, x_all, C, half, nb, xc, xT, late_layout, late_dram, layers_dram, arrived):
    late = Packed(nc, ctx, "late", late_layout, late_dram)
    lb = LayerBuffers(nc, ctx)
    args = (nc, ps, x_all, C, late, half, nb, xc, xT, lb)
    layers_start_stage(nc, lb, late, late_dram, layers_dram, arrived)
    with nc.Fori(0, DEPTH // 2) as i:
        layer_prepare_stage(nc, lb, late, 0, arrived)
        layer_fetch_stage(nc, lb, layers_dram, arrived, 0, 2 * i + 1)
        layer_stage(*args, "att0", 0, 0)
        with nc.Fori(1, B) as b:
            layer_stage(*args, "both0", 0, b, 0, b - 1)
        layer_prepare_stage(nc, lb, late, 1, arrived)
        layer_stage(*args, "cross", 1, 0, 0, B - 1)
        layer_fetch_stage(nc, lb, layers_dram, arrived, 1, 2 * i + 2)
        with nc.Fori(1, B) as b:
            layer_stage(*args, "both1", 1, b, 1, b - 1)
        last_mlp_stage(nc, ps, x_all, C, late, half, nb, lb, 1)
    with stage(nc, "laye", "none") as (block, s):
        @block.sync
        def _(e):
            e.wait_ge(arrived, 16)


def last_norm_stage(nc, x_all, x_in, half, nb, xc):
    with nc.Fori(0, B) as b:
        with stage(nc, "fin", "x_copied" + NORM_SIGNALS) as (block, s):
            @block.vector
            def _(e):
                e.tensor_tensor(nb.r[:], x_in[:, ds(NT * b, NT), :], x_all[:, ds(NT * b, NT), :], ALU.add).then_inc(s["sum_ready"], NT)
                vector_moments(e, s, nb, lambda t: nb.r[:, t])
                vector_normalize(e, s, nb, lambda t: nb.r[:, t], lambda t: x_all[:, ds(NT * b + t, 1), :])

            @block.gpsimd
            def _(e):
                pool_rstd(e, s, nb, half)



class Packed:

    def __init__(self, nc, ctx, name, layout, dram, first=0, dtype=F32):
        self.width = sum(w for _, w in layout)
        self.all = ctx.enter_context(nc.sbuf_tensor(name + "_sb", [P, self.width], dtype))
        self.dram = dram
        self.at = {}
        self.first = 0
        o = 0
        for n, w in layout:
            self.at[n] = (o, w)
            o += w
            if n == first:
                self.first = o

    def __getitem__(self, name):
        o, w = self.at[name]
        return self.all[:, o:o + w]


class Names:

    def __init__(self, *packs):
        self.packs = packs

    def __getitem__(self, name):
        return next(p for p in self.packs if name in p.at)[name]


def build(nc, a, layouts):
    with ExitStack() as ctx:
        def sb(name, shape, dtype=F32):
            return ctx.enter_context(nc.sbuf_tensor(name, shape, dtype))

        ps = [ctx.enter_context(nc.psum_tensor(f"bank{i}", [P, 512], F32)) for i in range(8)]
        arrived = ctx.enter_context(nc.semaphore("layer_weights_arrived"))
        x_all = sb("x_all", [P, B * NT, D])
        C = Packed(nc, ctx, "constants", layouts["constants"], a["constants"])
        nb = NormBuffers(sb)
        half = C["minus_half"]
        xc = sb("x_batch", [P, NT, D])
        xT = sb("x_batchT", [P, L])
        with ExitStack() as early:
            sbe = lambda n, shape, dtype=F32: early.enter_context(nc.sbuf_tensor(n, shape, dtype))
            W = Packed(nc, early, "weights", layouts["weights"], a["weights"], first="L0_b_out")
            CE = Packed(nc, early, "early", layouts["early"], a["early"])
            CC = Names(C, CE)
            recurrence_stage(nc, ps, a["L0_attn_x"], x_all, W, C, CE, half, nb)
            args = (nc, ps, x_all, W, CC, half, nb, xc, xT)
            experts_stage(*args)
            eg = Eigen(sbe)
            eigen_tables_stage(nc, ps, W, CC, eg)
            eigen_stage(*args, eg)
            ternary_weights_stage(nc, ps, W, CC)
            ternary_stage(*args)
            ident_bf, mask_bf = sbe("ident_bf", [P, P], BF16), sbe("mask_bf", [P, P], BF16)
            with stage(nc, "masks", "copied") as (block, s):
                @block.vector
                def _(e):
                    e.tensor_copy(ident_bf[:], C["ident"]).then_inc(s["copied"], 1)
                    e.tensor_copy(mask_bf[:], CE["causal_mask"]).then_inc(s["copied"], 1)
            causal_stage(*args, ident_bf, mask_bf)
            relu_stage(*args)
            features_stage(*args)
        x_in = sb("x_in", [P, B * NT, D])
        with stage(nc, "keep", "kept") as (block, s):
            @block.vector
            def _(e):
                e.tensor_copy(x_in[:], x_all[:]).then_inc(s["kept"], 1)
        with ExitStack() as last:
            layers(nc, last, ps, x_all, C, half, nb, xc, xT, layouts["late"], a["late"], a["layers"], arrived)
        last_norm_stage(nc, x_all, x_in, half, nb, xc)
        with stage(nc, "end", "stored") as (block, s):
            @block.sync
            def _(e):
                e.dma_start(a["out"].rearrange("b (j p) d -> p (b j) d", p=P), x_all[:]).then_inc(s["stored"], 16)
                e.wait_ge(s["stored"], 16)


def host_layouts(v):
    def rows(w):
        w = np.asarray(w)
        k, m = w.shape
        return w.reshape(k // P, P, m).transpose(1, 0, 2).reshape(P, -1)

    def cols(b):
        return np.asarray(b).reshape(-1, P).T

    def row(b):
        b = np.asarray(b).reshape(1, -1)
        return np.repeat(b, P, 0)

    z = np.zeros
    weights = []
    add = lambda n, w: weights.append((n, np.ascontiguousarray(w, dtype=np.float32)))
    A = np.asarray(v["L0_attn_A"])
    A_pad = z((E0, 32), np.float32)
    A_pad[:, :NS] = A
    CT = z((P, E0), np.float32)
    for b in range(B):
        CT[32 * b:32 * b + NS] = np.asarray(v["L0_attn_C"]).T
    add("L0_W_in", np.asarray(v["L0_attn_W_in"]))
    add("L0_b_in", cols(v["L0_attn_b_in"]))
    cw = np.asarray(v["L0_attn_conv_w"]).reshape(E0 // P, P, TAPS).transpose(1, 0, 2).reshape(P, -1)
    add("L0_conv_w", cw)
    add("L0_conv_b", cols(v["L0_attn_conv_b"]))
    add("L0_A", rows(A_pad))
    add("L0_CT", CT)
    add("L0_Dp", cols(v["L0_attn_Dp"]))
    add("L0_W_out", rows(v["L0_attn_W_out"]))
    add("L0_b_out", row(v["L0_attn_b_out"]))

    add("moe_router", np.asarray(v["L0_ffn_router_w"]))
    pairs = lambda w: np.asarray(w).transpose(1, 0, 2).reshape(D, NE * IE)
    add("moe_router_bias", row(v["L0_ffn_router_bias"]))
    add("moe_gate", np.concatenate([pairs(v["L0_ffn_gate_w"]), np.asarray(v["L0_ffn_s_gate_w"])], 1))
    add("moe_up", np.concatenate([pairs(v["L0_ffn_up_w"]), np.asarray(v["L0_ffn_s_up_w"])], 1))
    add("moe_down", rows(np.concatenate([np.asarray(v["L0_ffn_down_w"]).reshape(NE * IE, D), np.asarray(v["L0_ffn_s_down_w"])], 0)))
    w_in = np.asarray(v["L1_attn_w_in"])
    twice = lambda c: np.concatenate([np.asarray(c)] * 2).reshape(P, 1)
    coupling = z((P, P), np.float32)
    for i in range(P // 16):
        coupling[16 * i:16 * i + 16, 16 * i:16 * i + 16] = np.asarray(v["L1_attn_coupling"])[i % 4]
    add("L1_w_in", w_in.T)
    add("L1_w_in_swapped", np.concatenate([w_in[KS:], w_in[:KS]]).T)
    add("L1_coupling", coupling)
    add("L1_w_out", np.asarray(v["L1_attn_w_out"]).T)
    add("L1_w_gate", np.asarray(v["L1_attn_w_gate"]).T)
    add("L1_b_gate", row(v["L1_attn_b_gate"]))
    add("L1_log_decay", twice(v["L1_attn_log_decay"]))
    add("L1_frequency", twice(v["L1_attn_frequency"]))
    add("L1_w_mlp1", np.asarray(v["L1_attn_w_mlp1"]).T)
    add("L1_b_mlp1", cols(v["L1_attn_b_mlp1"]))
    add("L1_w_mlp2", rows(np.asarray(v["L1_attn_w_mlp2"]).T))
    add("L1_b_mlp2", row(v["L1_attn_b_mlp2"]))
    add("L1_ln1", np.stack([np.asarray(v["L1_attn_ln1_g"]), np.asarray(v["L1_attn_ln1_b"])], 1))
    add("L1_ln2", np.stack([np.asarray(v["L1_attn_ln2_g"]), np.asarray(v["L1_attn_ln2_b"])], 1))
    add("L1f_W_fc", np.asarray(v["L1_ffn_W_fc"]).T)
    add("L1f_W_proj", rows(np.asarray(v["L1_ffn_W_proj"]).T))
    add("L1f_ln_w", cols(v["L1_ffn_ln_w"]))
    add("L1f_ln_b", cols(v["L1_ffn_ln_b"]))
    partner = np.arange(H4 * DK4) ^ 1
    for w in "qk":
        wt, bt = np.asarray(v[f"L2_attn_w{w}"]), np.asarray(v[f"L2_attn_b{w}"])
        add(f"L2_w{w}", wt.T)
        add(f"L2_w{w}_turned", wt[partner].T)
        add(f"L2_b{w}", cols(bt))
        add(f"L2_b{w}_turned", cols(bt[partner]))
    add("L2_wv", np.asarray(v["L2_attn_wv"]).T)
    add("L2_bv", row(v["L2_attn_bv"]))
    add("L2_wo", rows(np.asarray(v["L2_attn_wo"]).T))
    add("L2_bo", row(v["L2_attn_bo"]))
    add("L2f_W1", np.asarray(v["L2_ffn_W1"]))
    add("L2f_b1", cols(v["L2_ffn_b1"]))
    add("L2f_W2", rows(v["L2_ffn_W2"]))
    add("L2f_b2", row(v["L2_ffn_b2"]))
    for w in ("Wq", "Wk", "Wv", "Wo", "Wfc"):
        add("L3_" + w, np.asarray(v["L3_attn_" + w]).T)
    for w in ("bq", "bk", "bo"):
        add("L3_" + w, cols(v["L3_attn_" + w]))
    add("L3_bv", row(v["L3_attn_bv"]))
    add("L3_bfc", row(v["L3_attn_bfc"]))
    proj = z((D, FEATS), np.float32)
    for h in range(H6):
        proj[DH6 * h:DH6 * (h + 1), M6 * h:M6 * (h + 1)] = np.asarray(v["L3_attn_proj"]).T
    add("L3_proj", proj)
    constants = []
    addc = lambda n, w: constants.append((n, np.ascontiguousarray(w, dtype=np.float32)))
    addc("ident", np.eye(P))
    addc("ones", np.ones((P, P)))
    addc("minus_half", np.full((P, 1), -0.5))
    early = []
    adde = lambda n, w: early.append((n, np.ascontiguousarray(w, dtype=np.float32)))
    spread = np.zeros((P, PAIRS * P))
    for i in range(NE):
        spread[i, IE * i:IE * (i + 1)] = 1
    adde("pair_of_expert", spread)
    adde("comes_first", np.repeat((np.arange(NE)[None] < np.arange(NE)[:, None]).reshape(1, -1), P, 0))
    adde("steps", np.repeat(np.arange(CH).reshape(1, -1), P, 0))
    adde("not_first", np.repeat((np.arange(CH) > 0).reshape(1, -1), P, 0))
    adde("half_sign", np.where(np.arange(P) < KS, 1.0, -1.0).reshape(P, 1))
    adde("swap", np.roll(np.eye(P), KS, 0))
    f32 = np.float32
    i, j = np.arange(P)[:, None], np.arange(P)[None]
    adde("causal_mask", np.where(j > i, MASKED, 0.0))
    theta = f32(10000.0) ** (np.arange(0, DK4, 2, dtype=f32) / f32(DK4))
    freqs = np.arange(L, dtype=f32)[:, None] * (f32(1) / theta)[None]
    emb = np.concatenate([freqs, freqs], 1).T
    sign = np.where(np.arange(DK4) % 2 == 0, -1.0, 1.0)[:, None]
    adde("rope4_cos", np.tile(np.cos(emb), (2, 1)))
    adde("rope4_sin", np.tile(np.sin(emb) * sign, (2, 1)))
    adde("head_of_feature", np.arange(P)[:, None] // DH6 == np.arange(H6)[None])
    own = np.zeros((P, FEATS // P, D + H6))
    for m in range(FEATS // P):
        h = (m * P + np.arange(P)) // M6
        own[:, m, :D] = h[:, None] == np.arange(D)[None] // DH6
        own[:, m, D:] = h[:, None] == np.arange(H6)[None]
    adde("own_columns", own.reshape(P, -1))

    late = []
    addl = lambda n, w: late.append((n, np.ascontiguousarray(w, dtype=np.float32)))
    back = np.arange(P)[:, None] - (np.arange(SPAN)[None] - WIN)
    band = np.where((back >= 0) & (back <= WIN), 0.0, MASKED)
    first = np.where(np.arange(SPAN)[None] < WIN, MASKED, band)
    addl("band_masks", np.concatenate([first, band], 1))
    addl("ident_late", np.eye(P))
    addl("next_token", np.eye(P, k=1))
    last_to_first = np.zeros((P, P))
    last_to_first[P - 1, 0] = 1
    addl("last_to_first", last_to_first)
    hw = np.arange(0, DK7, 2, dtype=f32)
    inv = f32(1.0) / f32(10000.0) ** (hw / f32(DK7))
    tt = np.arange(L, dtype=f32)
    fr = tt[:, None] * inv[None]
    base = (hw + f32(0.4 * DK7)) / f32(1.4 * DK7)
    power = (tt - L // 2) / f32(WIN // 2)
    sc = (base[None] ** power[:, None]).astype(f32)
    fr, sc = np.concatenate([fr, fr], 1), np.concatenate([sc, sc], 1)
    sg = np.where(np.arange(DK7) < DK7 // 2, -1.0, 1.0)[None]
    tok = lambda x: x.reshape(NT, P, DK7).transpose(1, 0, 2).reshape(P, -1)
    addl("rope7", np.concatenate([tok(np.cos(fr) * sc), tok(np.sin(fr) * sg * sc), tok(np.cos(fr) / sc), tok(np.sin(fr) * sg / sc)], 1))

    g = lambda n: np.asarray(v["L3_ffn_" + n])
    inner = g("W2").shape[1]
    layers_ = np.zeros((DEPTH + 1, P, sum(w for _, w in LAYER_COLUMNS)), np.float32)
    for d in range(DEPTH):
        w1, b1 = z((D, 2, HID7), np.float32), z((2, HID7), np.float32)
        w1[:, :, :inner] = g("W1")[d].reshape(D, 2, inner)
        b1[:, :inner] = g("b1")[d].reshape(2, inner)
        w2 = z((HID7, D), np.float32)
        w2[:inner] = g("W2")[d]
        part = {"qkv": g("Wqkv")[d], "wo": rows(g("Wo")[d]), "w1": w1.reshape(D, -1), "w2": rows(w2), "b1": cols(b1),
                "ln": np.stack([g("ln_g")[d], g("ln_b")[d]], 1), "b2": row(g("b2")[d]),
                "q_scale": row(g("q_scale")[d]), "q_scale_rolled": row(np.roll(g("q_scale")[d], DK7 // 2)),
                "k_scale": row(g("k_scale")[d]), "k_scale_rolled": row(np.roll(g("k_scale")[d], DK7 // 2))}
        layers_[d] = np.concatenate([part[n] for n, _ in LAYER_COLUMNS], 1)
    packs = {"weights": weights, "constants": constants, "early": early, "late": late}
    out = {k: np.concatenate([w for _, w in p], 1) for k, p in packs.items()}
    out["layers"] = layers_
    return out, {k: [(n, w.shape[1]) for n, w in p] for k, p in packs.items()}


def kernel(**v):
    import concourse.bacc as bacc
    from concourse.bass_utils import run_bass_kernel_spmd as run

    arrays, lay = host_layouts(v)
    arrays["L0_attn_x"] = np.asarray(v["L0_attn_x"])
    nc = bacc.Bacc("TRN2", target_bir_lowering=False, num_devices=1)
    aps = {n: nc.dram_tensor(n, x.shape, mybir.dt.from_np(x.dtype), kind="ExternalInput").ap() for n, x in arrays.items()}
    aps["out"] = nc.dram_tensor("out", (B, L, D), F32, kind="ExternalOutput").ap()
    build(nc, aps, lay)
    return run(nc, [arrays], core_ids=[0]).results[0]["out"]
```

```python
from contextlib import ExitStack, contextmanager

import numpy as np

import concourse.bass as bass
from concourse import mybir

F32 = mybir.dt.float32
BF16 = mybir.dt.bfloat16
ALU = mybir.AluOpType
ACT = mybir.ActivationFunctionType
AX_X = mybir.AxisListType.X
ds = bass.ds

P = 128
B, L, D = 4, 512, 128
NT = L // P
LN_EPS = 1e-5
FIRST_SEMAPHORE = 110
MASKED = -1e30


class Signals:

    def __init__(self, nc, ctx, stage, names):
        self.nums = []
        self.of = {}
        for i, n in enumerate(names.split()):
            s = ctx.enter_context(nc.semaphore(f"{stage}_{n}", num=FIRST_SEMAPHORE + i))
            self.nums.append(s.num)
            self.of[n] = s

    def __getitem__(self, name):
        return self.of[name]


@contextmanager
def stage(nc, name, signals):
    with ExitStack() as ctx:
        s = Signals(nc, ctx, name, signals)
        with nc.Block(no_gpsimd_drain=True) as block:
            yield block, s
        nc.all_engine_barrier(sems_to_clear=range(min(s.nums), max(s.nums) + 1))



NORM_SIGNALS = " sum_ready stats_ready moments_ready eps_added rstd_ready"


class NormBuffers:
    def __init__(self, sb):
        self.r = sb("norm_sum", [P, NT, D])
        self.stats = sb("norm_stats", [P, NT, 6])
        self.moments = sb("norm_moments", [P, NT, 2])
        self.veps = sb("norm_veps", [P, NT])
        self.rstd = sb("norm_rstd", [P, NT])


def vector_moments(e, s, nb, value, round_=0):
    for t in range(NT):
        e.wait_ge(s["sum_ready"], NT * round_ + t + 1)
        e.bn_stats(nb.stats[:, t], value(t)).then_inc(s["stats_ready"], 1)
    for t in range(NT):
        e.wait_ge(s["stats_ready"], NT * round_ + t + 1)
        e.bn_aggr(nb.moments[:, t], nb.stats[:, t]).then_inc(s["moments_ready"], 1)


def pool_rstd(e, s, nb, half, eps=LN_EPS, round_=0):
    e.wait_ge(s["moments_ready"], NT * (round_ + 1))
    e.tensor_scalar(nb.veps[:], nb.moments[:, :, 1], eps, None, ALU.add).then_inc(s["eps_added"], 1)
    e.wait_ge(s["eps_added"], round_ + 1)
    e.tensor_tensor(nb.rstd[:], nb.veps[:], half.to_broadcast([P, NT]), ALU.pow).then_inc(s["rstd_ready"], 1)


def vector_normalize(e, s, nb, value, out, round_=0, signal=None):
    e.wait_ge(s["rstd_ready"], round_ + 1)
    for t in range(NT):
        i = e.tensor_scalar(out(t), value(t), nb.moments[:, t, 0:1], nb.rstd[:, t:t + 1],
                            ALU.subtract, ALU.mult)
        if signal is not None:
            i.then_inc(s[signal], 1)



E0 = 256
NS = 16
TAPS = 4
SCAN_STEPS = 8


def recurrence_stage(nc, ps, x_dram, x_all, W, C, CE, half, nb):
    EC = E0 // P
    with ExitStack() as ctx:
        sbl = lambda n, shape: ctx.enter_context(nc.sbuf_tensor(n, shape, F32))
        xT = sbl("r_xT", [P, B, L])
        xp = sbl("r_xp", [P, EC, B, TAPS - 1 + L])
        xconv = sbl("r_xconv", [P, EC, B, L])
        sig = sbl("r_sig", [P, EC, B, L])
        h = sbl("r_h", [P, 1 + L])
        u = ps[5]
        names = ("x_loaded w_rest early_loaded w_loaded c_loaded xT_psum xT_ready xp_psum xp_ready z_psum sig_ready pad_zero tap_done "
                 "conv_ready u_ready h_zero h_step scan_done ch_psum skip_done y_ready out_psum out_read" + NORM_SIGNALS)
        with stage(nc, "rec", names) as (block, s):
            @block.sync
            def _(e):
                e.dma_start(C.all[:], C.dram).then_inc(s["c_loaded"], 16)
                e.dma_start(x_all[:], x_dram.rearrange("b (j p) d -> p (b j) d", p=P)).then_inc(s["x_loaded"], 16)
                e.dma_start(W.all[:, 0:W.first], W.dram[:, 0:W.first]).then_inc(s["w_loaded"], 16)
                e.dma_start(W.all[:, W.first:], W.dram[:, W.first:]).then_inc(s["w_rest"], 16)
                e.dma_start(CE.all[:], CE.dram).then_inc(s["early_loaded"], 16)
                e.wait_ge(s["w_rest"], 16)
                e.wait_ge(s["early_loaded"], 16)

            @block.tensor
            def _(e):
                e.wait_ge(s["x_loaded"], 16)
                e.wait_ge(s["c_loaded"], 16)
                e.wait_ge(s["w_loaded"], 16)
                for b in range(B):
                    if b >= 1:
                        e.wait_ge(s["xT_ready"], b)
                    for t in range(NT):
                        mm = e.transpose(ps[0][:, t * P:(t + 1) * P], x_all[:, NT * b + t, :], C["ident"])
                    mm.then_inc(s["xT_psum"], 1)
                    e.wait_ge(s["xT_ready"], b + 1)
                    for c in range(EC):
                        if b >= 1:
                            e.wait_ge(s["xp_ready"], EC * (b - 1) + c + 1)
                        e.matmul(ps[1 + c][:], W["L0_W_in"][:, c * P:(c + 1) * P], xT[:, b], start=True,
                                 stop=True).then_inc(s["xp_psum"], 1)
                    for c in range(EC):
                        if b >= 1:
                            e.wait_ge(s["sig_ready"], EC * (b - 1) + c + 1)
                        e.matmul(ps[3 + c][:], W["L0_W_in"][:, E0 + c * P:E0 + (c + 1) * P], xT[:, b], start=True,
                                 stop=True).then_inc(s["z_psum"], 1)
                for b in range(B):
                    e.wait_ge(s["conv_ready"], EC * (b + 1))
                    for c in range(EC):
                        mm = e.matmul(u[32 * b:32 * b + 32, :], W["L0_A"][:, 32 * c:32 * c + 32], xconv[:, c, b],
                                      start=(c == 0), stop=(c == EC - 1))
                    mm.then_inc(s["u_ready"], 1)
                e.wait_ge(s["scan_done"], 1)
                for b in range(B):
                    for c in range(EC):
                        if b >= 1:
                            e.wait_ge(s["skip_done"], EC * (b - 1) + c + 1)
                        e.matmul(ps[1 + c][:], W["L0_CT"][32 * b:32 * b + 32, c * P:(c + 1) * P],
                                 h[32 * b:32 * b + 32, 1:], start=True, stop=True).then_inc(s["ch_psum"], 1)
                    e.wait_ge(s["y_ready"], EC * (b + 1))
                    if b >= 2:
                        e.wait_ge(s["out_read"], NT * (b - 1))
                    for t in range(NT):
                        o = ps[6 + b % 2][:, t * P:(t + 1) * P]
                        e.matmul(o, C["ones"][0:1, :], W["L0_b_out"][0:1, :], start=True, stop=False)
                        for c in range(EC):
                            mm = e.matmul(o, xconv[:, c, b, t * P:(t + 1) * P], W["L0_W_out"][:, c * P:(c + 1) * P],
                                          start=False, stop=(c == EC - 1))
                    mm.then_inc(s["out_psum"], 1)

            @block.vector
            def _(e):
                for c in range(EC):
                    e.memset(xp[:, c, :, 0:TAPS - 1], 0.0).then_inc(s["pad_zero"], 1)
                e.memset(h[:, 0:1], 0.0).then_inc(s["h_zero"], 1)
                e.wait_ge(s["pad_zero"], EC)
                e.wait_ge(s["w_loaded"], 16)
                taps = 0
                for b in range(B):
                    e.wait_ge(s["xT_psum"], b + 1)
                    e.tensor_copy(xT[:, b], ps[0][:]).then_inc(s["xT_ready"], 1)
                    for c in range(EC):
                        e.wait_ge(s["xp_psum"], EC * b + c + 1)
                        e.tensor_scalar(xp[:, c, b, TAPS - 1:], ps[1 + c][:], W["L0_b_in"][:, c:c + 1], None,
                                        ALU.add).then_inc(s["xp_ready"], 1)
                    for c in range(EC):
                        cw = W["L0_conv_w"][:, TAPS * c:TAPS * (c + 1)]
                        e.wait_ge(s["xp_ready"], EC * b + c + 1)
                        e.tensor_scalar(xconv[:, c, b], xp[:, c, b, 0:L], cw[:, 0:1], W["L0_conv_b"][:, c:c + 1],
                                        ALU.mult, ALU.add).then_inc(s["tap_done"], 1)
                        taps += 1
                        for k in range(1, TAPS):
                            e.wait_ge(s["tap_done"], taps)
                            i = e.scalar_tensor_tensor(xconv[:, c, b], xp[:, c, b, k:k + L], cw[:, k:k + 1],
                                                       xconv[:, c, b], ALU.mult, ALU.add)
                            i.then_inc(s["tap_done" if k < TAPS - 1 else "conv_ready"], 1)
                            taps += k < TAPS - 1
                for b in range(B):
                    for c in range(EC):
                        e.wait_ge(s["ch_psum"], EC * b + c + 1)
                        e.wait_ge(s["conv_ready"], EC * b + c + 1)
                        e.scalar_tensor_tensor(xconv[:, c, b], xconv[:, c, b], W["L0_Dp"][:, c:c + 1], ps[1 + c][:],
                                               ALU.mult, ALU.add).then_inc(s["skip_done"], 1)
                        e.wait_ge(s["skip_done"], EC * b + c + 1)
                        e.wait_ge(s["sig_ready"], EC * b + c + 1)
                        e.tensor_tensor(xconv[:, c, b], xconv[:, c, b], sig[:, c, b], ALU.mult).then_inc(s["y_ready"], 1)
                    e.wait_ge(s["out_psum"], b + 1)
                    for t in range(NT):
                        e.tensor_tensor(nb.r[:, t], ps[6 + b % 2][:, t * P:(t + 1) * P], x_all[:, NT * b + t, :],
                                        ALU.add).then_inc(s["sum_ready"], 1)
                    e.wait_ge(s["sum_ready"], NT * (b + 1))
                    e.sem_inc(s["out_read"], NT)
                    vector_moments(e, s, nb, lambda t: nb.r[:, t], round_=b)
                    vector_normalize(e, s, nb, lambda t: nb.r[:, t], lambda t: x_all[:, NT * b + t, :], round_=b)

            @block.scalar
            def _(e):
                e.wait_ge(s["w_loaded"], 16)
                for b in range(B):
                    for c in range(EC):
                        e.wait_ge(s["z_psum"], EC * b + c + 1)
                        e.activation(sig[:, c, b], ps[3 + c][:], ACT.Sigmoid,
                                     bias=W["L0_b_in"][:, EC + c:EC + c + 1]).then_inc(s["sig_ready"], 1)
                e.wait_ge(s["h_zero"], 1)
                e.wait_ge(s["u_ready"], B)
                with e.Fori(0, L // SCAN_STEPS) as i:
                    for k in range(SCAN_STEPS):
                        if k:
                            e.wait_ge(s["h_step"], k)
                        e.activation(h[:, ds(i * SCAN_STEPS + k + 1, 1)], u[:, ds(i * SCAN_STEPS + k, 1)], ACT.Tanh,
                                     bias=h[:, ds(i * SCAN_STEPS + k, 1)]).then_inc(s["h_step"], 1)
                    e.wait_ge(s["h_step"], SCAN_STEPS)
                    e.sem_clear(s["h_step"])
                e.sem_inc(s["scan_done"], 1)

            @block.gpsimd
            def _(e):
                for b in range(B):
                    pool_rstd(e, s, nb, half, round_=b)



BATCH_SIGNALS = " x_copied xT_psum xT_ready out_psum" + NORM_SIGNALS


def vector_take(e, s, x_all, b, xc):
    e.tensor_copy(xc[:], x_all[:, ds(NT * b, NT), :]).then_inc(s["x_copied"], 1)


def tensor_turn(e, src, bank, ident, signal):
    for t in range(NT):
        mm = e.transpose(bank[:, t * P:(t + 1) * P], src(t), ident)
    mm.then_inc(signal, 1)


def vector_finish(e, s, nb, y, xc, x_all, b, extra=None):
    e.wait_ge(s["out_psum"], 1)
    for t in range(NT):
        e.tensor_tensor(nb.r[:, t], y(t), xc[:, t], ALU.add).then_inc(s["sum_ready"], 1)
    vector_moments(e, s, nb, lambda t: nb.r[:, t])
    vector_normalize(e, s, nb, lambda t: nb.r[:, t], lambda t: x_all[:, ds(NT * b + t, 1), :])



NE, TOPK = 8, 4
IE = 64
ISH = 256
PAIRS = NE * IE // P
CHUNKS = PAIRS + ISH // P


def experts_stage(nc, ps, x_all, W, C, half, nb, xc, xT):
    with ExitStack() as ctx:
        sbl = lambda n, shape: ctx.enter_context(nc.sbuf_tensor(n, shape, F32))
        g = sbl("moe_silu", [P, 2, L])
        prod = sbl("moe_prod", [P, CHUNKS, L])
        mx = sbl("moe_max", [P, NT])
        lg = sbl("moe_logits", [P, NT, NE])
        ex = sbl("moe_exp", [P, NT, NE])
        sm = sbl("moe_sum", [P, NT])
        rs = sbl("moe_rsum", [P, NT])
        sc = sbl("moe_scores", [P, NT, NE])
        co = sbl("moe_corrected", [P, NT, NE])
        gt = sbl("moe_greater", [P, NT, NE, NE])
        eq = sbl("moe_equal", [P, NT, NE, NE])
        rank = sbl("moe_rank", [P, NT, NE])
        picked = sbl("moe_picked", [P, NT, NE])
        w = sbl("moe_weight", [P, NT, NE])
        wT = sbl("moe_weightT", [NE, L])
        names = ("logits_psum shifted exp_ready route w_ready wT_psum wT_ready spread_psum spread_read "
                 "gate_psum up_psum silu_ready up_read prod_ready" + BATCH_SIGNALS)
        bc = lambda ap, shape: ap.to_broadcast(shape)
        with nc.Fori(0, B) as b:
            with stage(nc, "moe", names) as (block, s):
                @block.tensor
                def _(e):
                    e.wait_ge(s["x_copied"], 1)
                    tensor_turn(e, lambda t: xc[:, t], ps[0], C["ident"], s["xT_psum"])
                    e.wait_ge(s["xT_ready"], 1)
                    for t in range(NT):
                        mm = e.matmul(ps[1][:, t * NE:(t + 1) * NE], xT[:, t * P:(t + 1) * P], W["moe_router"],
                                      start=True, stop=True)
                    mm.then_inc(s["logits_psum"], 1)

                    def expand(c):
                        if c >= 2:
                            e.wait_ge(s["silu_ready"], c - 1)
                            e.wait_ge(s["up_read"], c - 1)
                        e.matmul(ps[2 + c % 2][:], W["moe_gate"][:, c * P:(c + 1) * P], xT[:], start=True,
                                 stop=True).then_inc(s["gate_psum"], 1)
                        e.matmul(ps[4 + c % 2][:], W["moe_up"][:, c * P:(c + 1) * P], xT[:], start=True,
                                 stop=True).then_inc(s["up_psum"], 1)

                    expand(0)
                    expand(1)
                    e.wait_ge(s["w_ready"], 1)
                    for t in range(NT):
                        mm = e.transpose(ps[6][0:NE, t * P:(t + 1) * P], w[:, t, :], C["ident"])
                    mm.then_inc(s["wT_psum"], 1)
                    e.wait_ge(s["wT_ready"], 1)
                    for c in range(CHUNKS):
                        if c >= 2:
                            expand(c)
                        if c < PAIRS:
                            if c >= 1:
                                e.wait_ge(s["spread_read"], c)
                            e.matmul(ps[0][:], C["pair_of_expert"][0:NE, c * P:(c + 1) * P], wT[:], start=True,
                                     stop=True).then_inc(s["spread_psum"], 1)
                    e.wait_ge(s["prod_ready"], CHUNKS)
                    for t in range(NT):
                        for c in range(CHUNKS):
                            mm = e.matmul(ps[7][:, t * P:(t + 1) * P], prod[:, c, t * P:(t + 1) * P],
                                          W["moe_down"][:, c * P:(c + 1) * P], start=(c == 0), stop=(c == CHUNKS - 1))
                    mm.then_inc(s["out_psum"], 1)

                @block.scalar
                def _(e):
                    e.wait_ge(s["xT_psum"], 1)
                    e.activation(xT[:], ps[0][:], ACT.Copy).then_inc(s["xT_ready"], 1)
                    e.wait_ge(s["shifted"], 1)
                    e.activation(ex[:], lg[:], ACT.Exp).then_inc(s["exp_ready"], 1)
                    for c in range(CHUNKS):
                        if c >= 2:
                            e.wait_ge(s["up_read"], c - 1)
                        e.wait_ge(s["gate_psum"], c + 1)
                        e.activation(g[:, c % 2], ps[2 + c % 2][:], ACT.Silu).then_inc(s["silu_ready"], 1)

                @block.vector
                def _(e):
                    vector_take(e, s, x_all, b, xc)
                    n = [0]

                    def routed(i):
                        n[0] += 1
                        i.then_inc(s["route"], 1)
                        e.wait_ge(s["route"], n[0])

                    s3, s4 = [P, NT, NE], [P, NT, NE, NE]
                    logits = ps[1][:, 0:NT * NE].rearrange("p (t e) -> p t e", e=NE)
                    e.wait_ge(s["logits_psum"], 1)
                    routed(e.tensor_reduce(mx[:], logits, AX_X, ALU.max))
                    e.tensor_tensor(lg[:], logits, bc(mx[:].unsqueeze(2), s3), ALU.subtract).then_inc(s["shifted"], 1)
                    e.wait_ge(s["exp_ready"], 1)
                    routed(e.tensor_reduce(sm[:], ex[:], AX_X, ALU.add))
                    routed(e.reciprocal(rs[:], sm[:]))
                    routed(e.tensor_tensor(sc[:], ex[:], bc(rs[:].unsqueeze(2), s3), ALU.mult))
                    routed(e.tensor_scalar(co[:], sc[:], W["moe_router_bias"], None, ALU.add))
                    other, own = bc(co[:].unsqueeze(2), s4), bc(co[:].unsqueeze(3), s4)
                    first = bc(C["comes_first"].rearrange("p (i j) -> p i j", j=NE).unsqueeze(1), s4)
                    e.tensor_tensor(gt[:], other, own, ALU.is_gt)
                    routed(e.tensor_tensor(eq[:], other, own, ALU.is_equal))
                    routed(e.tensor_tensor(eq[:], eq[:], first, ALU.mult))
                    routed(e.tensor_tensor(gt[:], gt[:], eq[:], ALU.add))
                    routed(e.tensor_reduce(rank[:], gt[:], AX_X, ALU.add))
                    routed(e.scalar_tensor_tensor(picked[:], rank[:], TOPK - 0.5, sc[:], ALU.is_lt, ALU.mult))
                    routed(e.tensor_reduce(sm[:], picked[:], AX_X, ALU.add))
                    routed(e.tensor_scalar(sm[:], sm[:], 1e-20, None, ALU.add))
                    routed(e.reciprocal(rs[:], sm[:]))
                    e.tensor_tensor(w[:], picked[:], bc(rs[:].unsqueeze(2), s3), ALU.mult).then_inc(s["w_ready"], 1)
                    e.wait_ge(s["wT_psum"], 1)
                    e.tensor_copy(wT[:], ps[6][0:NE, :]).then_inc(s["wT_ready"], 1)
                    for c in range(CHUNKS):
                        e.wait_ge(s["silu_ready"], c + 1)
                        e.wait_ge(s["up_psum"], c + 1)
                        i = e.tensor_tensor(prod[:, c], g[:, c % 2], ps[4 + c % 2][:], ALU.mult)
                        i.then_inc(s["up_read"], 1)
                        if c >= PAIRS:
                            e.wait_ge(s["up_read"], c + 1)
                            e.sem_inc(s["prod_ready"], 1)
                            continue
                        e.wait_ge(s["up_read"], c + 1)
                        e.wait_ge(s["spread_psum"], c + 1)
                        e.tensor_tensor(prod[:, c], prod[:, c], ps[0][:], ALU.mult).then_inc(s["prod_ready"], 1)
                        e.wait_ge(s["prod_ready"], c + 1)
                        e.sem_inc(s["spread_read"], 1)
                    vector_finish(e, s, nb, lambda t: ps[7][:, t * P:(t + 1) * P], xc, x_all, b)

                @block.gpsimd
                def _(e):
                    pool_rstd(e, s, nb, half)



KS = 64
CH = 64
NCH = L // CH
MLP1 = 512
TWO_PI_1, TWO_PI_2 = 6.28125, 0.0019350051879882812
TWO_PI_3 = 2 * np.pi - TWO_PI_1 - TWO_PI_2
ROUND = 1.5 * 2.0 ** 23


class Eigen:
    def __init__(self, sb):
        self.cos = sb("eig_cos", [P, CH])
        self.sin = sb("eig_sin", [P, CH])
        self.minus_sin = sb("eig_minus_sin", [P, CH])
        self.decay = sb("eig_decay", [P, NCH, CH])
        self.joined = sb("eig_joined", [P, D])


def eigen_tables_stage(nc, ps, W, C, eg):
    with ExitStack() as ctx:
        sbl = lambda n, shape: ctx.enter_context(nc.sbuf_tensor(n, shape, F32))
        ph, n_, r, sh, c2, s1 = (sbl(f"eigt_{k}", [P, CH]) for k in ("phase", "turns", "rest", "half", "sq", "sin"))
        mag, hold = sbl("eigt_mag", [P, 1]), sbl("eigt_hold", [P, CH])
        with stage(nc, "eigt", "vec mag_ready rest_ready sines_ready joined_psum") as (block, s):
            @block.tensor
            def _(e):
                e.matmul(ps[0][:, 0:D], W["L1_coupling"], W["L1_w_out"], start=True, stop=True).then_inc(s["joined_psum"], 1)

            @block.scalar
            def _(e):
                e.activation(mag[:], W["L1_log_decay"], ACT.Sigmoid).then_inc(s["mag_ready"], 1)
                e.wait_ge(s["rest_ready"], 1)
                e.activation(s1[:], r[:], ACT.Sin).then_inc(s["sines_ready"], 1)
                e.activation(sh[:], r[:], ACT.Sin, scale=0.5).then_inc(s["sines_ready"], 1)

            @block.vector
            def _(e):
                n = [0]

                def then(i):
                    n[0] += 1
                    i.then_inc(s["vec"], 1)
                    e.wait_ge(s["vec"], n[0])

                then(e.tensor_scalar(ph[:], C["steps"], W["L1_frequency"], None, ALU.mult))
                then(e.tensor_scalar(n_[:], ph[:], 1 / (2 * np.pi), ROUND, ALU.mult, ALU.add))
                then(e.tensor_scalar(n_[:], n_[:], -ROUND, None, ALU.add))
                then(e.scalar_tensor_tensor(r[:], n_[:], -TWO_PI_1, ph[:], ALU.mult, ALU.add))
                then(e.scalar_tensor_tensor(r[:], n_[:], -TWO_PI_2, r[:], ALU.mult, ALU.add))
                then(e.scalar_tensor_tensor(r[:], n_[:], -TWO_PI_3, r[:], ALU.mult, ALU.add))
                e.tensor_scalar(r[:], r[:], 3.1415925, -3.1415925, ALU.min, ALU.max).then_inc(s["rest_ready"], 1)
                e.wait_ge(s["joined_psum"], 1)
                e.tensor_copy(eg.joined[:], ps[0][:, 0:D])
                e.wait_ge(s["mag_ready"], 1)
                then(e.tensor_scalar(hold[:], C["not_first"], mag[:], None, ALU.mult))
                e.tensor_copy(eg.decay[:], hold[:].unsqueeze(1).to_broadcast([P, NCH, CH]))
                e.wait_ge(s["sines_ready"], 2)
                then(e.tensor_tensor(c2[:], sh[:], sh[:], ALU.mult))
                then(e.tensor_scalar(eg.cos[:], c2[:], -2.0, 1.0, ALU.mult, ALU.add))
                then(e.tensor_scalar(eg.sin[:], s1[:], C["half_sign"], None, ALU.mult))
                e.tensor_scalar(eg.minus_sin[:], eg.sin[:], -1.0, None, ALU.mult)


def eigen_stage(nc, ps, x_all, W, C, half, nb, xc, xT, eg):
    with ExitStack() as ctx:
        sbl = lambda n, shape: ctx.enter_context(nc.sbuf_tensor(n, shape, F32))
        xn = sbl("eig_xn", [P, NT, D])
        z, z2, dd = sbl("eig_z", [P, NCH, CH]), sbl("eig_z2", [P, NCH, CH]), sbl("eig_d", [P, NCH, CH])
        cc = sbl("eig_c", [P, L])
        gate = sbl("eig_gate", [P, NT, D])
        x1 = sbl("eig_x1", [P, NT, D])
        hid = sbl("eig_hid", [P, MLP1 // P, L])
        names = ("x_copied xn_ready xT_psum xT_ready beta_psum turned_in z_ready "
                 "c_whole d_ready swap2_psum c_half c_ready gate_psum gate_ready h_psum gated x1_ready "
                 "mlp_psum mlp_ready out_psum" + NORM_SIGNALS)
        wide = [P, NCH, CH]
        bc = lambda ap: ap.unsqueeze(1).to_broadcast(wide)
        chunked = lambda ap: ap.rearrange("p (n j) -> p n j", j=CH)
        HC = MLP1 // P
        with nc.Fori(0, B) as b:
            with stage(nc, "eig", names) as (block, s):
                @block.tensor
                def _(e):
                    e.wait_ge(s["xn_ready"], NT)
                    tensor_turn(e, lambda t: xn[:, t], ps[0], C["ident"], s["xT_psum"])
                    e.wait_ge(s["xT_ready"], 1)
                    e.matmul(ps[1][:], W["L1_w_in"], xT[:], start=True, stop=True).then_inc(s["beta_psum"], 1)
                    e.matmul(ps[2][:], W["L1_w_in_swapped"], xT[:], start=True, stop=True).then_inc(s["beta_psum"], 1)
                    for t in range(NT):
                        o = ps[3][:, t * P:(t + 1) * P]
                        e.matmul(o, C["ones"][0:1, :], W["L1_b_gate"][0:1, :], start=True, stop=False)
                        mm = e.matmul(o, xT[:, t * P:(t + 1) * P], W["L1_w_gate"], start=False, stop=True)
                    mm.then_inc(s["gate_psum"], 1)
                    e.wait_ge(s["d_ready"], 1)
                    e.matmul(ps[6][:], C["swap"], dd[:].rearrange("p n j -> p (n j)"), start=True,
                             stop=True).then_inc(s["swap2_psum"], 1)
                    e.wait_ge(s["c_ready"], 1)
                    for t in range(NT):
                        mm = e.matmul(ps[7][:, t * P:(t + 1) * P], cc[:, t * P:(t + 1) * P], eg.joined[:], start=True, stop=True)
                    mm.then_inc(s["h_psum"], 1)
                    e.wait_ge(s["xn_ready"], 2 * NT)
                    tensor_turn(e, lambda t: xn[:, t], ps[0], C["ident"], s["xT_psum"])
                    e.wait_ge(s["xT_ready"], 2)
                    for c in range(HC):
                        if c >= 2:
                            e.wait_ge(s["mlp_ready"], c - 1)
                        e.matmul(ps[1 + c % 2][:], W["L1_w_mlp1"][:, c * P:(c + 1) * P], xT[:], start=True,
                                 stop=True).then_inc(s["mlp_psum"], 1)
                    e.wait_ge(s["mlp_ready"], HC)
                    for t in range(NT):
                        o = ps[3][:, t * P:(t + 1) * P]
                        e.matmul(o, C["ones"][0:1, :], W["L1_b_mlp2"][0:1, :], start=True, stop=False)
                        for c in range(HC):
                            mm = e.matmul(o, hid[:, c, t * P:(t + 1) * P], W["L1_w_mlp2"][:, c * P:(c + 1) * P],
                                          start=False, stop=(c == HC - 1))
                    mm.then_inc(s["out_psum"], 1)

                @block.scalar
                def _(e):
                    for r in range(2):
                        ln = W[f"L1_ln{r + 1}"]
                        e.wait_ge(s["xT_psum"], r + 1)
                        e.activation(xT[:], ps[0][:], ACT.Identity, bias=ln[:, 1:2], scale=ln[:, 0:1]).then_inc(s["xT_ready"], 1)
                        if r == 0:
                            e.wait_ge(s["gate_psum"], 1)
                            e.activation(gate[:].rearrange("p t d -> p (t d)"), ps[3][:], ACT.Sigmoid).then_inc(s["gate_ready"], 1)
                    for c in range(HC):
                        e.wait_ge(s["mlp_psum"], c + 1)
                        e.activation(hid[:, c], ps[1 + c % 2][:], ACT.Silu, bias=W["L1_b_mlp1"][:, c:c + 1]).then_inc(s["mlp_ready"], 1)

                @block.vector
                def _(e):
                    vector_take(e, s, x_all, b, xc)
                    e.wait_ge(s["x_copied"], 1)
                    e.sem_inc(s["sum_ready"], NT)
                    vector_moments(e, s, nb, lambda t: xc[:, t])
                    vector_normalize(e, s, nb, lambda t: xc[:, t], lambda t: xn[:, t], signal="xn_ready")
                    e.wait_ge(s["beta_psum"], 1)
                    e.tensor_tensor(z[:], chunked(ps[1][:]), bc(eg.cos[:]), ALU.mult).then_inc(s["turned_in"], 1)
                    e.wait_ge(s["beta_psum"], 2)
                    e.tensor_tensor(z2[:], chunked(ps[2][:]), bc(eg.minus_sin[:]), ALU.mult).then_inc(s["turned_in"], 1)
                    e.wait_ge(s["turned_in"], 2)
                    e.tensor_tensor(z[:], z[:], z2[:], ALU.add).then_inc(s["z_ready"], 1)
                    flat = lambda x: x[:].rearrange("p n j -> p (n j)")
                    e.wait_ge(s["z_ready"], 1)
                    e.tensor_tensor_scan(flat(dd)[:, ::-1], flat(eg.decay), flat(z)[:, ::-1], 0.0, ALU.mult,
                                         ALU.add).then_inc(s["d_ready"], 1)
                    e.wait_ge(s["d_ready"], 1)
                    e.tensor_tensor(z[:], dd[:], bc(eg.cos[:]), ALU.mult).then_inc(s["c_half"], 1)
                    e.wait_ge(s["swap2_psum"], 1)
                    e.tensor_tensor(z2[:], chunked(ps[6][:]), bc(eg.sin[:]), ALU.mult).then_inc(s["c_half"], 1)
                    e.wait_ge(s["c_half"], 2)
                    e.tensor_tensor(cc[:], flat(z), flat(z2), ALU.add).then_inc(s["c_whole"], 1)
                    e.wait_ge(s["c_whole"], 1)
                    first = cc[:].rearrange("p (n j) -> p n j", j=CH)[:, 1:, 0]
                    e.tensor_tensor(first, chunked(ps[1][:])[:, 0:NCH - 1, CH - 1], first, ALU.add).then_inc(s["c_ready"], 1)
                    e.wait_ge(s["h_psum"], 1)
                    e.wait_ge(s["gate_ready"], 1)
                    e.tensor_tensor(gate[:].rearrange("p t d -> p (t d)"), gate[:].rearrange("p t d -> p (t d)"), ps[7][:],
                                    ALU.mult).then_inc(s["gated"], 1)
                    e.wait_ge(s["gated"], 1)
                    e.tensor_tensor(x1[:], gate[:], xc[:], ALU.add).then_inc(s["x1_ready"], 1)
                    e.wait_ge(s["x1_ready"], 1)
                    e.sem_inc(s["sum_ready"], NT)
                    vector_moments(e, s, nb, lambda t: x1[:, t], round_=1)
                    e.wait_ge(s["xT_psum"], 1)
                    vector_normalize(e, s, nb, lambda t: x1[:, t], lambda t: xn[:, t], round_=1, signal="xn_ready")
                    e.wait_ge(s["xn_ready"], 2 * NT)
                    e.tensor_tensor(x1[:], x1[:], xc[:], ALU.add).then_inc(s["x1_ready"], 1)
                    e.wait_ge(s["x1_ready"], 2)
                    e.wait_ge(s["out_psum"], 1)
                    for t in range(NT):
                        e.tensor_tensor(nb.r[:, t], ps[3][:, t * P:(t + 1) * P], x1[:, t], ALU.add).then_inc(s["sum_ready"], 1)
                    vector_moments(e, s, nb, lambda t: nb.r[:, t], round_=2)
                    vector_normalize(e, s, nb, lambda t: nb.r[:, t], lambda t: x_all[:, ds(NT * b + t, 1), :], round_=2)

                @block.gpsimd
                def _(e):
                    for r in range(3):
                        pool_rstd(e, s, nb, half, round_=r)



HID3 = 512
TERNARY_EPS = 1e-6


def ternary_weights_stage(nc, ps, W, C):
    names = ("L1f_W_fc", "L1f_W_proj")
    with ExitStack() as ctx:
        sbl = lambda n, shape: ctx.enter_context(nc.sbuf_tensor(n, shape, F32))
        part = sbl("ter_part", [P, 2, 4])
        gamma, rg = sbl("ter_gamma", [P, 2]), sbl("ter_rgamma", [P, 2])
        above, below = sbl("ter_above", [P, HID3]), sbl("ter_below", [P, HID3])
        with stage(nc, "ter", "vec parts_ready total_psum") as (block, s):
            @block.tensor
            def _(e):
                e.wait_ge(s["parts_ready"], 2)
                e.matmul(ps[0][:, 0:8], C["ones"], part[:].rearrange("p a b -> p (a b)"), start=True,
                         stop=True).then_inc(s["total_psum"], 1)

            @block.vector
            def _(e):
                n = [0]

                def then(i):
                    n[0] += 1
                    i.then_inc(s["vec"], 1)
                    e.wait_ge(s["vec"], n[0])

                for i, w in enumerate(names):
                    e.tensor_reduce(part[:, i], W[w].rearrange("p (a b) -> p a b", a=4), AX_X, ALU.add,
                                    apply_absolute_value=True).then_inc(s["parts_ready"], 1)
                e.wait_ge(s["total_psum"], 1)
                then(e.tensor_reduce(gamma[:], ps[0][:, 0:8].rearrange("p (a b) -> p a b", a=2), AX_X, ALU.add))
                then(e.tensor_scalar(gamma[:], gamma[:], 1.0 / (D * HID3), TERNARY_EPS, ALU.mult, ALU.add))
                then(e.reciprocal(rg[:], gamma[:]))
                for i, w in enumerate(names):
                    then(e.tensor_scalar(above[:], W[w], rg[:, i:i + 1], 0.5, ALU.mult, ALU.is_gt))
                    then(e.tensor_scalar(below[:], W[w], rg[:, i:i + 1], -0.5, ALU.mult, ALU.is_lt))
                    then(e.tensor_tensor(W[w], above[:], below[:], ALU.subtract))


def ternary_stage(nc, ps, x_all, W, C, half, nb, xc, xT):
    HC = HID3 // P
    with ExitStack() as ctx:
        sbl = lambda n, shape: ctx.enter_context(nc.sbuf_tensor(n, shape, F32))
        h = sbl("ter_h", [P, NT, HID3])
        hT = sbl("ter_hT", [P, HC, L])
        names = "h_psum gelu_ready h_normed hT_psum hT_ready" + BATCH_SIGNALS
        with nc.Fori(0, B) as b:
            with stage(nc, "tern", names) as (block, s):
                @block.tensor
                def _(e):
                    e.wait_ge(s["x_copied"], 1)
                    tensor_turn(e, lambda t: xc[:, t], ps[0], C["ident"], s["xT_psum"])
                    e.wait_ge(s["xT_ready"], 1)
                    for t in range(NT):
                        e.matmul(ps[1 + t][:], xT[:, t * P:(t + 1) * P], W["L1f_W_fc"], start=True,
                                 stop=True).then_inc(s["h_psum"], 1)
                    e.wait_ge(s["h_normed"], NT)
                    for c in range(HC):
                        if c >= 2:
                            e.wait_ge(s["hT_ready"], c - 1)
                        tensor_turn(e, lambda t: h[:, t, c * P:(c + 1) * P], ps[5 + c % 2], C["ident"], s["hT_psum"])
                    e.wait_ge(s["hT_ready"], HC)
                    for t in range(NT):
                        for c in range(HC):
                            mm = e.matmul(ps[7][:, t * P:(t + 1) * P], hT[:, c, t * P:(t + 1) * P],
                                          W["L1f_W_proj"][:, c * P:(c + 1) * P], start=(c == 0), stop=(c == HC - 1))
                    mm.then_inc(s["out_psum"], 1)

                @block.scalar
                def _(e):
                    e.wait_ge(s["xT_psum"], 1)
                    e.activation(xT[:], ps[0][:], ACT.Copy).then_inc(s["xT_ready"], 1)
                    for t in range(NT):
                        e.wait_ge(s["h_psum"], t + 1)
                        e.activation(h[:, t], ps[1 + t][:], ACT.Gelu).then_inc(s["sum_ready"], 1)
                    for c in range(HC):
                        e.wait_ge(s["hT_psum"], c + 1)
                        e.activation(hT[:, c], ps[5 + c % 2][:], ACT.Identity, bias=W["L1f_ln_b"][:, c:c + 1],
                                     scale=W["L1f_ln_w"][:, c:c + 1]).then_inc(s["hT_ready"], 1)

                @block.vector
                def _(e):
                    vector_take(e, s, x_all, b, xc)
                    vector_moments(e, s, nb, lambda t: h[:, t])
                    vector_normalize(e, s, nb, lambda t: h[:, t], lambda t: h[:, t], signal="h_normed")
                    e.wait_ge(s["out_psum"], 1)
                    for t in range(NT):
                        e.tensor_tensor(nb.r[:, t], ps[7][:, t * P:(t + 1) * P], xc[:, t], ALU.add).then_inc(s["sum_ready"], 1)
                    e.wait_ge(s["h_normed"], NT)
                    vector_moments(e, s, nb, lambda t: nb.r[:, t], round_=1)
                    vector_normalize(e, s, nb, lambda t: nb.r[:, t], lambda t: x_all[:, ds(NT * b + t, 1), :], round_=1)

                @block.gpsimd
                def _(e):
                    pool_rstd(e, s, nb, half)
                    pool_rstd(e, s, nb, half, round_=1)



H4, DK4 = 16, 64
PAIRS4 = H4 // 2
SCALE4 = DK4 ** -0.5


def causal_stage(nc, ps, x_all, W, C, half, nb, xc, xT, ident_bf, mask_bf):
    UNITS = [(qt, h) for qt in range(NT) for h in range(H4)]
    NU = len(UNITS)
    with ExitStack() as ctx:
        sbl = lambda n, shape: ctx.enter_context(nc.sbuf_tensor(n, shape, F32))
        qT, kT = sbl("att_qT", [P, PAIRS4, L]), sbl("att_kT", [P, PAIRS4, L])
        v = sbl("att_v", [P, NT, H4 * DK4])
        straight, turned = sbl("att_straight", [P, 2, L]), sbl("att_turned", [P, 2, L])
        mx, nmx, sm, rs = (sbl(f"att_{k}", [P, NT * H4]) for k in ("max", "minus_max", "sum", "rsum"))
        prob, probT = sbl("att_prob", [P, 3, L]), sbl("att_probT", [P, 3, NT, P])
        o, oT = sbl("att_o", [P, NT, H4 * DK4]), sbl("att_oT", [P, PAIRS4, L])
        names = ("proj_psum straight_ready turned_ready rope_ready v_psum v_ready s_psum max_ready bias_ready prob_ready "
                 "probT_psum probT_ready pv_psum rsum_ready o_ready oT_psum oT_ready" + BATCH_SIGNALS)
        with nc.Fori(0, B) as b:
            with stage(nc, "att", names) as (block, s):
                S = lambda u: ps[1 + u % 4]
                T = lambda u: ps[5 + u % 2]
                O = lambda h: (ps[7] if h < H4 // 2 else ps[0])[:, (h % 8) * DK4:(h % 8 + 1) * DK4]

                @block.tensor
                def _(e):
                    e.wait_ge(s["x_copied"], 1)
                    tensor_turn(e, lambda t: xc[:, t], ps[0], C["ident"], s["xT_psum"])
                    e.wait_ge(s["xT_ready"], 1)
                    for c in range(2 * PAIRS4):
                        w = "q" if c < PAIRS4 else "k"
                        cc = slice((c % PAIRS4) * P, (c % PAIRS4 + 1) * P)
                        if c >= 2:
                            e.wait_ge(s["straight_ready"], c - 1)
                            e.wait_ge(s["turned_ready"], c - 1)
                        e.matmul(ps[1 + 2 * (c % 2)][:], W[f"L2_w{w}"][:, cc], xT[:], start=True, stop=True).then_inc(s["proj_psum"], 1)
                        e.matmul(ps[2 + 2 * (c % 2)][:], W[f"L2_w{w}_turned"][:, cc], xT[:], start=True, stop=True).then_inc(s["proj_psum"], 1)
                    for i in range(2 * NT):
                        t, hf = divmod(i, 2)
                        if i >= 2:
                            e.wait_ge(s["v_ready"], i - 1)
                        cc = slice(512 * hf, 512 * (hf + 1))
                        e.matmul(ps[5 + i % 2][:], C["ones"][0:1, :], W["L2_bv"][0:1, cc], start=True, stop=False)
                        e.matmul(ps[5 + i % 2][:], xT[:, t * P:(t + 1) * P], W["L2_wv"][:, cc], start=False,
                                 stop=True).then_inc(s["v_psum"], 1)
                    e.wait_ge(s["rope_ready"], 2 * PAIRS4)
                    e.wait_ge(s["v_ready"], 2 * NT)
                    for u in range(NU + 3):
                        if u < NU:
                            qt, h = UNITS[u]
                            if u >= 4:
                                e.wait_ge(s["prob_ready"], u - 3)
                            r = slice(DK4 * (h % 2), DK4 * (h % 2 + 1))
                            e.matmul(S(u)[:, 0:(qt + 1) * P], qT[r, h // 2, qt * P:(qt + 1) * P], kT[r, h // 2, 0:(qt + 1) * P],
                                     start=True, stop=False, skip_group_check=True)
                            e.matmul(S(u)[:, qt * P:(qt + 1) * P], ident_bf[:], mask_bf[:], start=False, stop=True,
                                     skip_group_check=True).then_inc(s["s_psum"], 1)
                        if 2 <= u < NU + 2:
                            qt, h = UNITS[u - 2]
                            e.wait_ge(s["prob_ready"], u - 1)
                            if u >= 4:
                                e.wait_ge(s["probT_ready"], u - 3)
                            for k in range(qt + 1):
                                mm = e.transpose(T(u - 2)[:, k * P:(k + 1) * P], prob[:, (u - 2) % 3, k * P:(k + 1) * P], C["ident"])
                            mm.then_inc(s["probT_psum"], 1)
                        if u >= 3:
                            qt, h = UNITS[u - 3]
                            e.wait_ge(s["probT_ready"], u - 2)
                            if h % (H4 // 2) == 0 and qt >= 1:
                                e.wait_ge(s["o_ready"], 2 * (qt - 1) + 1 + h // (H4 // 2))
                            for k in range(qt + 1):
                                mm = e.matmul(O(h), probT[:, (u - 3) % 3, k], v[:, k, h * DK4:(h + 1) * DK4],
                                              start=(k == 0), stop=(k == qt))
                            mm.then_inc(s["pv_psum"], 1)
                    e.wait_ge(s["o_ready"], 2 * NT)
                    for c in range(PAIRS4):
                        if c >= 2:
                            e.wait_ge(s["oT_ready"], c - 1)
                        tensor_turn(e, lambda t: o[:, t, c * P:(c + 1) * P], ps[5 + c % 2], C["ident"], s["oT_psum"])
                    e.wait_ge(s["oT_ready"], PAIRS4)
                    for t in range(NT):
                        y = ps[1][:, t * P:(t + 1) * P]
                        e.matmul(y, C["ones"][0:1, :], W["L2_bo"][0:1, :], start=True, stop=False)
                        for c in range(PAIRS4):
                            mm = e.matmul(y, oT[:, c, t * P:(t + 1) * P], W["L2_wo"][:, c * P:(c + 1) * P], start=False,
                                          stop=(c == PAIRS4 - 1))
                    mm.then_inc(s["out_psum"], 1)

                @block.scalar
                def _(e):
                    e.wait_ge(s["xT_psum"], 1)
                    e.activation(xT[:], ps[0][:], ACT.Copy).then_inc(s["xT_ready"], 1)
                    for i in range(2 * NT):
                        t, hf = divmod(i, 2)
                        e.wait_ge(s["v_psum"], i + 1)
                        e.activation(v[:, t, 512 * hf:512 * (hf + 1)], ps[5 + i % 2][:], ACT.Copy).then_inc(s["v_ready"], 1)
                    for u, (qt, h) in enumerate(UNITS):
                        e.wait_ge(s["bias_ready"], u + 1)
                        if u >= 3:
                            e.wait_ge(s["probT_psum"], u - 2)
                        e.activation(prob[:, u % 3, 0:(qt + 1) * P], S(u)[:, 0:(qt + 1) * P], ACT.Exp, bias=nmx[:, u:u + 1],
                                     scale=SCALE4, accum_out=sm[:, u:u + 1]).then_inc(s["prob_ready"], 1)
                    for c in range(PAIRS4):
                        e.wait_ge(s["oT_psum"], c + 1)
                        e.activation(oT[:, c], ps[5 + c % 2][:], ACT.Copy).then_inc(s["oT_ready"], 1)

                @block.vector
                def _(e):
                    vector_take(e, s, x_all, b, xc)
                    for c in range(2 * PAIRS4):
                        w = "q" if c < PAIRS4 else "k"
                        bias, bias_turned = W[f"L2_b{w}"], W[f"L2_b{w}_turned"]
                        i = c % PAIRS4
                        if c >= 2:
                            e.wait_ge(s["rope_ready"], c - 1)
                        e.wait_ge(s["proj_psum"], 2 * c + 1)
                        e.scalar_tensor_tensor(straight[:, c % 2], ps[1 + 2 * (c % 2)][:], bias[:, i:i + 1], C["rope4_cos"],
                                               ALU.add, ALU.mult).then_inc(s["straight_ready"], 1)
                        e.wait_ge(s["proj_psum"], 2 * c + 2)
                        e.scalar_tensor_tensor(turned[:, c % 2], ps[2 + 2 * (c % 2)][:], bias_turned[:, i:i + 1], C["rope4_sin"],
                                               ALU.add, ALU.mult).then_inc(s["turned_ready"], 1)
                    for u in range(NU + 3):
                        if u < NU:
                            qt, h = UNITS[u]
                            e.wait_ge(s["s_psum"], u + 1)
                            e.tensor_reduce(mx[:, u:u + 1], S(u)[:, 0:(qt + 1) * P], AX_X, ALU.max).then_inc(s["max_ready"], 1)
                            e.wait_ge(s["max_ready"], u + 1)
                            e.tensor_scalar(nmx[:, u:u + 1], mx[:, u:u + 1], -SCALE4, None, ALU.mult).then_inc(s["bias_ready"], 1)
                        if 2 <= u < NU + 2:
                            qt, h = UNITS[u - 2]
                            e.wait_ge(s["probT_psum"], u - 1)
                            if u >= 5:
                                e.wait_ge(s["pv_psum"], u - 4)
                            e.tensor_copy(probT[:, (u - 2) % 3, 0:qt + 1].rearrange("p k q -> p (k q)"),
                                          T(u - 2)[:, 0:(qt + 1) * P]).then_inc(s["probT_ready"], 1)
                        if u >= 3 and u % (H4 // 2) == 2:
                            j = (u - 2) // (H4 // 2) - 1
                            qt, hf = divmod(j, 2)
                            cols = slice(8 * j, 8 * j + 8)
                            e.wait_ge(s["prob_ready"], 8 * (j + 1))
                            e.reciprocal(rs[:, cols], sm[:, cols]).then_inc(s["rsum_ready"], 1)
                            e.wait_ge(s["rsum_ready"], j + 1)
                            e.wait_ge(s["pv_psum"], 8 * (j + 1))
                            e.tensor_tensor(o[:, qt, 512 * hf:512 * (hf + 1)].rearrange("p (h d) -> p h d", d=DK4),
                                            (ps[0] if hf else ps[7])[:].rearrange("p (h d) -> p h d", d=DK4),
                                            rs[:, cols].unsqueeze(2).to_broadcast([P, 8, DK4]), ALU.mult).then_inc(s["o_ready"], 1)
                    vector_finish(e, s, nb, lambda t: ps[1][:, t * P:(t + 1) * P], xc, x_all, b)

                @block.gpsimd
                def _(e):
                    for c in range(2 * PAIRS4):
                        out = (qT if c < PAIRS4 else kT)[:, c % PAIRS4]
                        e.wait_ge(s["straight_ready"], c + 1)
                        e.wait_ge(s["turned_ready"], c + 1)
                        e.tensor_tensor(out, straight[:, c % 2], turned[:, c % 2], ALU.add).then_inc(s["rope_ready"], 1)
                    pool_rstd(e, s, nb, half)



HID5 = 512


def relu_stage(nc, ps, x_all, W, C, half, nb, xc, xT):
    HC = HID5 // P
    with ExitStack() as ctx:
        hT = ctx.enter_context(nc.sbuf_tensor("mlp_hT", [P, HC, L], F32))
        names = "h_psum h_ready" + BATCH_SIGNALS
        with nc.Fori(0, B) as b:
            with stage(nc, "mlp", names) as (block, s):
                @block.tensor
                def _(e):
                    e.wait_ge(s["x_copied"], 1)
                    tensor_turn(e, lambda t: xc[:, t], ps[0], C["ident"], s["xT_psum"])
                    e.wait_ge(s["xT_ready"], 1)
                    for c in range(HC):
                        e.matmul(ps[1 + c][:], W["L2f_W1"][:, c * P:(c + 1) * P], xT[:], start=True,
                                 stop=True).then_inc(s["h_psum"], 1)
                    e.wait_ge(s["h_ready"], HC)
                    for t in range(NT):
                        y = ps[7][:, t * P:(t + 1) * P]
                        e.matmul(y, C["ones"][0:1, :], W["L2f_b2"][0:1, :], start=True, stop=False)
                        for c in range(HC):
                            mm = e.matmul(y, hT[:, c, t * P:(t + 1) * P], W["L2f_W2"][:, c * P:(c + 1) * P], start=False,
                                          stop=(c == HC - 1))
                    mm.then_inc(s["out_psum"], 1)

                @block.scalar
                def _(e):
                    e.wait_ge(s["xT_psum"], 1)
                    e.activation(xT[:], ps[0][:], ACT.Copy).then_inc(s["xT_ready"], 1)
                    for c in range(HC):
                        e.wait_ge(s["h_psum"], c + 1)
                        e.activation(hT[:, c], ps[1 + c][:], ACT.Relu, bias=W["L2f_b1"][:, c:c + 1]).then_inc(s["h_ready"], 1)

                @block.vector
                def _(e):
                    vector_take(e, s, x_all, b, xc)
                    vector_finish(e, s, nb, lambda t: ps[7][:, t * P:(t + 1) * P], xc, x_all, b)

                @block.gpsimd
                def _(e):
                    pool_rstd(e, s, nb, half)



H6, DH6, M6 = 16, 8, 16
DN6 = DH6 ** -0.25
RATIO6 = M6 ** -0.5
EPS6 = 1e-4
FEATS = H6 * M6


def features_stage(nc, ps, x_all, W, C, half, nb, xc, xT):
    HF = FEATS // P
    with ExitStack() as ctx:
        sbl = lambda n, shape: ctx.enter_context(nc.sbuf_tensor(n, shape, F32))
        t_, sq = sbl("rf_t", [P, 2, L]), sbl("rf_sq", [P, 2, L])
        v1 = sbl("rf_v", [P, NT, D + 1])
        dg = sbl("rf_diag", [P, 2, NT * H6])
        mx = sbl("rf_max", [P, 2, NT * H6])
        kmx, kall, kdiag, kmax = sbl("rf_kmax_tok", [P, H6]), sbl("rf_kmax_h", [H6, 1]), sbl("rf_kmax_d", [H6, H6]), sbl("rf_kmax", [P, NT, H6])
        f = sbl("rf_f", [P, 2, NT, FEATS])
        fT = sbl("rf_fT", [P, HF, L])
        bd = sbl("rf_context", [P, HF, D + H6])
        den = sbl("rf_den", [P, NT, H6])
        o, oT, hT = sbl("rf_o", [P, NT, D]), sbl("rf_oT", [P, L]), sbl("rf_hT", [P, L])
        names = ("proj_psum t_ready sq_ready v_psum v_ready one_ready td_psum diag_psum diag_ready max_ready less_diag "
                 "less_max exp_ready f_ready ktok_ready kT_psum kall_ready kdiag_ready kmax_psum kmax_ready context_psum "
                 "context_ready fT_psum fT_ready ratio_psum den_ready o_ready oT_psum oT_ready h_psum hT_ready"
                 + BATCH_SIGNALS)
        heads = lambda ap: ap.rearrange("p (g m) -> p g m", m=M6)
        wide = [P, 2 * H6, M6]
        WK = D + H6
        with nc.Fori(0, B) as b:
            with stage(nc, "rf", names) as (block, s):
                td = lambda w, j: ps[4 + 2 * w + j]

                @block.tensor
                def _(e):
                    e.wait_ge(s["x_copied"], 1)
                    tensor_turn(e, lambda t: xc[:, t], ps[0], C["ident"], s["xT_psum"])
                    e.wait_ge(s["xT_ready"], 1)
                    e.matmul(ps[1][:], W["L3_Wq"], xT[:], start=True, stop=True).then_inc(s["proj_psum"], 1)
                    e.matmul(ps[2][:], W["L3_Wk"], xT[:], start=True, stop=True).then_inc(s["proj_psum"], 1)
                    for t in range(NT):
                        y = ps[3][:, t * P:(t + 1) * P]
                        e.matmul(y, C["ones"][0:1, :], W["L3_bv"][0:1, :], start=True, stop=False)
                        mm = e.matmul(y, xT[:, t * P:(t + 1) * P], W["L3_Wv"], start=False, stop=True)
                    mm.then_inc(s["v_psum"], 1)
                    for w in (1, 0):
                        e.wait_ge(s["t_ready"], 2 if w == 0 else 1)
                        for t in range(NT):
                            mm = e.matmul(td(w, t // 2)[:, (t % 2) * FEATS:(t % 2 + 1) * FEATS], t_[:, w, t * P:(t + 1) * P],
                                          W["L3_proj"], start=True, stop=True)
                        mm.then_inc(s["td_psum"], 1)
                        e.wait_ge(s["sq_ready"], 2 if w == 0 else 1)
                        for t in range(NT):
                            mm = e.matmul(ps[0][:, (w * NT + t) * H6:(w * NT + t + 1) * H6], sq[:, w, t * P:(t + 1) * P],
                                          C["head_of_feature"], start=True, stop=True)
                        mm.then_inc(s["diag_psum"], 1)
                    e.wait_ge(s["ktok_ready"], 1)
                    e.transpose(ps[1][0:H6, 0:P], kmx[:], C["ident"]).then_inc(s["kT_psum"], 1)
                    e.wait_ge(s["kdiag_ready"], 1)
                    e.matmul(ps[1][:, P:P + H6], C["ones"][0:H6, :], kdiag[:], start=True, stop=True).then_inc(s["kmax_psum"], 1)
                    e.wait_ge(s["v_ready"], 1)
                    e.wait_ge(s["one_ready"], 1)
                    e.wait_ge(s["f_ready"], 4)
                    for m in range(HF):
                        for t in range(NT):
                            mm = e.matmul(ps[2 + m][:, 0:D + 1], f[:, 1, t, m * P:(m + 1) * P], v1[:, t], start=(t == 0),
                                          stop=(t == NT - 1))
                        mm.then_inc(s["context_psum"], 1)
                    for m in range(HF):
                        tensor_turn(e, lambda t: f[:, 0, t, m * P:(m + 1) * P], ps[4 + m], C["ident"], s["fT_psum"])
                    e.wait_ge(s["fT_ready"], HF)
                    e.wait_ge(s["context_ready"], 2 * HF)
                    for t in range(NT):
                        for m in range(HF):
                            mm = e.matmul(ps[6 + t // 2][:, (t % 2) * WK:(t % 2 + 1) * WK], fT[:, m, t * P:(t + 1) * P], bd[:, m],
                                          start=(m == 0), stop=(m == HF - 1))
                    mm.then_inc(s["ratio_psum"], 1)
                    e.wait_ge(s["o_ready"], 2)
                    tensor_turn(e, lambda t: o[:, t], ps[0], C["ident"], s["oT_psum"])
                    e.wait_ge(s["oT_ready"], 1)
                    e.matmul(ps[1][:], W["L3_Wo"], oT[:], start=True, stop=True).then_inc(s["h_psum"], 1)
                    e.wait_ge(s["hT_ready"], 1)
                    for t in range(NT):
                        y = ps[2][:, t * P:(t + 1) * P]
                        e.matmul(y, C["ones"][0:1, :], W["L3_bfc"][0:1, :], start=True, stop=False)
                        mm = e.matmul(y, hT[:, t * P:(t + 1) * P], W["L3_Wfc"], start=False, stop=True)
                    mm.then_inc(s["out_psum"], 1)

                @block.scalar
                def _(e):
                    e.wait_ge(s["xT_psum"], 1)
                    e.activation(xT[:], ps[0][:], ACT.Copy).then_inc(s["xT_ready"], 1)
                    for n, w in enumerate((1, 0)):
                        e.wait_ge(s["t_ready"], n + 1)
                        e.activation(sq[:, w], t_[:, w], ACT.Square).then_inc(s["sq_ready"], 1)
                    e.wait_ge(s["v_psum"], 1)
                    e.activation(v1[:, :, 0:D], ps[3][:].rearrange("p (t d) -> p t d", d=D), ACT.Copy).then_inc(s["v_ready"], 1)
                    for n in range(4):
                        w, j = (0, n) if n < 2 else (1, n - 2)
                        e.wait_ge(s["less_max"], n + 1)
                        x = f[:, w, 2 * j:2 * j + 2]
                        e.activation(x, x, ACT.Exp).then_inc(s["exp_ready"], 1)
                    for m in range(HF):
                        e.wait_ge(s["fT_psum"], m + 1)
                        e.activation(fT[:, m], ps[4 + m][:], ACT.Copy).then_inc(s["fT_ready"], 1)
                    e.wait_ge(s["oT_psum"], 1)
                    e.activation(oT[:], ps[0][:], ACT.Copy).then_inc(s["oT_ready"], 1)
                    e.wait_ge(s["h_psum"], 1)
                    e.activation(hT[:], ps[1][:], ACT.Identity, bias=W["L3_bo"]).then_inc(s["hT_ready"], 1)

                @block.vector
                def _(e):
                    vector_take(e, s, x_all, b, xc)
                    e.memset(v1[:, :, D:], 1.0).then_inc(s["one_ready"], 1)
                    e.wait_ge(s["proj_psum"], 2)
                    for w, name in ((1, "k"), (0, "q")):
                        e.tensor_scalar(t_[:, w], ps[1 + w][:], W[f"L3_b{name}"], DN6, ALU.add, ALU.mult).then_inc(s["t_ready"], 1)
                    for n, w in enumerate((1, 0)):
                        e.wait_ge(s["diag_psum"], 2)
                        e.tensor_scalar(dg[:, w], ps[0][:, w * NT * H6:(w + 1) * NT * H6], 0.5, None,
                                        ALU.mult).then_inc(s["diag_ready"], 1)
                        for j in range(2):
                            e.tensor_reduce(mx[:, w, 2 * H6 * j:2 * H6 * (j + 1)], heads(td(w, j)[:]), AX_X,
                                            ALU.max).then_inc(s["max_ready"], 1)
                        if w == 1:
                            e.wait_ge(s["max_ready"], 2)
                            e.tensor_reduce(kmx[:], mx[:, 1].rearrange("p (t h) -> p h t", h=H6), AX_X,
                                            ALU.max).then_inc(s["ktok_ready"], 1)
                            e.wait_ge(s["kT_psum"], 1)
                            e.tensor_reduce(kall[:], ps[1][0:H6, 0:P], AX_X, ALU.max).then_inc(s["kall_ready"], 1)
                            e.wait_ge(s["kall_ready"], 1)
                            e.tensor_scalar(kdiag[:], C["ident"][0:H6, 0:H6], kall[:], None, ALU.mult).then_inc(s["kdiag_ready"], 1)
                            e.wait_ge(s["kmax_psum"], 1)
                            e.tensor_copy(kmax[:], ps[1][:, P:P + H6].unsqueeze(1).to_broadcast([P, NT, H6])).then_inc(s["kmax_ready"], 1)
                    e.wait_ge(s["diag_ready"], 2)
                    e.wait_ge(s["max_ready"], 4)
                    e.wait_ge(s["kmax_ready"], 1)
                    for n in range(4):
                        w, j = (0, n) if n < 2 else (1, n - 2)
                        x = f[:, w, 2 * j:2 * j + 2].rearrange("p t (h m) -> p (t h) m", m=M6)
                        cols = slice(2 * H6 * j, 2 * H6 * (j + 1))
                        most = mx[:, 0, cols] if w == 0 else kmax[:].rearrange("p t h -> p (t h)")[:, cols]
                        e.tensor_tensor(x, heads(td(w, j)[:]), dg[:, w, cols].unsqueeze(2).to_broadcast(wide),
                                        ALU.subtract).then_inc(s["less_diag"], 1)
                        e.wait_ge(s["less_diag"], n + 1)
                        e.tensor_tensor(x, x, most.unsqueeze(2).to_broadcast(wide), ALU.subtract).then_inc(s["less_max"], 1)
                    for n in range(4):
                        w, j = (0, n) if n < 2 else (1, n - 2)
                        x = f[:, w, 2 * j:2 * j + 2]
                        e.wait_ge(s["exp_ready"], n + 1)
                        e.tensor_scalar(x, x, EPS6, RATIO6, ALU.add, ALU.mult).then_inc(s["f_ready"], 1)
                    for m in range(HF):
                        e.wait_ge(s["context_psum"], m + 1)
                        own = C["own_columns"][:, m * WK:(m + 1) * WK]
                        e.tensor_tensor(bd[:, m, 0:D], ps[2 + m][:, 0:D], own[:, 0:D], ALU.mult).then_inc(s["context_ready"], 1)
                        e.tensor_scalar(bd[:, m, D:], own[:, D:], ps[2 + m][:, D:D + 1], None, ALU.mult).then_inc(s["context_ready"], 1)
                    e.wait_ge(s["ratio_psum"], 1)
                    for j in range(2):
                        r = ps[6 + j][:, 0:2 * WK].rearrange("p (t k) -> p t k", k=WK)
                        e.reciprocal(den[:, 2 * j:2 * j + 2], r[:, :, D:]).then_inc(s["den_ready"], 1)
                    for j in range(2):
                        r = ps[6 + j][:, 0:2 * WK].rearrange("p (t k) -> p t k", k=WK)
                        e.wait_ge(s["den_ready"], j + 1)
                        for t in range(2):
                            i = e.tensor_tensor(o[:, 2 * j + t].rearrange("p (h d) -> p h d", d=DH6),
                                                r[:, t, 0:D].rearrange("p (h d) -> p h d", d=DH6),
                                                den[:, 2 * j + t].unsqueeze(2).to_broadcast([P, H6, DH6]), ALU.mult)
                        i.then_inc(s["o_ready"], 1)
                    e.wait_ge(s["out_psum"], 1)
                    for t in range(NT):
                        e.scalar_tensor_tensor(nb.r[:, t], ps[2][:, t * P:(t + 1) * P], 0.0, xc[:, t], ALU.max,
                                               ALU.add).then_inc(s["sum_ready"], 1)
                    vector_moments(e, s, nb, lambda t: nb.r[:, t])
                    vector_normalize(e, s, nb, lambda t: nb.r[:, t], lambda t: x_all[:, ds(NT * b + t, 1), :])

                @block.gpsimd
                def _(e):
                    pool_rstd(e, s, nb, half)



DEPTH = 6
H7, DK7 = 16, 64
INNER7 = H7 * DK7
PAIRS7 = H7 // 2
WIN = 32
SPAN = WIN + P
HALF = D // 2
QK_SCALE = 8.0
GROUP = 4
NG = H7 // GROUP
HID7 = 384
LAYER_COLUMNS = (("qkv", 3 * INNER7), ("wo", PAIRS7 * D), ("w1", 2 * HID7), ("w2", HID7), ("b1", 2 * HID7 // P),
                 ("ln", 2), ("b2", D), ("q_scale", DK7), ("q_scale_rolled", DK7), ("k_scale", DK7), ("k_scale_rolled", DK7))


HC7 = HID7 // P


class LayerBuffers:
    def __init__(self, nc, ctx):
        sbl = lambda n, shape, dtype=F32: ctx.enter_context(nc.sbuf_tensor(n, shape, dtype))
        width = sum(w for _, w in LAYER_COLUMNS)
        self.weights = [sbl(f"lay_weights{i}", [P, width]) for i in range(2)]
        self.at, o = {}, 0
        for n, w in LAYER_COLUMNS:
            self.at[n] = slice(o, o + w)
            o += w
        self.table = sbl("lay_table", [P, 4, NT, DK7])
        self.raw = sbl("lay_raw", [P, 2 * INNER7])
        self.sq = sbl("lay_sq", [P, 2 * INNER7])
        self.part = sbl("lay_turned", [P, 2 * INNER7])
        self.qk = sbl("lay_qk", [P, 2 * INNER7])
        self.v = sbl("lay_v", [P, NT, INNER7])
        self.o = sbl("lay_o", [P, 2, INNER7])
        self.oT = sbl("lay_oT", [P, PAIRS7, P])
        self.qT = sbl("lay_qT", [P, PAIRS7, 2, P])
        self.kT = sbl("lay_kT", [P, PAIRS7, WIN + L])
        self.ss = sbl("lay_squares", [P, NT, 2 * H7])
        self.norm2 = sbl("lay_norm2", [P, NT, 2 * H7])
        self.rn = sbl("lay_rnorm", [P, NT, 2 * H7])
        self.q8 = sbl("lay_q8", [P, NT, H7])
        self.mx = sbl("lay_max", [P, NT * NG, GROUP])
        self.nmx = sbl("lay_minus_max", [P, NT * NG, GROUP])
        self.sm = sbl("lay_sum", [P, NT * NG, GROUP])
        self.rs = sbl("lay_rsum", [P, NT * NG, GROUP])
        self.mask = sbl("lay_mask", [P, 2, SPAN], BF16)
        self.ident = sbl("lay_ident", [P, P], BF16)
        self.prob = sbl("lay_prob", [P, 2, GROUP, SPAN])
        self.probT = sbl("lay_probT", [P, 2, GROUP, P])
        self.probTb = sbl("lay_probT_before", [P, 2, GROUP, WIN])
        self.xg = sbl("lay_x_mlp", [P, NT, D])
        self.xs = sbl("lay_x_shifted", [P, NT, D])
        self.xgT = sbl("lay_x_mlpT", [P, L])
        self.hid = sbl("lay_hidden", [P, HC7, L])

    def w(self, parity, name):
        return self.weights[parity][:, self.at[name]]


def layers_start_stage(nc, lb, xT, late, late_dram, layers_dram, arrived):
    with stage(nc, "lays", "late_loaded zero_layer zeroed masks") as (block, s):
        @block.sync
        def _(e):
            e.dma_start(late.all[:], late_dram).then_inc(s["late_loaded"], 16)
            e.dma_start(lb.weights[0][:], layers_dram[0]).then_inc(arrived, 16)
            e.dma_start(lb.weights[1][:], layers_dram[DEPTH]).then_inc(s["zero_layer"], 16)
            e.wait_ge(s["zero_layer"], 16)

        @block.vector
        def _(e):
            e.memset(lb.kT[:, :, 0:WIN], 0.0).then_inc(s["zeroed"], 1)
            e.memset(xT[HALF:, 0:1], 0.0).then_inc(s["zeroed"], 1)
            e.memset(lb.o[:, (NT - 1) % 2], 0.0).then_inc(s["zeroed"], 1)
            e.wait_ge(s["late_loaded"], 16)
            e.tensor_copy(lb.mask[:], late["band_masks"].rearrange("p (a b) -> p a b", a=2)).then_inc(s["masks"], 1)
            e.tensor_copy(lb.ident[:], late["ident_late"]).then_inc(s["masks"], 1)


def layer_table_stage(nc, lb, late, parity, arrived, tiles, first=False):
    with stage(nc, f"tab{parity}{tiles.start}", "weights_ready table_ready") as (block, s):
        if first:
            @block.sync
            def _(e):
                e.wait_ge(arrived, 16)
                e.sem_inc(s["weights_ready"], 1)
                e.sem_clear(arrived)

        @block.vector
        def _(e):
            if first:
                e.wait_ge(s["weights_ready"], 1)
            for i, n in enumerate(("q_scale", "q_scale_rolled", "k_scale", "k_scale_rolled")):
                plain = late["rope7"][:, i * NT * DK7:(i + 1) * NT * DK7].rearrange("p (t d) -> p t d", d=DK7)
                e.tensor_tensor(lb.table[:, i, tiles], plain[:, tiles],
                                lb.w(parity, n).unsqueeze(1).to_broadcast([P, tiles.stop - tiles.start, DK7]),
                                ALU.mult).then_inc(s["table_ready"], 1)


def layer_fetch_stage(nc, lb, layers_dram, arrived, parity, following):
    with stage(nc, f"layf{parity}", "none") as (block, s):
        @block.sync
        def _(e):
            e.dma_start(lb.weights[1 - parity][:], layers_dram[ds(following, 1)].rearrange("a p w -> (a p) w")).then_inc(arrived, 16)


NU = NT * NG
OF_TILE = {
    0: ([("kT", 1, 0), ("qT", 1, 0)], [("v", 0, 1)], [("v", 1, 1)]),
    1: ([], [("k", 0, 2)], [("k", 1, 2)]),
    2: ([], [("oT", 0, -1)], [("kT", 0, 1), ("q", 0, 2)]),
    3: ([("q", 1, 2), ("oT", 1, -1)], [("qT", 0, 1)], [("out", 0, -1)]),
}
OF_BATCH = {
    (4, 1): [("shift", 0, 0)],
    (8, 0): [("mlpT", 0, 0)],
    (9, 0): [("x", 0, NT)],
    (10, 0): [("gate", 0, 0)],
    (11, 0): [("gate", 1, 0)],
    (11, 1): [("gate", 2, 0)],
    (13, 0): [("value", 0, 0)],
    (13, 1): [("value", 1, 0)],
    (14, 0): [("value", 2, 0)],
    (16, 0): [("mlp", 0, 0)],
}
VECTOR_WORK = {3: ["take_mlp"], 5: ["moments"], 7: ["normalize"], 8: ["take_next"]}
SCALAR_WORK = {4: ["first_half"], 12: ["gelu"]}
VECTOR_TILE_WORK = {
    0: [("straight", "k", 1), ("turned", "k", 1)],
    1: [("normalize_k", "k", 1), ("straight", "q", 1)],
    2: [("turned", "q", 1), ("squares", "k", 2)],
    3: [("squares", "q", 2)],
}


def attention_plan():
    steps = []
    for u in range(NU + 3):
        slots, vector, scalar = [[], [], []], list(VECTOR_WORK.get(u, [])), list(SCALAR_WORK.get(u, []))
        t, g = divmod(u, NG)
        for p in range(3):
            slots[p] += OF_BATCH.get((u, p), [])
            if u < NU:
                slots[p] += [(what, i, t + d) for what, i, d in OF_TILE[g][p]]
        if u < NU:
            vector += [(work, what, t + d) for work, what, d in VECTOR_TILE_WORK[g]]
            scalar += {2: [("square", "k", t + 2)], 3: [("square", "q", t + 2)]}.get(g, [])
        steps.append((u, slots, vector, scalar))
    return steps


def first_tiles_plan():
    return [(None, [[("x", 0, NT)], [], [("k", 0, NT), ("k", 1, NT)]], [], []),
            (None, [[], [], [("q", 0, NT), ("q", 1, NT), ("v", 0, NT), ("v", 1, NT)]],
             [("squares", "k", NT), ("straight", "k", NT), ("turned", "k", NT), ("squares", "q", NT), ("straight", "q", NT),
              ("turned", "q", NT), ("normalize_k", "k", NT)],
             [("square", "k", NT), ("square", "q", NT)]),
            (None, [[], [], [("kT", 0, NT), ("qT", 0, NT), ("k", 0, NT + 1), ("k", 1, NT + 1)]], [], []),
            (None, [[], [], [("q", 0, NT + 1), ("q", 1, NT + 1)]], [("squares", "k", NT + 1), ("squares", "q", NT + 1)],
             [("square", "k", NT + 1), ("square", "q", NT + 1)])]


def last_mlp_plan():
    return [(None, [[("oT", 0, -1), ("oT", 1, -1)], [], [("out", 0, -1)]], ["take_mlp"], ["first_half"]),
            (None, [[], [], [("shift", 0, 0)]], ["moments", "normalize"], []),
            (None, [[], [], [("mlpT", 0, 0)]], [], []),
            (None, [[], [], [("gate", 0, 0), ("gate", 1, 0), ("gate", 2, 0)]], [], ["gelu"]),
            (None, [[], [], [("value", 0, 0), ("value", 1, 0), ("value", 2, 0), ("mlp", 0, 0)]], [], [])]


def layer_stage(nc, ps, x_all, C, late, half, nb, xc, xT, lb, name, plan, own=None, following=None, mlp=None):
    names = ("x_copied first_half_turned slot_full slot0_read slot1_read slot2_read raw_ready sq_ready squares_ready "
             "straight_ready turned_ready rotated norm2_ready rnorm_ready q8_ready k_normed s_psum max_ready bias_ready "
             "prob_ready probT_psum probT_ready probTb_ready rsum_ready o_ready xg_copied first_half second_half normed "
             "gelu_ready hid_ready" + NORM_SIGNALS)
    heads = lambda ap: ap.rearrange("p (h d) -> p h d", d=DK7)
    part_of = {"q": slice(0, INNER7), "k": slice(INNER7, 2 * INNER7)}
    heads_of = {"q": slice(0, H7), "k": slice(H7, 2 * H7)}
    SLOT = {}
    for u, slots, _, _ in plan:
        order = slots[0] + slots[1] + ([("pv", 0, u - 2)] if u is not None and 2 <= u < NU + 2 else []) + slots[2]
        for slot in order:
            SLOT[slot] = len(SLOT)
    projected = {t: i for i, t in enumerate(sorted({slot[2] for slot in SLOT if slot[0] == "k"}))}
    rotated = {t: i for i, t in enumerate(sorted({work[2] for _, _, vector, _ in plan for work in vector if work[0] == "straight"}))}
    group_of = lambda t: (own if 0 <= t < NT else mlp if t < 0 else following)
    W = lambda t, n: lb.w(group_of(t)[0], n)
    WM = lambda n: lb.w(mlp[0], n)
    with stage(nc, name, names) as (block, s):
        S = lambda u, odd: ps[2 + 2 * (u % 2) + odd]

        def bank(slot):
            return ps[(0, 1, 7)[SLOT[slot] % 3]]

        def read_signal(slot):
            return s[f"slot{SLOT[slot] % 3}_read"]

        def wait_free(e, slot):
            if SLOT[slot] >= 3:
                e.wait_ge(read_signal(slot), SLOT[slot] // 3)

        def wait_full(e, slot):
            e.wait_ge(s["slot_full"], SLOT[slot] + 1)

        def wait_read(e, slot):
            if slot in SLOT:
                e.wait_ge(read_signal(slot), SLOT[slot] // 3 + 1)

        @block.tensor
        def _(e):
            def fill(slot):
                what, i, t = slot
                out = bank(slot)
                wait_free(e, slot)
                if what == "x":
                    e.wait_ge(s["x_copied"], 1)
                    for c in range(NT):
                        mm = e.transpose(out[:, c * P:(c + 1) * P], xc[:, c], C["ident"])
                elif what in ("q", "k", "v"):
                    c = 2 * "qkv".index(what) + i
                    if t >= NT:
                        wait_read(e, ("x", 0, NT))
                        e.wait_ge(s["first_half_turned"], 1)
                    mm = e.matmul(out[:], xT[:, t % NT * P:(t % NT + 1) * P], W(t, "qkv")[:, 512 * c:512 * (c + 1)], start=True, stop=True)
                elif what in ("qT", "kT"):
                    if what == "kT":
                        if t in rotated:
                            e.wait_ge(s["k_normed"], rotated[t] + 1)
                    elif t in rotated:
                        e.wait_ge(s["rotated"], 2 * rotated[t] + 2)
                    src = lb.qk[:, part_of[what[0]]]
                    for c in range(4):
                        mm = e.transpose(out[:, c * P:(c + 1) * P], src[:, (4 * i + c) * P:(4 * i + c + 1) * P], C["ident"])
                elif what == "oT":
                    if t >= 0:
                        e.wait_ge(s["o_ready"], NG * (t + 1))
                    for c in range(4):
                        mm = e.transpose(out[:, c * P:(c + 1) * P], lb.o[:, t % 2, (4 * i + c) * P:(4 * i + c + 1) * P], C["ident"])
                elif what == "out":
                    for j in range(2):
                        wait_read(e, ("oT", j, t))
                    for c in range(PAIRS7):
                        mm = e.matmul(out[:, 0:D], lb.oT[:, c], W(t, "wo")[:, c * D:(c + 1) * D], start=(c == 0), stop=(c == PAIRS7 - 1))
                elif what == "shift":
                    e.wait_ge(s["xg_copied"], 1)
                    e.matmul(out[:, 0:NT * HALF], late["next_token"], lb.xg[:, :, HALF:], start=True, stop=False, skip_group_check=True)
                    mm = e.matmul(out[:, HALF:NT * HALF], late["last_to_first"], lb.xg[:, 0:NT - 1, HALF:], start=False, stop=True,
                                  skip_group_check=True)
                elif what == "mlpT":
                    e.wait_ge(s["normed"], NT)
                    for c in range(NT):
                        mm = e.transpose(out[:, c * P:(c + 1) * P], lb.xs[:, c], C["ident"])
                elif what in ("gate", "value"):
                    wait_read(e, ("mlpT", 0, 0))
                    o = i * P + (HID7 if what == "gate" else 0)
                    mm = e.matmul(out[:], WM("w1")[:, o:o + P], lb.xgT[:], start=True, stop=True)
                elif what == "mlp":
                    e.wait_ge(s["hid_ready"], HC7)
                    for c in range(NT):
                        y = out[:, c * P:(c + 1) * P]
                        e.matmul(y, C["ones"][0:1, :], WM("b2")[0:1, :], start=True, stop=False)
                        for h in range(HC7):
                            mm = e.matmul(y, lb.hid[:, h, c * P:(c + 1) * P], WM("w2")[:, h * P:(h + 1) * P], start=False,
                                          stop=(h == HC7 - 1))
                mm.then_inc(s["slot_full"], 1)

            def scores(u):
                t, g = divmod(u, NG)
                if u >= 2:
                    e.wait_ge(s["prob_ready"], u - 1)
                if u >= NG + 2:
                    e.wait_ge(s["probTb_ready"], u - NG - 1)
                wait_read(e, ("kT", g // 2, t))
                wait_read(e, ("qT", g // 2, t))
                for j, odd in ((0, 0), (0, 1), (1, 0), (1, 1)):
                    r = slice(DK7 * odd, DK7 * (odd + 1))
                    e.matmul(S(u, odd)[:, j * SPAN:(j + 1) * SPAN], lb.qT[r, 2 * g + j, t % 2],
                             lb.kT[r, 2 * g + j, t * P:t * P + SPAN], start=(j == 0), stop=False, skip_group_check=True)
                    if j == 1:
                        e.matmul(S(u, odd)[:, 0:2 * SPAN], lb.ident[:], lb.mask[:, min(t, 1)].unsqueeze(1).to_broadcast([P, 2, SPAN]),
                                 start=False, stop=True, skip_group_check=True).then_inc(s["s_psum"], 1)

            def turn_probabilities(u):
                e.wait_ge(s["prob_ready"], u + 1)
                if u >= 1:
                    e.wait_ge(s["probT_ready"], u)
                for j in range(GROUP):
                    mm = e.transpose(ps[6][:, j * P:(j + 1) * P], lb.prob[:, u % 2, j, WIN:], C["ident"])
                if u // NG >= 1:
                    if u > NG:
                        e.wait_ge(s["probTb_ready"], u - NG)
                    for j in range(GROUP):
                        mm = e.transpose(S(u, 0)[0:WIN, j * WIN:(j + 1) * WIN], lb.prob[0:WIN, u % 2, j, 0:WIN], C["ident"][0:WIN, 0:WIN])
                mm.then_inc(s["probT_psum"], 1)

            def values(u):
                t, g = divmod(u, NG)
                slot = ("pv", 0, u)
                wait_free(e, slot)
                e.wait_ge(s["probT_ready"], u + 1)
                if t >= 1:
                    e.wait_ge(s["probTb_ready"], u - NG + 1)
                for i in range(2):
                    wait_read(e, ("v", i, t))
                for j in range(GROUP):
                    cols = slice((GROUP * g + j) * DK7, (GROUP * g + j + 1) * DK7)
                    mm = e.matmul(bank(slot)[:, j * DK7:(j + 1) * DK7], lb.probT[:, u % 2, j], lb.v[:, t, cols],
                                  start=True, stop=(t == 0), skip_group_check=True)
                    if t >= 1:
                        mm = e.matmul(bank(slot)[0:WIN, j * DK7:(j + 1) * DK7], lb.probTb[P - WIN:, u % 2, j],
                                      lb.v[P - WIN:, t - 1, cols], start=False, stop=True, skip_group_check=True)
                mm.then_inc(s["slot_full"], 1)

            for u, slots, _, _ in plan:
                if u is not None and u < NU:
                    scores(u)
                for slot in slots[0]:
                    fill(slot)
                if u is not None and 1 <= u < NU + 1:
                    turn_probabilities(u - 1)
                for slot in slots[1]:
                    fill(slot)
                if u is not None and 2 <= u < NU + 2:
                    values(u - 2)
                for slot in slots[2]:
                    fill(slot)

        @block.scalar
        def _(e):
            def take(slot):
                what, i, t = slot
                if what in ("out", "shift", "value", "mlp"):
                    return
                wait_full(e, slot)
                src = bank(slot)
                if what == "oT":
                    e.activation(lb.oT[:, 4 * i:4 * i + 4].rearrange("p c q -> p (c q)"), src[:], ACT.Copy).then_inc(read_signal(slot), 1)
                if what == "x":
                    e.activation(xT[0:HALF, :], src[0:HALF, :], ACT.Copy).then_inc(s["first_half_turned"], 1)
                    e.activation(xT[HALF:, 1:], src[HALF:, 0:L - 1], ACT.Copy).then_inc(read_signal(slot), 1)
                elif what in ("q", "k"):
                    if t - 1 in rotated:
                        m = 2 * rotated[t - 1] + (what == "q")
                        e.wait_ge(s["straight_ready"], m + 1)
                        e.wait_ge(s["turned_ready"], 2 * m + 2)
                    if t - 1 in projected:
                        e.wait_ge(s["sq_ready"], 2 * projected[t - 1] + (what == "q") + 1)
                    o = part_of[what].start + 512 * i
                    e.activation(lb.raw[:, o:o + 512], src[:], ACT.Copy).then_inc(read_signal(slot), 1)
                    if i == 1:
                        wait_read(e, (what, 0, t))
                        wait_read(e, (what, 1, t))
                        e.sem_inc(s["raw_ready"], 1)
                elif what == "v":
                    e.activation(lb.v[:, t % NT, 512 * i:512 * (i + 1)], src[:], ACT.Copy).then_inc(read_signal(slot), 1)
                elif what in ("qT", "kT"):
                    dst = (lb.qT[:, 4 * i:4 * i + 4, t % 2] if what == "qT" else
                           lb.kT[:, 4 * i:4 * i + 4, WIN + (t % NT) * P:WIN + (t % NT + 1) * P])
                    e.activation(dst, src[:].rearrange("p (c q) -> p c q", q=P), ACT.Copy).then_inc(read_signal(slot), 1)
                elif what == "mlpT":
                    e.activation(lb.xgT[:], src[:], ACT.Identity, bias=WM("ln")[:, 1:2], scale=WM("ln")[:, 0:1]).then_inc(read_signal(slot), 1)
                elif what == "gate":
                    e.activation(lb.hid[:, i], src[:], ACT.Identity, bias=WM("b1")[:, HC7 + i:HC7 + i + 1]).then_inc(read_signal(slot), 1)

            def square(what, t):
                m = 2 * projected[t] + (what == "q")
                e.wait_ge(s["raw_ready"], m + 1)
                if m >= 2:
                    e.wait_ge(s["squares_ready"], m - 1)
                part = part_of[what]
                e.activation(lb.sq[:, part], lb.raw[:, part], ACT.Square).then_inc(s["sq_ready"], 1)

            def exponentials(u):
                t, g = divmod(u, NG)
                if t in projected:
                    e.wait_ge(s["q8_ready"], projected[t] + 1)
                if u >= 2:
                    e.wait_ge(s["probT_psum"], u - 1)
                for j in (0, 2, 1, 3):
                    h = GROUP * g + j
                    if j < 2:
                        e.wait_ge(s["bias_ready"], 2 * u + j + 1)
                    i = e.activation(lb.prob[:, u % 2, j], S(u, j % 2)[:, (j // 2) * SPAN:(j // 2 + 1) * SPAN], ACT.Exp,
                                     bias=lb.nmx[:, u, j:j + 1], scale=lb.q8[:, t, h:h + 1], accum_out=lb.sm[:, u, j:j + 1])
                i.then_inc(s["prob_ready"], 1)

            for u, slots, _, work in plan:
                squared = [w[1:] for w in work if w[0] == "square"]
                for slot in slots[0]:
                    take(slot)
                if u is not None and u < NU:
                    exponentials(u)
                for slot in slots[1]:
                    take(slot)
                if u is not None and NG < u < NU + 1:
                    e.wait_ge(s["probT_psum"], u)
                    if u >= NG + 3:
                        wait_full(e, ("pv", 0, u - 3))
                    e.activation(lb.probTb[P - WIN:, (u - 1) % 2].rearrange("p j q -> p (j q)"), S(u - 1, 0)[0:WIN, 0:GROUP * WIN],
                                 ACT.Copy).then_inc(s["probTb_ready"], 1)
                if u is not None:
                    for w in squared:
                        square(*w)
                for slot in slots[2]:
                    take(slot)
                if u is None:
                    for w in squared:
                        square(*w)
                if "first_half" in work:
                    e.wait_ge(s["xg_copied"], 1)
                    e.activation(lb.xs[:, :, 0:HALF], lb.xg[:, :, 0:HALF], ACT.Copy).then_inc(s["first_half"], 1)
                if "gelu" in work:
                    for c in range(HC7):
                        wait_read(e, ("gate", c, 0))
                    e.activation(lb.hid[:], lb.hid[:], ACT.Gelu).then_inc(s["gelu_ready"], 1)

        @block.vector
        def _(e):
            def straight(what, t):
                if t in projected:
                    e.wait_ge(s["raw_ready"], 2 * projected[t] + (what == "q") + 1)
                if (what + "T", 1, t - 1) in SLOT:
                    wait_full(e, (what + "T", 1, t - 1))
                cos = lb.table[:, 0 if what == "q" else 2, t % NT].unsqueeze(1).to_broadcast([P, H7, DK7])
                e.tensor_tensor(heads(lb.qk[:, part_of[what]]), heads(lb.raw[:, part_of[what]]), cos,
                                ALU.mult).then_inc(s["straight_ready"], 1)

            def turned(what, t):
                if t - 1 in rotated:
                    e.wait_ge(s["rotated"], 2 * rotated[t - 1] + (what == "q") + 1)
                src, part = heads(lb.raw[:, part_of[what]]), heads(lb.part[:, part_of[what]])
                for hf in range(2):
                    to, of = slice(32 * hf, 32 * hf + 32), slice(32 - 32 * hf, 64 - 32 * hf)
                    sin = lb.table[:, 1 if what == "q" else 3, t % NT, to].unsqueeze(1).to_broadcast([P, H7, DK7 // 2])
                    e.tensor_tensor(part[:, :, to], src[:, :, of], sin, ALU.mult).then_inc(s["turned_ready"], 1)

            def squares(what, t):
                e.wait_ge(s["sq_ready"], 2 * projected[t] + (what == "q") + 1)
                e.tensor_reduce(lb.ss[:, t % NT, heads_of[what]], heads(lb.sq[:, part_of[what]]), AX_X, ALU.add).then_inc(s["squares_ready"], 1)

            def normalize_k(_, t):
                e.wait_ge(s["rotated"], 2 * rotated[t] + 1)
                if t in projected:
                    e.wait_ge(s["rnorm_ready"], 2 * projected[t] + 1)
                k = heads(lb.qk[:, part_of["k"]])
                e.tensor_tensor(k, k, lb.rn[:, t % NT, heads_of["k"]].unsqueeze(2).to_broadcast([P, H7, DK7]), ALU.mult).then_inc(s["k_normed"], 1)

            def take(slot):
                what, i, t = slot
                src = bank(slot)
                if what not in ("out", "shift", "value", "mlp"):
                    return
                wait_full(e, slot)
                if what == "out":
                    x = x_all[:, ds(NT * group_of(t)[1] + t % NT, 1), :]
                    e.tensor_tensor(x, src[:, 0:D].unsqueeze(1), x, ALU.add).then_inc(read_signal(slot), 1)
                elif what == "shift":
                    e.tensor_copy(lb.xs[:, :, HALF:], src[:, 0:NT * HALF].rearrange("p (t d) -> p t d", d=HALF)).then_inc(read_signal(slot), 1)
                elif what == "value":
                    e.wait_ge(s["gelu_ready"], 1)
                    e.scalar_tensor_tensor(lb.hid[:, i], src[:], WM("b1")[:, i:i + 1], lb.hid[:, i], ALU.add, ALU.mult).then_inc(read_signal(slot), 1)
                    wait_read(e, slot)
                    e.sem_inc(s["hid_ready"], 1)
                else:
                    e.tensor_tensor(x_all[:, ds(NT * mlp[1], NT), :], src[:].rearrange("p (t d) -> p t d", d=D), lb.xg[:],
                                    ALU.add).then_inc(read_signal(slot), 1)

            def maxima(u):
                t, g = divmod(u, NG)
                if t in projected:
                    e.wait_ge(s["q8_ready"], projected[t] + 1)
                for odd in range(2):
                    e.wait_ge(s["s_psum"], 2 * u + odd + 1)
                    e.tensor_reduce(lb.mx[:, u, odd::2], S(u, odd)[:, 0:2 * SPAN].rearrange("p (j k) -> p j k", k=SPAN), AX_X,
                                    ALU.max).then_inc(s["max_ready"], 1)
                    e.wait_ge(s["max_ready"], 2 * u + odd + 1)
                    e.scalar_tensor_tensor(lb.nmx[:, u, odd::2], lb.mx[:, u, odd::2], -1.0,
                                           lb.q8[:, t, GROUP * g + odd:GROUP * (g + 1):2], ALU.mult, ALU.mult).then_inc(s["bias_ready"], 1)

            def divide(u):
                t, g = divmod(u, NG)
                e.wait_ge(s["prob_ready"], u + 1)
                e.reciprocal(lb.rs[:, u], lb.sm[:, u]).then_inc(s["rsum_ready"], 1)
                e.wait_ge(s["rsum_ready"], u + 1)
                slot = ("pv", 0, u)
                wait_full(e, slot)
                if g == 0 and t >= 1:
                    wait_full(e, ("oT", 1, t - 2))
                e.tensor_tensor(heads(lb.o[:, t % 2, GROUP * DK7 * g:GROUP * DK7 * (g + 1)]), heads(bank(slot)[:, 0:GROUP * DK7]),
                                lb.rs[:, u].unsqueeze(2).to_broadcast([P, GROUP, DK7]), ALU.mult).then_inc(read_signal(slot), 1)
                wait_read(e, slot)
                e.sem_inc(s["o_ready"], 1)

            if own is None and following is not None:
                vector_take(e, s, x_all, following[1], xc)
            for u, slots, work, _ in plan:
                if u is not None and u < NU:
                    maxima(u)
                for slot in slots[0]:
                    take(slot)
                if u is not None and 1 <= u < NU + 1:
                    e.wait_ge(s["probT_psum"], u)
                    if u >= 3:
                        wait_full(e, ("pv", 0, u - 3))
                    e.tensor_copy(lb.probT[:, (u - 1) % 2].rearrange("p j q -> p (j q)"), ps[6][:]).then_inc(s["probT_ready"], 1)
                for slot in slots[1]:
                    take(slot)
                if u is not None and 2 <= u < NU + 2:
                    divide(u - 2)
                for slot in slots[2]:
                    take(slot)
                for w in work:
                    if w == "take_mlp":
                        wait_read(e, ("out", 0, -1))
                        e.tensor_copy(lb.xg[:], x_all[:, ds(NT * mlp[1], NT), :]).then_inc(s["xg_copied"], 1)
                    elif w == "moments":
                        wait_read(e, ("shift", 0, 0))
                        e.wait_ge(s["first_half"], 1)
                        e.sem_inc(s["sum_ready"], NT)
                        vector_moments(e, s, nb, lambda t: lb.xs[:, t])
                    elif w == "normalize":
                        vector_normalize(e, s, nb, lambda t: lb.xs[:, t], lambda t: lb.xs[:, t], signal="normed")
                    elif w == "take_next":
                        vector_take(e, s, x_all, following[1], xc)
                    else:
                        {"straight": straight, "turned": turned, "squares": squares, "normalize_k": normalize_k}[w[0]](*w[1:])

        @block.gpsimd
        def _(e):
            def add(what, t):
                m = 2 * rotated[t] + (what == "q")
                e.wait_ge(s["straight_ready"], m + 1)
                e.wait_ge(s["turned_ready"], 2 * m + 2)
                qk = lb.qk[:, part_of[what]]
                e.tensor_tensor(qk, qk, lb.part[:, part_of[what]], ALU.add).then_inc(s["rotated"], 1)

            def norms(what, t):
                m = 2 * projected[t] + (what == "q")
                e.wait_ge(s["squares_ready"], m + 1)
                h = heads_of[what]
                e.tensor_scalar(lb.norm2[:, t % NT, h], lb.ss[:, t % NT, h], 1e-24, None, ALU.max).then_inc(s["norm2_ready"], 1)
                e.wait_ge(s["norm2_ready"], m + 1)
                e.tensor_tensor(lb.rn[:, t % NT, h], lb.norm2[:, t % NT, h], half.to_broadcast([P, H7]), ALU.pow).then_inc(s["rnorm_ready"], 1)
                if what == "q":
                    e.wait_ge(s["rnorm_ready"], m + 1)
                    e.tensor_scalar(lb.q8[:, t % NT], lb.rn[:, t % NT, h], QK_SCALE, None, ALU.mult).then_inc(s["q8_ready"], 1)

            if own is None:
                if mlp is not None:
                    pool_rstd(e, s, nb, half)
                for t in rotated:
                    norms("k", t)
                    add("k", t)
                    norms("q", t)
                    add("q", t)
                    norms("k", t + 1)
                    norms("q", t + 1)
            else:
                for t in range(NT):
                    add("k", t + 1)
                    add("q", t + 1)
                    if t == 1:
                        pool_rstd(e, s, nb, half)
                    norms("k", t + 2)
                    norms("q", t + 2)


def layers(nc, ctx, ps, x_all, C, half, nb, xc, xT, late_layout, late_dram, layers_dram, arrived):
    late = Packed(nc, ctx, "late", late_layout, late_dram)
    lb = LayerBuffers(nc, ctx)
    args = (nc, ps, x_all, C, late, half, nb, xc, xT, lb)
    plan = attention_plan()
    layers_start_stage(nc, lb, xT, late, late_dram, layers_dram, arrived)
    layer_table_stage(nc, lb, late, 0, arrived, slice(0, 1), first=True)
    layer_stage(*args, "ltile", first_tiles_plan(), following=(0, 0))
    with nc.Fori(0, DEPTH // 2) as i:
        for parity in range(2):
            other = 1 - parity
            layer_table_stage(nc, lb, late, parity, arrived, slice(1, NT))
            layer_stage(*args, f"latt{parity}_first", plan, own=(parity, 0), following=(parity, 1), mlp=(other, B - 1))
            layer_fetch_stage(nc, lb, layers_dram, arrived, parity, 2 * i + parity + 1)
            with nc.Fori(1, B - 1) as b:
                layer_stage(*args, f"latt{parity}", plan, own=(parity, b), following=(parity, b + 1), mlp=(parity, b - 1))
            layer_table_stage(nc, lb, late, other, arrived, slice(0, 1), first=True)
            layer_stage(*args, f"latt{parity}_last", plan, own=(parity, B - 1), following=(other, 0), mlp=(parity, B - 2))
    layer_stage(*args, "lmlp", last_mlp_plan(), mlp=(1, B - 1))


def last_norm_stage(nc, x_all, x_in, half, nb, xc):
    with nc.Fori(0, B) as b:
        with stage(nc, "fin", "x_copied" + NORM_SIGNALS) as (block, s):
            @block.vector
            def _(e):
                e.tensor_tensor(nb.r[:], x_in[:, ds(NT * b, NT), :], x_all[:, ds(NT * b, NT), :], ALU.add).then_inc(s["sum_ready"], NT)
                vector_moments(e, s, nb, lambda t: nb.r[:, t])
                vector_normalize(e, s, nb, lambda t: nb.r[:, t], lambda t: x_all[:, ds(NT * b + t, 1), :])

            @block.gpsimd
            def _(e):
                pool_rstd(e, s, nb, half)



class Packed:

    def __init__(self, nc, ctx, name, layout, dram, first=0, dtype=F32):
        self.width = sum(w for _, w in layout)
        self.all = ctx.enter_context(nc.sbuf_tensor(name + "_sb", [P, self.width], dtype))
        self.dram = dram
        self.at = {}
        self.first = 0
        o = 0
        for n, w in layout:
            self.at[n] = (o, w)
            o += w
            if n == first:
                self.first = o

    def __getitem__(self, name):
        o, w = self.at[name]
        return self.all[:, o:o + w]


class Names:

    def __init__(self, *packs):
        self.packs = packs

    def __getitem__(self, name):
        return next(p for p in self.packs if name in p.at)[name]


def build(nc, a, layouts):
    with ExitStack() as ctx:
        def sb(name, shape, dtype=F32):
            return ctx.enter_context(nc.sbuf_tensor(name, shape, dtype))

        ps = [ctx.enter_context(nc.psum_tensor(f"bank{i}", [P, 512], F32)) for i in range(8)]
        arrived = ctx.enter_context(nc.semaphore("layer_weights_arrived"))
        x_all = sb("x_all", [P, B * NT, D])
        C = Packed(nc, ctx, "constants", layouts["constants"], a["constants"])
        nb = NormBuffers(sb)
        half = C["minus_half"]
        xc = sb("x_batch", [P, NT, D])
        xT = sb("x_batchT", [P, L])
        with ExitStack() as early:
            sbe = lambda n, shape, dtype=F32: early.enter_context(nc.sbuf_tensor(n, shape, dtype))
            W = Packed(nc, early, "weights", layouts["weights"], a["weights"], first="L0_b_out")
            CE = Packed(nc, early, "early", layouts["early"], a["early"])
            CC = Names(C, CE)
            recurrence_stage(nc, ps, a["L0_attn_x"], x_all, W, C, CE, half, nb)
            args = (nc, ps, x_all, W, CC, half, nb, xc, xT)
            experts_stage(*args)
            eg = Eigen(sbe)
            eigen_tables_stage(nc, ps, W, CC, eg)
            eigen_stage(*args, eg)
            ternary_weights_stage(nc, ps, W, CC)
            ternary_stage(*args)
            ident_bf, mask_bf = sbe("ident_bf", [P, P], BF16), sbe("mask_bf", [P, P], BF16)
            with stage(nc, "masks", "copied") as (block, s):
                @block.vector
                def _(e):
                    e.tensor_copy(ident_bf[:], C["ident"]).then_inc(s["copied"], 1)
                    e.tensor_copy(mask_bf[:], CE["causal_mask"]).then_inc(s["copied"], 1)
            causal_stage(*args, ident_bf, mask_bf)
            relu_stage(*args)
            features_stage(*args)
        x_in = sb("x_in", [P, B * NT, D])
        with stage(nc, "keep", "kept") as (block, s):
            @block.vector
            def _(e):
                e.tensor_copy(x_in[:], x_all[:]).then_inc(s["kept"], 1)
        with ExitStack() as last:
            layers(nc, last, ps, x_all, C, half, nb, xc, xT, layouts["late"], a["late"], a["layers"], arrived)
        last_norm_stage(nc, x_all, x_in, half, nb, xc)
        with stage(nc, "end", "stored") as (block, s):
            @block.sync
            def _(e):
                e.dma_start(a["out"].rearrange("b (j p) d -> p (b j) d", p=P), x_all[:]).then_inc(s["stored"], 16)
                e.wait_ge(s["stored"], 16)


def host_layouts(v):
    def rows(w):
        w = np.asarray(w)
        k, m = w.shape
        return w.reshape(k // P, P, m).transpose(1, 0, 2).reshape(P, -1)

    def cols(b):
        return np.asarray(b).reshape(-1, P).T

    def row(b):
        b = np.asarray(b).reshape(1, -1)
        return np.repeat(b, P, 0)

    z = np.zeros
    weights = []
    add = lambda n, w: weights.append((n, np.ascontiguousarray(w, dtype=np.float32)))
    A = np.asarray(v["L0_attn_A"])
    A_pad = z((E0, 32), np.float32)
    A_pad[:, :NS] = A
    CT = z((P, E0), np.float32)
    for b in range(B):
        CT[32 * b:32 * b + NS] = np.asarray(v["L0_attn_C"]).T
    add("L0_W_in", np.asarray(v["L0_attn_W_in"]))
    add("L0_b_in", cols(v["L0_attn_b_in"]))
    cw = np.asarray(v["L0_attn_conv_w"]).reshape(E0 // P, P, TAPS).transpose(1, 0, 2).reshape(P, -1)
    add("L0_conv_w", cw)
    add("L0_conv_b", cols(v["L0_attn_conv_b"]))
    add("L0_A", rows(A_pad))
    add("L0_CT", CT)
    add("L0_Dp", cols(v["L0_attn_Dp"]))
    add("L0_W_out", rows(v["L0_attn_W_out"]))
    add("L0_b_out", row(v["L0_attn_b_out"]))

    add("moe_router", np.asarray(v["L0_ffn_router_w"]))
    pairs = lambda w: np.asarray(w).transpose(1, 0, 2).reshape(D, NE * IE)
    add("moe_router_bias", row(v["L0_ffn_router_bias"]))
    add("moe_gate", np.concatenate([pairs(v["L0_ffn_gate_w"]), np.asarray(v["L0_ffn_s_gate_w"])], 1))
    add("moe_up", np.concatenate([pairs(v["L0_ffn_up_w"]), np.asarray(v["L0_ffn_s_up_w"])], 1))
    add("moe_down", rows(np.concatenate([np.asarray(v["L0_ffn_down_w"]).reshape(NE * IE, D), np.asarray(v["L0_ffn_s_down_w"])], 0)))
    w_in = np.asarray(v["L1_attn_w_in"])
    twice = lambda c: np.concatenate([np.asarray(c)] * 2).reshape(P, 1)
    coupling = z((P, P), np.float32)
    for i in range(P // 16):
        coupling[16 * i:16 * i + 16, 16 * i:16 * i + 16] = np.asarray(v["L1_attn_coupling"])[i % 4]
    add("L1_w_in", w_in.T)
    add("L1_w_in_swapped", np.concatenate([w_in[KS:], w_in[:KS]]).T)
    add("L1_coupling", coupling)
    add("L1_w_out", np.asarray(v["L1_attn_w_out"]).T)
    add("L1_w_gate", np.asarray(v["L1_attn_w_gate"]).T)
    add("L1_b_gate", row(v["L1_attn_b_gate"]))
    add("L1_log_decay", twice(v["L1_attn_log_decay"]))
    add("L1_frequency", twice(v["L1_attn_frequency"]))
    add("L1_w_mlp1", np.asarray(v["L1_attn_w_mlp1"]).T)
    add("L1_b_mlp1", cols(v["L1_attn_b_mlp1"]))
    add("L1_w_mlp2", rows(np.asarray(v["L1_attn_w_mlp2"]).T))
    add("L1_b_mlp2", row(v["L1_attn_b_mlp2"]))
    add("L1_ln1", np.stack([np.asarray(v["L1_attn_ln1_g"]), np.asarray(v["L1_attn_ln1_b"])], 1))
    add("L1_ln2", np.stack([np.asarray(v["L1_attn_ln2_g"]), np.asarray(v["L1_attn_ln2_b"])], 1))
    add("L1f_W_fc", np.asarray(v["L1_ffn_W_fc"]).T)
    add("L1f_W_proj", rows(np.asarray(v["L1_ffn_W_proj"]).T))
    add("L1f_ln_w", cols(v["L1_ffn_ln_w"]))
    add("L1f_ln_b", cols(v["L1_ffn_ln_b"]))
    partner = np.arange(H4 * DK4) ^ 1
    for w in "qk":
        wt, bt = np.asarray(v[f"L2_attn_w{w}"]), np.asarray(v[f"L2_attn_b{w}"])
        add(f"L2_w{w}", wt.T)
        add(f"L2_w{w}_turned", wt[partner].T)
        add(f"L2_b{w}", cols(bt))
        add(f"L2_b{w}_turned", cols(bt[partner]))
    add("L2_wv", np.asarray(v["L2_attn_wv"]).T)
    add("L2_bv", row(v["L2_attn_bv"]))
    add("L2_wo", rows(np.asarray(v["L2_attn_wo"]).T))
    add("L2_bo", row(v["L2_attn_bo"]))
    add("L2f_W1", np.asarray(v["L2_ffn_W1"]))
    add("L2f_b1", cols(v["L2_ffn_b1"]))
    add("L2f_W2", rows(v["L2_ffn_W2"]))
    add("L2f_b2", row(v["L2_ffn_b2"]))
    for w in ("Wq", "Wk", "Wv", "Wo", "Wfc"):
        add("L3_" + w, np.asarray(v["L3_attn_" + w]).T)
    for w in ("bq", "bk", "bo"):
        add("L3_" + w, cols(v["L3_attn_" + w]))
    add("L3_bv", row(v["L3_attn_bv"]))
    add("L3_bfc", row(v["L3_attn_bfc"]))
    proj = z((D, FEATS), np.float32)
    for h in range(H6):
        proj[DH6 * h:DH6 * (h + 1), M6 * h:M6 * (h + 1)] = np.asarray(v["L3_attn_proj"]).T
    add("L3_proj", proj)
    constants = []
    addc = lambda n, w: constants.append((n, np.ascontiguousarray(w, dtype=np.float32)))
    addc("ident", np.eye(P))
    addc("ones", np.ones((P, P)))
    addc("minus_half", np.full((P, 1), -0.5))
    early = []
    adde = lambda n, w: early.append((n, np.ascontiguousarray(w, dtype=np.float32)))
    spread = np.zeros((P, PAIRS * P))
    for i in range(NE):
        spread[i, IE * i:IE * (i + 1)] = 1
    adde("pair_of_expert", spread)
    adde("comes_first", np.repeat((np.arange(NE)[None] < np.arange(NE)[:, None]).reshape(1, -1), P, 0))
    adde("steps", np.repeat(np.arange(CH).reshape(1, -1), P, 0))
    adde("not_first", np.repeat((np.arange(CH) > 0).reshape(1, -1), P, 0))
    adde("half_sign", np.where(np.arange(P) < KS, 1.0, -1.0).reshape(P, 1))
    adde("swap", np.roll(np.eye(P), KS, 0))
    f32 = np.float32
    i, j = np.arange(P)[:, None], np.arange(P)[None]
    adde("causal_mask", np.where(j > i, MASKED, 0.0))
    theta = f32(10000.0) ** (np.arange(0, DK4, 2, dtype=f32) / f32(DK4))
    freqs = np.arange(L, dtype=f32)[:, None] * (f32(1) / theta)[None]
    emb = np.concatenate([freqs, freqs], 1).T
    sign = np.where(np.arange(DK4) % 2 == 0, -1.0, 1.0)[:, None]
    adde("rope4_cos", np.tile(np.cos(emb), (2, 1)))
    adde("rope4_sin", np.tile(np.sin(emb) * sign, (2, 1)))
    adde("head_of_feature", np.arange(P)[:, None] // DH6 == np.arange(H6)[None])
    own = np.zeros((P, FEATS // P, D + H6))
    for m in range(FEATS // P):
        h = (m * P + np.arange(P)) // M6
        own[:, m, :D] = h[:, None] == np.arange(D)[None] // DH6
        own[:, m, D:] = h[:, None] == np.arange(H6)[None]
    adde("own_columns", own.reshape(P, -1))

    late = []
    addl = lambda n, w: late.append((n, np.ascontiguousarray(w, dtype=np.float32)))
    back = np.arange(P)[:, None] - (np.arange(SPAN)[None] - WIN)
    band = np.where((back >= 0) & (back <= WIN), 0.0, MASKED)
    first = np.where(np.arange(SPAN)[None] < WIN, MASKED, band)
    addl("band_masks", np.concatenate([first, band], 1))
    addl("ident_late", np.eye(P))
    addl("next_token", np.eye(P, k=1))
    last_to_first = np.zeros((P, P))
    last_to_first[P - 1, 0] = 1
    addl("last_to_first", last_to_first)
    hw = np.arange(0, DK7, 2, dtype=f32)
    inv = f32(1.0) / f32(10000.0) ** (hw / f32(DK7))
    tt = np.arange(L, dtype=f32)
    fr = tt[:, None] * inv[None]
    base = (hw + f32(0.4 * DK7)) / f32(1.4 * DK7)
    power = (tt - L // 2) / f32(WIN // 2)
    sc = (base[None] ** power[:, None]).astype(f32)
    fr, sc = np.concatenate([fr, fr], 1), np.concatenate([sc, sc], 1)
    sg = np.where(np.arange(DK7) < DK7 // 2, -1.0, 1.0)[None]
    tok = lambda x: x.reshape(NT, P, DK7).transpose(1, 0, 2).reshape(P, -1)
    addl("rope7", np.concatenate([tok(np.cos(fr) * sc), tok(np.sin(fr) * sg * sc), tok(np.cos(fr) / sc), tok(np.sin(fr) * sg / sc)], 1))

    g = lambda n: np.asarray(v["L3_ffn_" + n])
    inner = g("W2").shape[1]
    layers_ = np.zeros((DEPTH + 1, P, sum(w for _, w in LAYER_COLUMNS)), np.float32)
    for d in range(DEPTH):
        w1, b1 = z((D, 2, HID7), np.float32), z((2, HID7), np.float32)
        w1[:, :, :inner] = g("W1")[d].reshape(D, 2, inner)
        b1[:, :inner] = g("b1")[d].reshape(2, inner)
        w2 = z((HID7, D), np.float32)
        w2[:inner] = g("W2")[d]
        part = {"qkv": g("Wqkv")[d], "wo": rows(g("Wo")[d]), "w1": w1.reshape(D, -1), "w2": rows(w2), "b1": cols(b1),
                "ln": np.stack([g("ln_g")[d], g("ln_b")[d]], 1), "b2": row(g("b2")[d]),
                "q_scale": row(g("q_scale")[d]), "q_scale_rolled": row(np.roll(g("q_scale")[d], DK7 // 2)),
                "k_scale": row(g("k_scale")[d]), "k_scale_rolled": row(np.roll(g("k_scale")[d], DK7 // 2))}
        layers_[d] = np.concatenate([part[n] for n, _ in LAYER_COLUMNS], 1)
    packs = {"weights": weights, "constants": constants, "early": early, "late": late}
    out = {k: np.concatenate([w for _, w in p], 1) for k, p in packs.items()}
    out["layers"] = layers_
    return out, {k: [(n, w.shape[1]) for n, w in p] for k, p in packs.items()}


def kernel(**v):
    import concourse.bacc as bacc
    from concourse.bass_utils import run_bass_kernel_spmd as run

    arrays, lay = host_layouts(v)
    arrays["L0_attn_x"] = np.asarray(v["L0_attn_x"])
    nc = bacc.Bacc("TRN2", target_bir_lowering=False, num_devices=1)
    aps = {n: nc.dram_tensor(n, x.shape, mybir.dt.from_np(x.dtype), kind="ExternalInput").ap() for n, x in arrays.items()}
    aps["out"] = nc.dram_tensor("out", (B, L, D), F32, kind="ExternalOutput").ap()
    build(nc, aps, lay)
    return run(nc, [arrays], core_ids=[0]).results[0]["out"]
```
